# Optimizing a Trainium2 kernel written in Bass

```python
import numpy as np
import jax
import jax.numpy as jnp

def _softmax(x, axis=-1):
    return jax.nn.softmax(x, axis=axis)

def _gelu(x):
    return jax.nn.gelu(x, approximate=True)

def _silu(x):
    return jax.nn.silu(x)

def _sigmoid(x):
    return jax.nn.sigmoid(x)

def _layernorm(x, axis=-1, eps=1e-05):
    m = jnp.mean(x, axis=axis, keepdims=True)
    v = jnp.var(x, axis=axis, keepdims=True)
    return (x - m) / jnp.sqrt(v + eps)

def _scatter_add(tgt, idx, src, axis=0):
    return tgt.at[idx].add(src)

def _segment_sum(src, seg, n):
    return jax.ops.segment_sum(src, seg, n)
kernel_name = 'mk_gnn_ffn_d2_gnn_r32_ca5d2a'

def setup_inputs(seed: int=0):
    np.random.seed(seed)
    _w = jnp.asarray

    def _rec_inputs():
        import jax
        import jax.numpy as jnp
        _gk = jax.random.key(seed)
        x = -0.0002117 + 1 * jax.random.normal(jax.random.fold_in(_gk, 1), (3125, 256), jnp.float32)
        src = jax.random.randint(jax.random.fold_in(_gk, 2), (50000,), 0, 3125, jnp.int32)
        dst = jnp.minimum((3125 * jax.random.uniform(jax.random.fold_in(_gk, 3), (50000,)) ** 2.0).astype(jnp.int32), 99999)
        _o = jnp.argsort(dst, stable=True)
        src = src[_o]
        dst = dst[_o]
        edge_weight = jax.random.uniform(jax.random.fold_in(_gk, 13), (50000,), jnp.float32, 0.0, 1)
        return (x, src, dst, edge_weight)
    x, src, dst, edge_weight = _rec_inputs()

    def _L0_gnn_setup():
        import jax, jax.numpy as jnp
        import numpy as np
        N_NODES = 3125
        N_EDGES = 100000
        D_IN = 256
        D_OUT = 256
        key = jax.random.key(seed)
        k1, k2, k3, k4, k5 = jax.random.split(key, 5)
        x = jax.random.normal(k1, (N_NODES, D_IN), dtype=jnp.float32)
        limit = float(np.sqrt(6.0 / (D_IN + D_OUT)))
        weight = jax.random.uniform(k2, (D_IN, D_OUT), dtype=jnp.float32, minval=-limit, maxval=limit)
        edge_val = jax.random.uniform(k3, (N_EDGES,), dtype=jnp.float32)
        edge_row = jax.random.randint(k4, (N_EDGES,), 0, N_NODES, dtype=jnp.int32)
        edge_col = jax.random.randint(k5, (N_EDGES,), 0, N_NODES, dtype=jnp.int32)
        return {'x': x, 'weight': weight, 'edge_val': edge_val, 'edge_row': edge_row, 'edge_col': edge_col}
    _L0_gnn_all = _L0_gnn_setup()
    _L0_gnn_in = {k: v for k, v in _L0_gnn_all.items() if k in ('weight',)}
    del _L0_gnn_all

    def _L0_ffn_setup():
        import jax, jax.numpy as jnp
        import numpy as np
        N_EXPERTS = 8
        TOP_K = 2
        key = jax.random.key(seed)
        ks = jax.random.split(key, 5)
        B, T, C, E, H = (8, 64, 256, 8, 682)
        scale = 1.0 / np.sqrt(C)
        return {'x': jax.random.normal(ks[0], (B, T, C), dtype=jnp.float32), 'router_w': jax.random.normal(ks[1], (E, C), dtype=jnp.float32) * scale, 'w1': jax.random.normal(ks[2], (E, H, C), dtype=jnp.float32) * scale, 'w2': jax.random.normal(ks[3], (E, C, H), dtype=jnp.float32) * (1.0 / np.sqrt(H)), 'w3': jax.random.normal(ks[4], (E, H, C), dtype=jnp.float32) * scale}
    _L0_ffn_all = _L0_ffn_setup()
    _L0_ffn_in = {k: v for k, v in _L0_ffn_all.items() if k in ('router_w', 'w1', 'w2', 'w3')}
    del _L0_ffn_all

    def _L1_gnn_setup():
        import jax, jax.numpy as jnp
        import numpy as np
        N_NODES = 50000
        N_EDGES = 25000
        N_FEAT = 256
        N_CLASSES = 256
        K_HOPS = 2
        key = jax.random.key(seed)
        k1, k2, k3 = jax.random.split(key, 3)
        x = jax.random.normal(k1, (N_NODES, N_FEAT), dtype=jnp.float32)
        edge_index = jax.random.randint(k2, (2, N_EDGES), 0, N_NODES, dtype=jnp.int32)
        W = jax.random.normal(k3, (N_CLASSES, N_FEAT), dtype=jnp.float32) * 0.05
        b = jnp.zeros((N_CLASSES,), dtype=jnp.float32)
        return {'x': x, 'edge_index': edge_index, 'W': W, 'b': b}
    _L1_gnn_all = _L1_gnn_setup()
    _L1_gnn_in = {k: v for k, v in _L1_gnn_all.items() if k in ('W', 'b')}
    del _L1_gnn_all

    def _L1_ffn_setup():
        import jax, jax.numpy as jnp
        import numpy as np
        E = 8
        K = 2
        D = 256
        H = 512
        DOUT = 256
        EPS = 1e-05
        key = jax.random.key(seed)
        ks = jax.random.split(key, 9)
        s = 0.02
        return {'x': jax.random.normal(ks[0], (4, 256, D), jnp.float32), 'gamma': 1.0 + 0.05 * jax.random.normal(ks[1], (D,), jnp.float32), 'beta': 0.05 * jax.random.normal(ks[2], (D,), jnp.float32), 'Wr': 0.01 * jax.random.normal(ks[3], (D, E), jnp.float32), 'br': jnp.zeros((E,), jnp.float32), 'W1': s * jax.random.normal(ks[4], (E, D, H), jnp.float32), 'b1': s * jax.random.normal(ks[5], (E, H), jnp.float32), 'W2': s * jax.random.normal(ks[6], (E, H, DOUT), jnp.float32), 'b2': s * jax.random.normal(ks[7], (E, DOUT), jnp.float32)}
    _L1_ffn_all = _L1_ffn_setup()
    _L1_ffn_in = {k: v for k, v in _L1_ffn_all.items() if k in ('gamma', 'beta', 'Wr', 'br', 'W1', 'b1', 'W2', 'b2')}
    del _L1_ffn_all
    return {'x': x, 'src': src, 'dst': dst, 'edge_weight': edge_weight, 'L0_gnn_weight': _L0_gnn_in['weight'], 'L0_ffn_router_w': _L0_ffn_in['router_w'], 'L0_ffn_w1': _L0_ffn_in['w1'], 'L0_ffn_w2': _L0_ffn_in['w2'], 'L0_ffn_w3': _L0_ffn_in['w3'], 'L1_gnn_W': _L1_gnn_in['W'], 'L1_gnn_b': _L1_gnn_in['b'], 'L1_ffn_gamma': _L1_ffn_in['gamma'], 'L1_ffn_beta': _L1_ffn_in['beta'], 'L1_ffn_Wr': _L1_ffn_in['Wr'], 'L1_ffn_br': _L1_ffn_in['br'], 'L1_ffn_W1': _L1_ffn_in['W1'], 'L1_ffn_b1': _L1_ffn_in['b1'], 'L1_ffn_W2': _L1_ffn_in['W2'], 'L1_ffn_b2': _L1_ffn_in['b2']}

def reference(x, src, dst, edge_weight, L0_gnn_weight, L0_ffn_router_w, L0_ffn_w1, L0_ffn_w2, L0_ffn_w3, L1_gnn_W, L1_gnn_b, L1_ffn_gamma, L1_ffn_beta, L1_ffn_Wr, L1_ffn_br, L1_ffn_W1, L1_ffn_b1, L1_ffn_W2, L1_ffn_b2):
    import jax
    import jax.numpy as jnp

    def _L0_gnn_ref(x, weight, edge_val, edge_row, edge_col):
        import jax, jax.numpy as jnp
        import numpy as np
        N_NODES = 3125
        N_EDGES = 100000
        D_IN = 256
        D_OUT = 256
        support = x @ weight
        msgs = support[edge_col] * edge_val[:, None]
        out = jax.ops.segment_sum(msgs, edge_row, num_segments=N_NODES)
        return jax.nn.relu(out)

    def _L0_ffn_ref(x, router_w, w1, w2, w3):
        import jax, jax.numpy as jnp
        import numpy as np
        N_EXPERTS = 8
        TOP_K = 2
        B, T, C = x.shape
        flat = x.reshape(-1, C)
        logits = flat @ router_w.T
        probs = jax.nn.softmax(logits, axis=-1)
        topk_probs, topk_idx = jax.lax.top_k(probs, TOP_K)
        topk_probs = topk_probs / (jnp.sum(topk_probs, axis=-1, keepdims=True) + 1e-09)
        onehot = jax.nn.one_hot(topk_idx, N_EXPERTS, dtype=flat.dtype)
        gates = jnp.einsum('nk,nke->ne', topk_probs, onehot)
        h1 = jnp.einsum('nc,ehc->neh', flat, w1)
        h3 = jnp.einsum('nc,ehc->neh', flat, w3)
        h = jax.nn.silu(h1) * h3
        y = jnp.einsum('neh,ech->nec', h, w2)
        out = jnp.einsum('ne,nec->nc', gates, y)
        return out.reshape(B, T, C)

    def _L1_gnn_ref(x, edge_index, W, b):
        import jax, jax.numpy as jnp
        import numpy as np
        N_NODES = 50000
        N_EDGES = 25000
        N_FEAT = 256
        N_CLASSES = 256
        K_HOPS = 2
        n = x.shape[0]
        loop = jnp.arange(n, dtype=edge_index.dtype)
        row = jnp.concatenate([edge_index[0], loop])
        col = jnp.concatenate([edge_index[1], loop])
        deg = jax.ops.segment_sum(jnp.ones_like(col, dtype=x.dtype), col, num_segments=n)
        dinv = jnp.where(deg > 0, jax.lax.rsqrt(deg), jnp.zeros_like(deg))
        norm = dinv[row] * dinv[col]

        def hop(h, _):
            msg = h[row] * norm[:, None]
            h_new = jax.ops.segment_sum(msg, col, num_segments=n)
            return (h_new, None)
        h, _ = jax.lax.scan(hop, x, None, length=K_HOPS)
        logits = h @ W.T + b
        return jax.nn.log_softmax(logits, axis=1)

    def _L1_ffn_ref(x, gamma, beta, Wr, br, W1, b1, W2, b2):
        import jax, jax.numpy as jnp
        import numpy as np
        E = 8
        K = 2
        D = 256
        H = 512
        DOUT = 256
        EPS = 1e-05
        mu = jnp.mean(x, axis=-1, keepdims=True)
        var = jnp.mean(jnp.square(x - mu), axis=-1, keepdims=True)
        xn = (x - mu) * jax.lax.rsqrt(var + EPS) * gamma + beta
        logits = jnp.einsum('bsd,de->bse', xn, Wr) + br
        top_vals, top_idx = jax.lax.top_k(logits, K)
        w = jax.nn.softmax(top_vals, axis=-1)
        w_full = jnp.einsum('bsk,bske->bse', w, jax.nn.one_hot(top_idx, E, dtype=w.dtype))
        y = jnp.zeros(x.shape[:-1] + (DOUT,), x.dtype)
        for e in range(E):
            h = jax.nn.gelu(jnp.einsum('bsd,dh->bsh', xn, W1[e]) + b1[e], approximate=False)
            y_e = jnp.einsum('bsh,hd->bsd', h, W2[e]) + b2[e]
            y = y + y_e * w_full[..., e, None]
        return y
    edge_index = jnp.stack([src, dst])
    x = x + _L0_gnn_ref(_layernorm(x, axis=-1), L0_gnn_weight, edge_weight, src, dst)
    x = x + _L0_ffn_ref(_layernorm(x, axis=-1)[None], L0_ffn_router_w, L0_ffn_w1, L0_ffn_w2, L0_ffn_w3)[0]
    x = x + _L1_gnn_ref(_layernorm(x, axis=-1), edge_index, L1_gnn_W, L1_gnn_b)
    x = x + _L1_ffn_ref(_layernorm(x, axis=-1)[None], L1_ffn_gamma, L1_ffn_beta, L1_ffn_Wr, L1_ffn_br, L1_ffn_W1, L1_ffn_b1, L1_ffn_W2, L1_ffn_b2)[0]
    return x

_drawn_inputs = setup_inputs


def setup_inputs(seed=0):
    import zlib

    import numpy as np

    out = dict(_drawn_inputs(seed))
    spreads = {'L1_gnn_b': (0.0, 0.378), 'L1_ffn_br': (0.0, 0.8)}
    factors = {'L1_gnn_W': 2.725,
     'L1_ffn_gamma': 8.0,
     'L1_ffn_beta': 8.0,
     'L1_ffn_Wr': 6.012,
     'L1_ffn_W1': 5.227,
     'L1_ffn_b1': 38.25,
     'L1_ffn_W2': 5.057,
     'L1_ffn_b2': 63.539}
    for name, (base, spread) in spreads.items():
        noise = np.random.default_rng([zlib.crc32(name.encode()), seed]).standard_normal(out[name].shape)
        drawn = base * np.exp(spread * noise) if base else spread * noise
        out[name] = jnp.asarray(drawn.astype(out[name].dtype))
    for name, factor in factors.items():
        out[name] = (out[name] * factor).astype(out[name].dtype)
    return out
```

```python
import concourse.bass as bass
from concourse import mybir
from contextlib import ExitStack

FP32 = mybir.dt.float32
FP16 = mybir.dt.float16
BF16 = mybir.dt.bfloat16
I32 = mybir.dt.int32
ALU = mybir.AluOpType
ACT = mybir.ActivationFunctionType
AX = mybir.AxisListType

P = 128
NODES, C = 3125, 256
EDGES = 50000
NT = 26
FULL = NODES // P
REST = NODES - FULL * P
ROWS = NT * P
EC = 392
ELAST = EDGES - (P - 1) * EC
PADKEY = (NT - 1) * P
NG = 224
NCH = 2 * NG
GU = 8
MID = 1600
SU = 4
E8 = 8
H0 = 682
H0C = 6
H0R = H0 - 5 * P
H1 = 512
TT = 56
TRASH = TT * P
XROWS = TRASH + 4 * P
EPS = 1e-5
BIG = 3.0e38
HALF = H0 // 2


class Chain:

    def __init__(self, eng, sem):
        self.eng, self.sem, self.n, self.i, self.per, self.start = eng, sem, 0, None, 0, 0

    def __call__(self, ins, wait=True):
        ins.then_inc(self.sem, 1)
        self.n += 1
        if wait:
            self.sync()

    def at(self):
        if self.i is None:
            return self.n
        return self.i * self.per + (self.start + self.n)

    def sync(self):
        self.eng.wait_ge(self.sem, self.at())

    def loop(self, count, per, body):
        body(0)
        entry = self.n
        with self.eng.Fori(1, count) as i:
            self.n, self.i, self.per, self.start = 0, i, per, entry - per
            body(i)
            assert self.n == per, (self.n, per)
            self.i, self.n = None, entry + (count - 1) * per


def after(eng, sem, value):
    if isinstance(value, int) and value <= 0:
        return
    eng.wait_ge(sem, value)


def pool_after(pool, sem, value):
    if isinstance(value, int) and value <= 0:
        return
    pool.wait_ge(sem, value)
    pool.nop(nofuse=True)


def turns(eng, count, body, peel=1):
    for i in range(peel):
        body(i)
    with eng.Fori(peel, count) as i:
        body(i)


def gnn_moe_program(nc, x_in, src, dst, edge_weight, w_gnn0, router0, w1_0, w2_0, w3_0,
                    w_gnn1, b_gnn1, gamma, beta, wr1, br1, w1_1, b1_1, w2_1, b2_1, out):
    ctx = ExitStack()
    with ctx:
        def sb(name, shape, dt=FP32):
            return ctx.enter_context(nc.sbuf_tensor(name, shape, dt))

        def sem(name):
            return ctx.enter_context(nc.semaphore(name))

        def dram(name, shape):
            return nc.dram_tensor(name, shape, FP32, kind="Internal").ap()

        support_t = dram("support_t", (ROWS, C))
        u1_t = dram("u1_t", (ROWS, C))
        u2_t = dram("u2_t", (ROWS, C))
        xs_t = dram("xs_t", (XROWS, C))
        y_t = [dram("y0_t", (TRASH, C)), dram("y1_t", (TRASH, C))]
        tables = [support_t, u1_t, u2_t]

        X = sb("X", [P, NT * C])
        A = sb("A", [P, NT * C])
        W = sb("W", [P, 34112])
        S = sb("S", [P, 6 * C])
        iota_f = sb("iota_f", [P, P])
        ident = sb("ident", [P, P])
        below = sb("below", [P, P])
        ones = sb("ones", [P, P])
        iota_h = sb("iota_h", [P, NCH], FP16)
        pcol = sb("pcol", [P, 1])
        low_s = [sb("low0", [P, NCH]), sb("low1", [P, NCH])]
        idx_s = [sb("idx0", [P, NCH], I32), sb("idx1", [P, NCH], I32)]
        wgt_s = sb("wgt_s", [P, NCH])
        goff = [sb("goff0", [1, NG + 2], I32), sb("goff1", [1, NG + 2], I32)]
        dinv = sb("dinv", [P, NT])
        dinv2 = sb("dinv2", [P, NT])
        mv = sb("mv", [P, NT, 2])
        rstd = sb("rstd", [P, NT])
        stats = sb("stats", [P, 2, 6])
        pair = sb("pair", [P, 2, 2])
        small = sb("small", [P, 192])
        istage = sb("istage", [P, 16], I32)

        x3 = X[:, :].rearrange("p (t c) -> p t c", c=C)
        a3 = A[:, :].rearrange("p (t c) -> p t c", c=C)

        ps = ctx.enter_context(nc.psum_tensor("ps", [P, 8, 512], FP32))

        xn = S[:, 0:2 * C].rearrange("p (s c) -> p s c", s=2)
        xT = S[:, 2 * C:4 * C].rearrange("p (s c) -> p s c", s=2)
        ot = S[:, 4 * C:6 * C].rearrange("p (s c) -> p s c", s=2)

        def earr(k):
            return X[:, k * EC:(k + 1) * EC]

        key_f, low_f, oth_f, wh_f, wm_f, wl_f, pos_f, lane_f, chunk_f, t1_f, t2_f = [earr(k) for k in range(11)]
        key_i, oth_i, t1_i, t2_i = [earr(k).bitcast(I32) for k in range(11, 15)]
        w_f = earr(15)
        assert 16 * EC <= NT * C
        oc = A[:, 0:SU * NCH // 2].bitcast(BF16).rearrange("p (s n) -> p s n", s=SU)
        LO = SU * NCH // 2
        Lh = A[:, LO:LO + SU * 2 * 64].bitcast(FP16).rearrange("p (s k n) -> p s k n", s=SU, k=2)
        LB = LO + SU * 2 * 64
        Lb = A[:, LB:LB + SU * 4 * 64].bitcast(BF16).rearrange("p (s k n) -> p s k n", s=SU, k=4)
        KB = LB + SU * 4 * 64
        okb = A[:, KB:KB + SU * NT // 2].bitcast(BF16).rearrange("p (s n) -> p s n", s=SU)
        zero = A[:, (NT - 1) * C:NT * C]
        raw13 = A[:, 0:2 * 1536].rearrange("p (w j c) -> p w j c", w=2, j=H0C)
        raw2 = A[:, 3072:3072 + 2 * H0].rearrange("p (m h) -> p m h", m=2)

        W13N = 2 * 2 * H0
        W2N = H0C * C
        W13 = W[:, 0:E8 * W13N]
        W2 = W[:, E8 * W13N:E8 * (W13N + W2N)]
        wg0 = W[:, 0:2 * C].rearrange("p (k n) -> p k n", k=2)
        rwn = W[0:E8, 2 * C:3 * C]
        rwT = sb("rwT", [P, 2, E8])
        o = 0

        def wslice(n):
            nonlocal o
            o += n
            return W[:, o - n:o]

        W1b = wslice(E8 * 2 * H1)
        W2b = wslice(E8 * 4 * C)
        b1b = wslice(E8 * H1)
        b2b = wslice(E8 * C)
        wgT = wslice(2 * C).rearrange("p (k n) -> p k n", k=2)
        wgn = wslice(2 * C).rearrange("p (k n) -> p k n", k=2)
        bg = wslice(C)
        gam = wslice(C)
        bet = wslice(C)
        wr_s = wslice(2 * E8).rearrange("p (k n) -> p k n", k=2)
        br_s = wslice(E8)
        rows1 = wslice(GU * 2 * C)
        oh1 = wslice(4 * 2 * P)
        rows0 = X[:, 0:GU * 2 * C]
        oh0 = X[:, GU * 2 * C:GU * 2 * C + 4 * 2 * P]
        hop_rows = [r.rearrange("p (g k c) -> p g k c", g=GU, k=2) for r in (rows0, rows1, rows1)]
        hop_oh = [r.rearrange("p (g k c) -> p g k c", g=4, k=2) for r in (oh0, oh1, oh1)]

        xs = A[:, 0:2 * C].rearrange("p (s c) -> p s c", s=2)
        fT = A[:, 512:512 + C]
        sil = A[:, 768:768 + H0]
        hh = A[:, 1450:1450 + H0]
        hT = A[:, 2132:2132 + H0C * P]
        ys = A[:, 2900:2900 + 2 * C].rearrange("p (s c) -> p s c", s=2)
        yg = A[:, 3412:3412 + 4 * C].rearrange("p (s k c) -> p s k c", s=2, k=2)
        R = 4436
        lg = A[:, R:R + NT * E8].rearrange("p (t e) -> p t e", e=E8)
        pr = A[:, R + 208:R + 416].rearrange("p (t e) -> p t e", e=E8)
        ta = A[:, R + 416:R + 624].rearrange("p (t e) -> p t e", e=E8)
        tb = A[:, R + 624:R + 832].rearrange("p (t e) -> p t e", e=E8)
        MS = A[:, R + 832:R + 832 + 2 * NT * E8].rearrange("p (e c) -> p e c", e=E8)
        v1 = A[:, R + 1248:R + 1248 + NT]
        v2 = A[:, R + 1274:R + 1274 + NT]
        v3 = A[:, R + 1300:R + 1300 + NT]
        fpos = A[:, R + 1326:R + 1326 + 2 * NT]
        ft1 = A[:, R + 1378:R + 1378 + 2 * NT]
        ft2 = A[:, R + 1430:R + 1430 + 2 * NT]
        wrev = A[:, R + 1482:R + 1490]
        gate = sb("gate", [P, 2, NT])
        scat_i = sb("scat_i", [P, 2, NT], I32)
        gath_i = sb("gath_i", [P, 2, NT], I32)
        eoff = sb("eoff", [1, TT], I32)
        v_signal = small[0:1, 190:191]
        cnt = small[:, 0:26]
        incl = small[:, 32:58]
        padn = small[:, 64:90]
        init = small[:, 96:122]
        i1 = small[:, 128:154].bitcast(I32)
        i2 = small[:, 160:186].bitcast(I32)
        est = S[0:1, 0:TT]
        ecount = S[0:1, TT:2 * TT]

        const_ready = sem("const_ready")
        dve_step = sem("dve_step")
        act_step = sem("act_step")
        pool_step = sem("pool_step")
        x_loaded = sem("x_loaded")
        wg0_loaded = sem("wg0_loaded")
        xs_zeroed = sem("xs_zeroed")
        edges_loaded = sem("edges_loaded")
        edges_cleared = sem("edges_cleared")
        x_free = sem("x_free")
        raw_loaded = sem("raw_loaded")
        raw_transposed = sem("raw_transposed")
        raw_copied = sem("raw_copied")
        gnn1_loaded = sem("gnn1_loaded")
        ffn1_loaded = sem("ffn1_loaded")
        small_mm_in = sem("small_mm_in")
        small_mm_out = sem("small_mm_out")
        x_reloaded = sem("x_reloaded")
        hops_added = [sem(f"hop{h}_added") for h in range(3)]
        hops_mm = [sem(f"hop{h}_mm") for h in range(3)]
        hops_oh = [sem(f"hop{h}_onehot") for h in range(3)]
        row_gathered = [sem(f"row_gathered{g}") for g in range(GU)]
        hop_table = [sem(f"hop{h}_table") for h in range(3)]
        hop_start = [sem(f"hop{h}_start") for h in range(3)]
        sort_onehot = [sem(f"sort{k}_onehot") for k in range(2)]
        sort_weighted = sem("sort_weighted")
        sort_mm = [sem(f"sort{k}_mm") for k in range(2)]
        sort_ready = [sem(f"sort{k}_ready") for k in range(2)]
        proj = [{n: sem(f"proj{k}_{n}") for n in ("xn", "tr", "xt", "mm", "ev")} for k in range(4)]
        support_out = [sem(f"support_out{s}") for s in range(2)]
        routed = sem("routed")
        wgT_ready = sem("wgT_ready")
        dve_to_act = sem("dve_to_act")
        act_to_dve = sem("act_to_dve")
        disp_ready = [sem(f"disp{m}_ready") for m in range(2)]
        disp_done = [[sem(f"disp{m}_done{s}") for s in range(2)] for m in range(2)]
        ffn = [{n: sem(f"ffn{m}_{n}") for n in ("tx", "fT", "h", "act", "hh", "th", "hT", "y", "ys", "bias")} for m in range(2)]
        xs_loaded = [[sem(f"xs{m}_loaded{s}") for s in range(2)] for m in range(2)]
        ys_stored = [[sem(f"ys{m}_stored{s}") for s in range(2)] for m in range(2)]
        y_gathered = [[sem(f"y{m}_gathered{s}") for s in range(2)] for m in range(2)]
        comb_used = [sem(f"comb{m}_used") for m in range(2)]
        out_done = sem("out_done")

        block = ctx.enter_context(nc.Block())
        NI = NT // 2

        def tile(ap3, t):
            if isinstance(t, int):
                return ap3[:, t, :]
            return ap3[:, bass.ds(t, 1), :].rearrange("p a c -> p (a c)")

        def col(ap2, t):
            return ap2[:, bass.ds(t, 1)] if not isinstance(t, int) else ap2[:, t:t + 1]

        @block.sync
        def _(sp):
            sp.wait_ge(const_ready, 1)
            sp.dma_start(x3[:, 0:FULL, :], x_in[0:FULL * P, :].rearrange("(t p) c -> p t c", p=P)).then_inc(x_loaded, 16)
            sp.dma_start(x3[0:REST, FULL, :], x_in[FULL * P:NODES, :]).then_inc(x_loaded, 16)
            sp.dma_start(wg0, w_gnn0.rearrange("(k p) n -> p k n", p=P)).then_inc(wg0_loaded, 16)
            sp.dma_start(rwn, router0).then_inc(wg0_loaded, 16)
            sp.wait_ge(const_ready, 2)
            sp.dma_start(xs_t.rearrange("(n p) c -> p n c", p=P),
                         zero.rearrange("p (a c) -> p a c", a=1).to_broadcast([P, XROWS // P, C])).then_inc(xs_zeroed, 16)
            sp_rows = support_t.rearrange("(t p) c -> t p c", p=P)

            def store_support(i):
                for s in range(2):
                    q = 2 * i + s
                    sp.wait_ge(proj[0]["ev"], q + 1)
                    sp.nop(nofuse=True)
                    dstrow = sp_rows[q, :, :] if isinstance(q, int) else sp_rows[bass.ds(q, 1), :, :].rearrange("t p c -> (t p) c")
                    sp.dma_start(dstrow, ot[:, s, :]).then_inc(support_out[s], 16)
            turns(sp, NI, store_support)

            for k, (kk, oo) in enumerate(((src, dst), (dst, src))):
                sp.wait_ge(edges_cleared, k + 1)
                for arr, vec in ((key_i, kk), (oth_i, oo)) + (((w_f, edge_weight),) if k == 0 else ()):
                    sp.dma_start(arr[0:P - 1, :], vec[0:(P - 1) * EC].rearrange("(p t) -> p t", t=EC)).then_inc(edges_loaded, 16)
                    sp.dma_start(arr[P - 1:P, 0:ELAST], vec[(P - 1) * EC:EDGES].rearrange("(p t) -> p t", p=1)).then_inc(edges_loaded, 16)

            sp.wait_ge(hops_added[0], NG)
            sp.wait_ge(x_reloaded, 1)
            sp.dma_start(x3[:, 0:FULL, :], x_in[0:FULL * P, :].rearrange("(t p) c -> p t c", p=P)).then_inc(x_loaded, 16)
            sp.dma_start(x3[0:REST, FULL, :], x_in[FULL * P:NODES, :]).then_inc(x_loaded, 16)

            def mixture(m):
                for s in range(2):
                    sp.wait_ge(disp_done[m][s], 32 * NI)
                xr = xs_t.rearrange("(t p) c -> t p c", p=P)
                yr = y_t[m].rearrange("(t p) c -> t p c", p=P)

                def load(q, s, n):
                    if not (isinstance(n, int) and n < 2):
                        sp.wait_ge(ffn[m]["tx"], n - 1)
                        sp.nop(nofuse=True)
                    row = xr[q, :, :] if isinstance(q, int) else xr[bass.ds(q, 1), :, :].rearrange("t p c -> (t p) c")
                    sp.dma_start(xs[:, s, :], row).then_inc(xs_loaded[m][s], 16)

                def store(q, s):
                    sp.wait_ge(ffn[m]["ys"], q + 1)
                    sp.nop(nofuse=True)
                    row = yr[q, :, :] if isinstance(q, int) else yr[bass.ds(q, 1), :, :].rearrange("t p c -> (t p) c")
                    sp.dma_start(row, ys[:, s, :]).then_inc(ys_stored[m][s], 16)

                load(0, 0, 0)
                load(1, 1, 1)

                with sp.Fori(1, TT // 2) as i:
                    for s in range(2):
                        load(2 * i + s, s, 2 * i + s)
                        store(2 * i + s - 2, s)
                store(TT - 2, 0)
                store(TT - 1, 1)

            mixture(0)
            sp.wait_ge(ffn[0]["y"], TT)
            sp.dma_start(wgn, w_gnn1.rearrange("(m p) c -> p m c", p=P)).then_inc(gnn1_loaded, 16)
            sp.dma_start(bg, b_gnn1.rearrange("(a n) -> a n", a=1).to_broadcast([P, C])).then_inc(gnn1_loaded, 16)
            sp.dma_start(gam, gamma.rearrange("(a n) -> a n", a=1).to_broadcast([P, C])).then_inc(gnn1_loaded, 16)
            sp.dma_start(bet, beta.rearrange("(a n) -> a n", a=1).to_broadcast([P, C])).then_inc(gnn1_loaded, 16)
            sp.dma_start(wr_s, wr1.rearrange("(k p) e -> p k e", p=P)).then_inc(gnn1_loaded, 16)
            sp.dma_start(br_s, br1.rearrange("(a n) -> a n", a=1).to_broadcast([P, E8])).then_inc(gnn1_loaded, 16)
            for h in (1, 2):
                sp.wait_ge(hop_start[h], 1)
                sp.dma_start(tables[h].rearrange("(t p) c -> p t c", p=P), a3).then_inc(hop_table[h], 16)
                if h == 1:
                    sp.dma_start(W1b.rearrange("p (e k n) -> p e k n", e=E8, k=2),
                                 w1_1.rearrange("e (k p) n -> p e k n", p=P)).then_inc(ffn1_loaded, 16)
                    sp.dma_start(W2b.rearrange("p (e k n) -> p e k n", e=E8, k=4),
                                 w2_1.rearrange("e (k p) n -> p e k n", p=P)).then_inc(ffn1_loaded, 16)
                    sp.dma_start(b1b, b1_1.rearrange("(a e) n -> a (e n)", a=1).to_broadcast([P, E8 * H1])).then_inc(ffn1_loaded, 16)
                    sp.dma_start(b2b, b2_1.rearrange("(a e) n -> a (e n)", a=1).to_broadcast([P, E8 * C])).then_inc(ffn1_loaded, 16)
            mixture(1)
            sp.wait_ge(comb_used[1], NT)
            sp.dma_start(out[0:FULL * P, :].rearrange("(t p) c -> p t c", p=P), x3[:, 0:FULL, :]).then_inc(out_done, 16)
            sp.dma_start(out[FULL * P:NODES, :], x3[0:REST, FULL, :]).then_inc(out_done, 16)
            sp.wait_ge(out_done, 32)
            sp.wait_ge(xs_zeroed, 16)
            for s in range(2):
                sp.wait_ge(support_out[s], 16 * NI)
                for m in range(2):
                    sp.wait_ge(ys_stored[m][s], 16 * TT // 2)
                    sp.wait_ge(disp_done[m][s], 32 * NI)
            for h in (1, 2):
                sp.wait_ge(hop_table[h], 16)

        @block.gpsimd
        def _(pool):
            pool.iota(iota_f[:, :], [[1, P]], base=0, channel_multiplier=0, allow_small_or_imprecise_dtypes=True).then_inc(pool_step, 1)
            pool.iota(iota_h[:, :], [[1, NCH]], base=0, channel_multiplier=0, allow_small_or_imprecise_dtypes=True).then_inc(pool_step, 1)
            pool.iota(pcol[:, :], [[0, 1]], base=0, channel_multiplier=1, allow_small_or_imprecise_dtypes=True).then_inc(pool_step, 1)
            def stage(dst_ap, src_ap):
                pool.tensor_copy(dst_ap, src_ap).then_inc(pool_step, 1)

            def hop(h):
                edges = idx_s[0 if h == 0 else 1]
                rows = hop_rows[h]
                base = 3 if h == 0 else pool_base[h]

                def turn(i):
                    for half in range(2):
                        g0 = i * GU + 4 * half
                        after(pool, hops_mm[h], g0 - 4)
                        st = istage[:, 8 * half:8 * half + 8]
                        stage(st, edges[:, bass.ds(i * (2 * GU) + 8 * half, 8)] if not isinstance(i, int)
                              else edges[:, 8 * half:8 * half + 8])
                        pool_after(pool, pool_step, i * 2 + (base + half + 1))
                        for g in range(4):
                            for k in range(2):
                                c = 2 * g + k
                                pool.indirect_dma_start(rows[:, 4 * half + g, k, :], None, tables[h],
                                                        bass.IndirectOffsetOnAxis(ap=st[:, c:c + 1], axis=0)
                                                        ).then_inc(row_gathered[4 * half + g], 16)
                turns(pool, NG // GU, turn)

            per_hop = 2 * (NG // GU)
            per_tiles = 2 * NI
            pool_base = {1: 3 + per_hop + 2 * per_tiles, 2: 3 + 2 * per_hop + 2 * per_tiles}

            def mixture_dispatch(m, base):
                def turn(i):
                    for s in range(2):
                        t = 2 * i + s
                        pool.wait_ge(disp_ready[m], t + 1)
                        st = istage[:, 2 * s:2 * s + 2]
                        after(pool, disp_done[m][s], i * 32)
                        stage(st, scat_i[:, :, bass.ds(t, 1)].rearrange("p k a -> p (k a)") if not isinstance(t, int)
                              else scat_i[:, :, t])
                        pool_after(pool, pool_step, t + (base + 1))
                        for k in range(2):
                            pool.indirect_dma_start(xs_t, bass.IndirectOffsetOnAxis(ap=st[:, k:k + 1], axis=0),
                                                    xn[:, s, :], None).then_inc(disp_done[m][s], 16)
                turns(pool, NI, turn)

            def mixture_gather(m, base):
                for s in range(2):
                    pool.wait_ge(ys_stored[m][s], 16 * TT // 2)

                def turn(i):
                    for s in range(2):
                        t = 2 * i + s
                        after(pool, comb_used[m], t - 1)
                        st = istage[:, 4 + 2 * s:6 + 2 * s]
                        stage(st, gath_i[:, :, bass.ds(t, 1)].rearrange("p k a -> p (k a)") if not isinstance(t, int)
                              else gath_i[:, :, t])
                        pool_after(pool, pool_step, t + (base + 1))
                        for k in range(2):
                            pool.indirect_dma_start(yg[:, s, k, :], None, y_t[m],
                                                    bass.IndirectOffsetOnAxis(ap=st[:, k:k + 1], axis=0)
                                                    ).then_inc(y_gathered[m][s], 16)
                turns(pool, NI, turn)

            for s in range(2):
                pool.wait_ge(support_out[s], 16 * NI)
            pool.wait_ge(sort_ready[0], 1)
            pool.wait_ge(hop_start[0], 1)
            hop(0)
            pool.wait_ge(xs_zeroed, 16)
            mixture_dispatch(0, 3 + per_hop)
            mixture_gather(0, 3 + per_hop + per_tiles)
            pool.wait_ge(hop_table[1], 16)
            hop(1)
            pool.wait_ge(hop_table[2], 16)
            hop(2)
            mixture_dispatch(1, 3 + 3 * per_hop + 2 * per_tiles)
            mixture_gather(1, 3 + 3 * per_hop + 3 * per_tiles)

        @block.tensor
        def _(pe):
            def project(k, rhs, n):
                sm = proj[k]

                def turn(i):
                    for s in range(2):
                        q = 2 * i + s
                        pe.wait_ge(sm["xn"], q + 1)
                        after(pe, sm["xt"], q - 1)
                        for b in range(2):
                            last = nc.tensor.transpose(ps[:, s, b * P:(b + 1) * P], xn[:, s, b * P:(b + 1) * P], ident[:, :])
                        last.then_inc(sm["tr"], 1)
                    for s in range(2):
                        q = 2 * i + s
                        pe.wait_ge(sm["xt"], q + 1)
                        after(pe, sm["ev"], q - 1)
                        for b in range(2):
                            last = nc.tensor.matmul(ps[:, 2 + s, 0:n], xT[:, s, b * P:(b + 1) * P], rhs[:, b, :],
                                                    start=(b == 0), stop=(b == 1))
                        last.then_inc(sm["mm"], 1)
                turns(pe, NI, turn)

            pe.wait_ge(const_ready, 4)
            pe.wait_ge(wg0_loaded, 32)
            project(0, wg0, C)
            for b in range(2):
                last = nc.tensor.transpose(ps[:, 4, b * E8:(b + 1) * E8], rwn[:, b * P:(b + 1) * P], ident[0:E8, 0:E8])
            last.then_inc(small_mm_out, 1)

            def prep(e):
                pe.wait_ge(raw_loaded, e * 96 + 96)
                for w in range(2):
                    for b in range(2):
                        after(pe, raw_copied, e * 12 + 2 * b + (2 if w else -6))
                        for j in range(H0C):
                            n = P if j < 5 else H0R
                            last = nc.tensor.transpose(ps[:, 2 * b + j // 4, (j % 4) * P:(j % 4) * P + n],
                                                       raw13[0:n, w, j, b * P:(b + 1) * P], ident[0:n, 0:n])
                            if j == 3 or j == 5:
                                last.then_inc(raw_transposed, 1)
                after(pe, raw_copied, e * 12)
                for j in range(H0C):
                    n = P if j < 5 else H0R
                    bank = 4 + j // 2 if j < 5 else 7
                    for mb in range(2):
                        last = nc.tensor.transpose(ps[0:n, bank, (j % 2 if j < 4 else 0) * C + mb * P:(j % 2 if j < 4 else 0) * C + (mb + 1) * P],
                                                   raw2[:, mb, j * P:j * P + n], ident[:, :])
                    if j != 0 and j != 2:
                        last.then_inc(raw_transposed, 1)
            pe.wait_ge(proj[0]["ev"], NT)
            pe.wait_ge(act_step, 1)
            turns(pe, E8, prep)

            def prefix(k, n):
                pe.wait_ge(small_mm_in, k)
                nc.tensor.matmul(ps[:, 7, 0:n], below[:, :], cnt[:, 0:n], start=True, stop=True)
                nc.tensor.matmul(ps[:, 7, 32:32 + n], ones[:, :], cnt[:, 0:n], start=True, stop=True).then_inc(small_mm_out, 1)

            def sort(k):
                words = 5 if k == 0 else 3
                prefix(k + 1, NT)

                def piece(s, j):
                    if j < 2:
                        return Lh[:, s, j, :]
                    return Lb[:, s, j - 1 if k == 0 else 0, :]

                def column(q, s, start):
                    pe.wait_ge(sort_onehot[k], q + 1)
                    if k == 0:
                        pe.wait_ge(sort_weighted, q + 1)
                    for j in range(words):
                        wide = not (k == 1 and j == 2)
                        last = nc.tensor.matmul(ps[:, j, 0:NCH if wide else NT], piece(s, j), oc[:, s, :] if wide else okb[:, s, :],
                                                start=start, stop=not start, skip_group_check=True)
                    last.then_inc(sort_mm[k], 1)

                def turn(i):
                    for s in range(SU):
                        column(SU * i + s, s, isinstance(i, int) and s == 0)
                turns(pe, EC // SU, turn)

            def hop(h):
                rows, oh = hop_rows[h], hop_oh[h]
                base = 32 * (NG // GU) * h

                def turn(i):
                    for g in range(GU):
                        q = GU * i + g
                        pe.wait_ge(row_gathered[g], i * 32 + (base + 32))
                        pe.wait_ge(hops_oh[h], q + 1)
                        after(pe, hops_added[h], q - 3)
                        for k in range(2):
                            last = nc.tensor.matmul(ps[:, g % 4, 0:C], oh[:, g % 4, k, :], rows[:, g, k, :],
                                                    start=(k == 0), stop=(k == 1))
                        last.then_inc(hops_mm[h], 1)
                turns(pe, NG // GU, turn)

            def mixture(m):
                sm = ffn[m]
                nj = H0C if m == 0 else 4

                def rows_of(j):
                    return H0R if (m == 0 and j == 5) else P

                def turn_x(q, s, i):
                    pe.wait_ge(xs_loaded[m][s], i * 16 + 16)
                    for b in range(2):
                        last = nc.tensor.transpose(ps[:, 6, b * P:(b + 1) * P], xs[:, s, b * P:(b + 1) * P], ident[:, :])
                    last.then_inc(sm["tx"], 1)

                def turn_h(q):
                    pe.wait_ge(sm["hh"], q + 1)
                    for j in range(nj):
                        n = rows_of(j)
                        last = nc.tensor.transpose(ps[0:n, 4 + j // 4, (j % 4) * P:(j % 4 + 1) * P], hh[:, j * P:j * P + n], ident[:, :])
                    last.then_inc(sm["th"], 1)

                def up(q, e):
                    pe.wait_ge(sm["fT"], q + 1)
                    if m == 0:
                        for part in range(4):
                            for b in range(2):
                                at = b * 2 * H0 + part * HALF
                                last = nc.tensor.matmul(ps[:, part, 0:HALF], fT[:, b * P:(b + 1) * P],
                                                        W13[:, bass.ds(e * W13N + at, HALF)], start=(b == 0), stop=(b == 1))
                        last.then_inc(sm["h"], 1)
                    else:
                        for b in range(2):
                            last = nc.tensor.matmul(ps[:, 0, :], fT[:, b * P:(b + 1) * P],
                                                    W1b[:, bass.ds(e * (2 * H1) + b * H1, H1)], start=(b == 0), stop=(b == 1))
                        last.then_inc(sm["h"], 1)

                def down(q, e):
                    pe.wait_ge(sm["hT"], q + 1)
                    after(pe, sm["ys"], q)
                    w, n_w = (W2, W2N) if m == 0 else (W2b, 4 * C)
                    for j in range(nj):
                        n = rows_of(j)
                        last = nc.tensor.matmul(ps[:, 7, 0:C], hT[0:n, j * P:(j + 1) * P],
                                                w[0:n, bass.ds(e * n_w + j * C, C)], start=(j == 0), stop=(j == nj - 1))
                    last.then_inc(sm["y"], 1)

                def expert(q):
                    return pe.value_load(eoff[0:1, bass.ds(q, 1)] if not isinstance(q, int) else eoff[0:1, q:q + 1], min_val=0, max_val=E8 - 1)

                def turn(i):
                    for s in range(2):
                        q = 2 * i + s
                        turn_x(q, s, i)
                        if not (isinstance(i, int) and s == 0):
                            turn_h(q - 1)
                        up(q, expert(q))
                        if not (isinstance(i, int) and s == 0):
                            down(q - 1, expert(q - 1))
                turns(pe, TT // 2, turn)
                turn_h(TT - 1)
                down(TT - 1, expert(TT - 1))

            pe.wait_ge(raw_copied, 12 * E8)
            sort(0)
            sort(1)
            hop(0)
            pe.wait_ge(act_step, 1)
            project(1, rwT, E8)
            prefix(3, E8)
            pe.wait_ge(routed, 1)
            mixture(0)
            pe.wait_ge(gnn1_loaded, 16 * 6)
            for b in range(2):
                for mb in range(2):
                    last = nc.tensor.transpose(ps[:, b, mb * P:(mb + 1) * P], wgn[:, mb, b * P:(b + 1) * P], ident[:, :])
            last.then_inc(small_mm_out, 1)
            hop(1)
            hop(2)
            pe.wait_ge(wgT_ready, 1)
            project(2, wgT, C)
            project(3, wr_s, E8)
            prefix(4, E8)
            pe.wait_ge(routed, 2)
            pe.wait_ge(ffn1_loaded, 16 * 4)
            mixture(1)

        @block.scalar
        def _(act):
            AF = nc.scalar.activation

            def project(k, evacuate):
                sm = proj[k]

                def turn(i):
                    for s in range(2):
                        q = 2 * i + s
                        act.wait_ge(sm["tr"], q + 1)
                        after(act, sm["mm"], q - 1)
                        AF(xT[:, s, :], ps[:, s, 0:C], ACT.Copy).then_inc(sm["xt"], 1)
                    if evacuate:
                        for s in range(2):
                            q = 2 * i + s
                            act.wait_ge(sm["mm"], q + 1)
                            after(act, support_out[s], i * 16)
                            AF(ot[:, s, :], ps[:, 2 + s, 0:C], ACT.Copy).then_inc(sm["ev"], 1)
                turns(act, NI, turn)

            def root(k):
                act.wait_ge(dve_to_act, k)
                AF(rstd[:, :], rstd[:, :], ACT.Sqrt).then_inc(act_to_dve, 1)

            root(1)
            project(0, True)
            act.wait_ge(small_mm_out, 1)
            AF(rwT[:, :, :].rearrange("p k e -> p (k e)"), ps[:, 4, 0:2 * E8], ACT.Copy).then_inc(act_step, 1)

            def prep(e):
                if isinstance(e, int):
                    act.wait_ge(const_ready, 3)
                    act.wait_ge(proj[0]["mm"], NT)
                else:
                    act.wait_ge(raw_transposed, e * 12)
                act.nop(nofuse=True)
                for w, t in ((0, w1_0), (1, w3_0)):
                    tv = t[e, :, :] if isinstance(e, int) else t[bass.ds(e, 1), :, :].rearrange("a h c -> (a h) c")
                    act.dma_start(raw13[:, w, 0:5, :], tv[0:5 * P, :].rearrange("(j p) c -> p j c", p=P)).then_inc(raw_loaded, 16)
                    act.dma_start(raw13[0:H0R, w, 5, :], tv[5 * P:H0, :]).then_inc(raw_loaded, 16)
                tv = w2_0[e, :, :] if isinstance(e, int) else w2_0[bass.ds(e, 1), :, :].rearrange("a c h -> (a c) h")
                act.dma_start(raw2, tv.rearrange("(m p) h -> p m h", p=P)).then_inc(raw_loaded, 32)
                n = 0
                for w in range(2):
                    for b in range(2):
                        for half in range(2):
                            n += 1
                            width = 512 if half == 0 else H0 - 512
                            at = b * 2 * H0 + w * H0 + half * 512
                            act.wait_ge(raw_transposed, e * 12 + n)
                            AF(W13[:, bass.ds(e * W13N + at, width)] if not isinstance(e, int) else W13[:, at:at + width],
                               ps[:, 2 * b + half, 0:width], ACT.Copy).then_inc(raw_copied, 1)
                for j0, j1, r, bank in ((0, 2, P, 4), (2, 4, P, 5), (4, 5, P, 6), (5, 6, H0R, 7)):
                    n += 1
                    width = (j1 - j0) * C
                    act.wait_ge(raw_transposed, e * 12 + n)
                    AF(W2[0:r, bass.ds(e * W2N + j0 * C, width)] if not isinstance(e, int) else W2[0:r, j0 * C:j0 * C + width],
                       ps[0:r, bank, 0:width], ACT.Copy).then_inc(raw_copied, 1)
            turns(act, E8, prep)

            def weigh(i):
                for s in range(SU):
                    q = SU * i + s
                    act.wait_ge(sort_onehot[0], q + 1)
                    after(act, sort_mm[0], q - SU + 1)
                    for j, part in enumerate((wh_f, wm_f, wl_f)):
                        last = AF(Lb[:, s, 1 + j, :], Lb[:, s, 0, :], ACT.Copy, scale=col(part, q))
                    last.then_inc(sort_weighted, 1)
            turns(act, EC // SU, weigh)

            def mixture(m):
                sm = ffn[m]

                def transposed_x(q):
                    act.wait_ge(sm["tx"], q + 1)
                    AF(fT, ps[:, 6, 0:C], ACT.Copy).then_inc(sm["fT"], 1)

                def transposed_h(q):
                    act.wait_ge(sm["th"], q + 1)
                    if m == 0:
                        AF(hT[:, 0:512], ps[:, 4, :], ACT.Copy)
                        AF(hT[:, 512:640], ps[:, 5, 0:P], ACT.Copy)
                        AF(hT[0:H0R, 640:768], ps[0:H0R, 5, P:2 * P], ACT.Copy).then_inc(sm["hT"], 1)
                    else:
                        AF(hT[:, 0:512], ps[:, 4, :], ACT.Copy).then_inc(sm["hT"], 1)

                def nonlinear(q):
                    if m == 0:
                        act.wait_ge(sm["h"], q + 1)
                        for part in range(2):
                            AF(sil[:, part * HALF:(part + 1) * HALF], ps[:, part, 0:HALF], ACT.Silu).then_inc(sm["act"], 1)
                    else:
                        act.wait_ge(sm["bias"], q + 1)
                        AF(hh[:, 0:H1], sil[:, 0:H1], ACT.Gelu).then_inc(sm["hh"], 1)

                def turn(i):
                    for s in range(2):
                        q = 2 * i + s
                        transposed_x(q)
                        if not (isinstance(i, int) and s == 0):
                            transposed_h(q - 1)
                        nonlinear(q)
                turns(act, TT // 2, turn)
                transposed_h(TT - 1)

            root(2)
            project(1, False)
            act.wait_ge(dve_to_act, 3)
            AF(ta, tb, ACT.Exp).then_inc(act_to_dve, 1)
            mixture(0)
            act.wait_ge(small_mm_out, 5)
            AF(wgT[:, 0, :], ps[:, 0, 0:C], ACT.Copy)
            AF(wgT[:, 1, :], ps[:, 1, 0:C], ACT.Copy).then_inc(wgT_ready, 1)
            AF(dinv[:, :], dinv2[:, :], ACT.Sqrt)
            root(4)
            project(2, False)
            act.wait_ge(dve_to_act, 5)

            def exps(i):
                for s in range(2):
                    t = 2 * i + s
                    after(act, act_step, t)
                    AF(xn[:, s, :], tile(a3, t), ACT.Exp, bias=col(rstd, t), accum_out=col(dinv2, t)).then_inc(act_step, 1)
            turns(act, NI, exps)
            act.wait_ge(act_step, 1 + NT)
            AF(dinv2[:, :], dinv2[:, :], ACT.Ln).then_inc(act_to_dve, 1)
            root(6)
            project(3, False)
            act.wait_ge(dve_to_act, 7)
            AF(v3, v3, ACT.Exp).then_inc(act_to_dve, 1)
            mixture(1)

        @block.vector
        def _(dve):
            V = nc.vector
            ch = Chain(dve, dve_step)

            loop = ch.loop

            def layernorm_stats(k):
                def turn(i):
                    for s in range(2):
                        ch(V.bn_stats(stats[:, s, :], tile(x3, 2 * i + s)), wait=(s == 1))
                    dve.nop(nofuse=True)
                    for s in range(2):
                        ch(V.bn_aggr(pair[:, s, :], stats[:, s, :]), wait=(s == 1))
                    ch(V.tensor_copy(mv[:, bass.ds(2 * i, 2), :] if not isinstance(i, int) else mv[:, 0:2, :], pair[:, :, :]))
                loop(NI, 5, turn)
                V.tensor_scalar(rstd[:, :], mv[:, :, 1], EPS, None, ALU.add).then_inc(dve_to_act, 1)
                dve.wait_ge(act_to_dve, k)
                ch(V.reciprocal(rstd[:, :], rstd[:, :]))

            def normalise(t, out_ap, scale):
                return V.tensor_scalar(out_ap, tile(x3, t), mv_mean(t), col(scale, t), ALU.subtract, ALU.mult)

            def mv_mean(t):
                return mv[:, bass.ds(t, 1), 0:1].rearrange("p a b -> p (a b)") if not isinstance(t, int) else mv[:, t, 0:1]

            ch(V.memset(small[:, :], 0.0), wait=False)
            ch(V.memset(x3[:, FULL:NT, :], 0.0))
            V.memset(zero, 0.0).then_inc(const_ready, 1)
            V.memset(ones[:, :], 1.0).then_inc(const_ready, 1)
            dve.wait_ge(pool_step, 3)
            V.tensor_scalar(ident[:, :], iota_f[:, :], pcol[:, :], None, ALU.is_equal).then_inc(const_ready, 1)
            V.tensor_scalar(below[:, :], iota_f[:, :], pcol[:, :], None, ALU.is_gt).then_inc(const_ready, 1)

            dve.wait_ge(x_loaded, 32)
            layernorm_stats(1)

            def give(i):
                for s in range(2):
                    q = 2 * i + s
                    after(dve, proj[0]["tr"], q - 1)
                    normalise(q, xn[:, s, :], rstd).then_inc(proj[0]["xn"], 1)
            turns(dve, NI, give)

            def padded_ends(n, bits):
                ch(V.tensor_scalar(i1[:, 0:n], ps[:, 7, 32:32 + n], float((1 << bits) - 1), None, ALU.add))
                ch(V.tensor_scalar(i2[:, 0:n], i1[:, 0:n], bits, bits, ALU.arith_shift_right, ALU.logical_shift_left))
                ch(V.tensor_copy(padn[:, 0:n], i2[:, 0:n]))
                ch(V.tensor_tensor_scan(incl[:, 0:n], padn[:, 0:n], padn[:, 0:n], 0.0, ALU.add, ALU.max))
                ch(V.tensor_tensor(init[:, 0:n], incl[:, 0:n], padn[:, 0:n], ALU.subtract))
                ch(V.tensor_tensor(init[:, 0:n], init[:, 0:n], ps[:, 7, 0:n], ALU.add))

            def table(starts, count, n, width, ends):
                ch(V.memset(count, 0.0))
                for b in range(n):
                    ch(V.scalar_tensor_tensor(count, starts, incl[0:1, b:b + 1], count, ALU.is_ge, ALU.add))
                ch(V.tensor_scalar(count, count, float(ends), float(width), ALU.min, ALU.mult))

            def sort(k):
                if k == 0:
                    dve.wait_ge(proj[0]["xn"], NT)
                V.memset(key_i, PADKEY)
                if k == 0:
                    V.memset(w_f, 0.0)
                V.memset(oth_i, 0).then_inc(edges_cleared, 1)
                dve.wait_ge(edges_loaded, 96 if k == 0 else 160)
                ch(V.tensor_scalar(t1_i, key_i, 7, None, ALU.arith_shift_right), wait=False)
                ch(V.tensor_scalar(t2_i, key_i, P - 1, None, ALU.bitwise_and))
                ch(V.tensor_copy(key_f, t1_i), wait=False)
                ch(V.tensor_scalar(low_f, t2_i, 1.0, None, ALU.add), wait=False)
                ch(V.tensor_scalar(oth_f, oth_i, -float(MID), None, ALU.add))
                if k == 0:
                    bf = t1_i.bitcast(BF16)[:, 0:EC]
                    rest = t1_f
                    for n, part in enumerate((wh_f, wm_f, wl_f)):
                        ch(V.tensor_copy(bf, w_f if n == 0 else rest))
                        ch(V.tensor_copy(part, bf))
                        if n < 2:
                            ch(V.tensor_tensor(rest, w_f if n == 0 else rest, part, ALU.subtract))
                for b in range(NT):
                    ch(V.tensor_scalar((t1_f, t2_f, pos_f, lane_f)[b % 4], key_f, float(b), None, ALU.is_equal, ALU.add,
                                       accum_out=cnt[:, b:b + 1]), wait=(b % 4 == 3))
                ch.sync()
                V.memset(pos_f, 0.0).then_inc(small_mm_in, 1)
                dve.wait_ge(small_mm_out, k + 2)
                padded_ends(NT, 8)
                for b in range(NT):
                    ch(V.tensor_scalar(t1_f, key_f, float(b), None, ALU.is_equal))
                    ch(V.tensor_tensor_scan(t2_f, t1_f, t1_f, init[:, b:b + 1], ALU.add, ALU.max))
                    ch(V.tensor_tensor(t2_f, t1_f, t2_f, ALU.mult))
                    ch(V.tensor_tensor(pos_f, pos_f, t2_f, ALU.add))
                ch(V.tensor_scalar(t1_i, pos_f, -1.0, None, ALU.add))
                ch(V.tensor_scalar(t2_i, t1_i, P - 1, None, ALU.bitwise_and), wait=False)
                ch(V.tensor_scalar(t1_i, t1_i, 7, None, ALU.arith_shift_right))
                ch(V.tensor_copy(lane_f, t2_i), wait=False)
                ch(V.tensor_copy(chunk_f, t1_i))
                gs, gc = t1_f[0:1, 0:NG], t2_f[0:1, 0:NG]
                ch(V.tensor_scalar(gs, iota_h[0:1, 0:NG], 256.0, None, ALU.mult))
                table(gs, gc, NT, C, NT - 1)
                ch(V.memset(goff[k][:, 0:2], 0), wait=False)
                ch(V.tensor_copy(goff[k][:, 2:NG + 2], gc))
                if k == 0:
                    dve.wait_ge(raw_transposed, 12 * E8)

                def turn(i):
                    for s in range(SU):
                        q = SU * i + s
                        after(dve, sort_mm[k], q - SU + 1)
                        V.tensor_scalar(oc[:, s, :], iota_h[:, :], col(chunk_f, q), None, ALU.is_equal)
                        V.tensor_scalar(Lh[:, s, 0, :], iota_h[:, 0:P], col(lane_f, q), col(low_f, q), ALU.is_equal, ALU.mult)
                        V.tensor_scalar(Lh[:, s, 1, :], iota_h[:, 0:P], col(lane_f, q), col(oth_f, q), ALU.is_equal, ALU.mult)
                        if k == 0:
                            V.tensor_scalar(Lb[:, s, 0, :], iota_h[:, 0:P], col(lane_f, q), None, ALU.is_equal).then_inc(sort_onehot[k], 1)
                        else:
                            V.tensor_scalar(okb[:, s, :], iota_h[:, 0:NT], col(key_f, q), None, ALU.is_equal)
                            V.tensor_scalar(Lb[:, s, 0, :], iota_h[:, 1:P + 1], col(low_f, q), None, ALU.is_equal).then_inc(sort_onehot[k], 1)
                turns(dve, EC // SU, turn)
                dve.wait_ge(sort_mm[k], EC)
                ch(V.tensor_scalar(low_s[k][:, :], ps[:, 0, 0:NCH], -1.0, None, ALU.add), wait=False)
                ch(V.tensor_scalar(idx_s[k][:, :], ps[:, 1, 0:NCH], float(MID), None, ALU.add))
                if k == 0:
                    ch(V.tensor_copy(wgt_s[:, :], ps[:, 4, 0:NCH]))
                    ch(V.tensor_tensor(wgt_s[:, :], wgt_s[:, :], ps[:, 3, 0:NCH], ALU.add))
                    V.tensor_tensor(wgt_s[:, :], wgt_s[:, :], ps[:, 2, 0:NCH], ALU.add).then_inc(sort_ready[k], 1)
                else:
                    ch(V.tensor_scalar(dinv2[:, :], ps[:, 2, 0:NT], 1.0, None, ALU.add))
                    V.reciprocal(dinv2[:, :], dinv2[:, :]).then_inc(sort_ready[k], 1)
                dve.wait_ge(sort_ready[k], 1)

            sort(0)
            sort(1)
            dve.wait_ge(xs_zeroed, 16)
            V.memset(A[:, :], 0.0).then_inc(hop_start[0], 1)
            dve.wait_ge(hop_start[0], 1)

            def hop(h):
                e = 0 if h == 0 else 1
                oh = hop_oh[h]

                def onehot(q, g):
                    after(dve, hops_mm[h], q - 3)
                    for k in range(2):
                        c = 2 * q + k
                        if h == 0:
                            ins = V.tensor_scalar(oh[:, g % 4, k, :], iota_f[:, :], col(low_s[e], c), col(wgt_s, c), ALU.is_equal, ALU.mult)
                        else:
                            ins = V.tensor_scalar(oh[:, g % 4, k, :], iota_f[:, :], col(low_s[e], c), None, ALU.is_equal)
                    ins.then_inc(hops_oh[h], 1)

                def add(q, g, at):
                    dve.wait_ge(hops_mm[h], q + 1)
                    after(dve, hops_added[h], q)
                    a = A[:, bass.ds(at, C)]
                    V.tensor_tensor(a, a, ps[:, g % 4, 0:C], ALU.add).then_inc(hops_added[h], 1)

                def at_of(n):
                    return dve.value_load(goff[e][0:1, bass.ds(n, 1)] if not isinstance(n, int) else goff[e][0:1, n:n + 1],
                                          min_val=0, max_val=(NT - 1) * C)

                def turn(i):
                    for g in range(GU):
                        q = GU * i + g
                        onehot(q, g)
                        if not (isinstance(i, int) and g < 2):
                            add(q - 2, (g - 2) % GU, at_of(q))
                turns(dve, NG // GU, turn)
                for q in (NG - 2, NG - 1):
                    add(q, q % GU, at_of(q + 2))
                dve.wait_ge(hops_added[h], NG)

            hop(0)

            V.memset(x3[:, FULL:NT, :], 0.0).then_inc(x_reloaded, 1)
            dve.wait_ge(x_loaded, 64)
            ch(V.scalar_tensor_tensor(X[:, :], A[:, :], 0.0, X[:, :], ALU.max, ALU.add))

            def route_project(k, full):
                def turn(i):
                    for s in range(2):
                        q = 2 * i + s
                        after(dve, proj[k]["tr"], q - 1)
                        full(s, q, proj[k]["xn"])
                    for s in range(2):
                        q = 2 * i + s
                        dve.wait_ge(proj[k]["mm"], q + 1)
                        dstt = lg[:, bass.ds(q, 1), :].rearrange("p a e -> p (a e)") if not isinstance(q, int) else lg[:, q, :]
                        if k == 1:
                            V.tensor_copy(dstt, ps[:, 2 + s, 0:E8]).then_inc(proj[k]["ev"], 1)
                        else:
                            V.tensor_tensor(dstt, ps[:, 2 + s, 0:E8], br_s, ALU.add).then_inc(proj[k]["ev"], 1)
                if k == 1:
                    turns(dve, NI, turn)
                else:
                    loop(NI, 4, turn)
                dve.wait_ge(proj[k]["ev"], NT)

            def bc(v):
                return v.rearrange("p (t a) -> p t a", a=1).to_broadcast([P, NT, E8])

            def masks(val, drop):
                ch(V.tensor_copy(wrev, iota_f[:, 0:E8]))
                ch(V.tensor_scalar(wrev, wrev, -1.0, float(E8), ALU.mult, ALU.add))
                wb = wrev.rearrange("p (a e) -> p a e", a=1).to_broadcast([P, NT, E8])
                for k in range(2):
                    ch(V.tensor_reduce(v1 if k == 0 else v2, val, AX.X, ALU.max))
                    ch(V.tensor_tensor(ta, val, bc(v1 if k == 0 else v2), ALU.is_equal))
                    ch(V.tensor_tensor(ta, ta, wb, ALU.mult))
                    ch(V.tensor_reduce(v3, ta, AX.X, ALU.max))
                    Mk = MS[:, :, k * NT:(k + 1) * NT].rearrange("p e t -> p t e")
                    ch(V.tensor_tensor(Mk, ta, bc(v3), ALU.is_equal))
                    if k == 0:
                        ch(V.tensor_scalar(ta, Mk, -drop, None, ALU.mult))
                        ch(V.tensor_tensor(val, val, ta, ALU.add))
                for k in range(2):
                    mk = MS[:, :, k * NT + FULL]
                    ch(V.tensor_scalar(v3[:, 0:1], pcol[:, :], float(REST), None, ALU.is_lt))
                    ch(V.tensor_scalar(mk, mk, v3[:, 0:1], None, ALU.mult))
                    ch(V.memset(MS[:, :, k * NT + NT - 1], 0.0))

            def places(m):
                V.tensor_reduce(cnt[:, 0:E8], MS, AX.X, ALU.add).then_inc(small_mm_in, 1)
                dve.wait_ge(small_mm_out, 4 + 2 * m)
                padded_ends(E8, 7)
                ch(V.memset(fpos, 0.0))
                for e in range(E8):
                    ch(V.tensor_tensor_scan(ft1, MS[:, e, :], MS[:, e, :], init[:, e:e + 1], ALU.add, ALU.max))
                    ch(V.tensor_tensor(ft1, ft1, MS[:, e, :], ALU.mult))
                    ch(V.tensor_tensor(fpos, fpos, ft1, ALU.add))
                ch(V.tensor_scalar(v3[:, 0:1], pcol[:, :], float(REST), None, ALU.is_ge))
                for k in range(2):
                    ch(V.tensor_scalar(v2[:, 0:1], pcol[:, :], float(TRASH + 1 + P * k), None, ALU.add))
                    ch(V.tensor_tensor(v2[:, 1:2], v2[:, 0:1], v3[:, 0:1], ALU.mult))
                    f = fpos[:, k * NT + FULL:k * NT + FULL + 1]
                    ch(V.tensor_tensor(f, f, v2[:, 1:2], ALU.add))
                    ch(V.tensor_scalar(fpos[:, k * NT + NT - 1:k * NT + NT], v2[:, 0:1], float(2 * P), None, ALU.add))
                ch(V.tensor_scalar(scat_i[:, :, :].rearrange("p k t -> p (k t)"), fpos, -1.0, None, ALU.add))
                ch(V.tensor_scalar(gath_i[:, :, :].rearrange("p k t -> p (k t)"), fpos, -1.0, float(TRASH - 1), ALU.add, ALU.min))
                ch(V.tensor_scalar(est, iota_f[0:1, 0:TT], float(P), None, ALU.mult))
                table(est, ecount, E8, 1, E8 - 1)
                V.tensor_copy(eoff[:, :], ecount).then_inc(routed, 1)
                dve.wait_ge(routed, m + 1)

            def dispatch(m, full):
                def turn(i):
                    for s in range(2):
                        q = 2 * i + s
                        after(dve, disp_done[m][s], i * 32)
                        full(s, q, disp_ready[m])
                if m == 0:
                    turns(dve, NI, turn)
                else:
                    loop(NI, 4, turn)

            def combine(m):
                def turn(i):
                    for s in range(2):
                        t = 2 * i + s
                        dve.wait_ge(y_gathered[m][s], i * 32 + 32)
                        ch(V.scalar_tensor_tensor(tile(x3, t), yg[:, s, 0, :], col(gate[:, 0, :], t), tile(x3, t), ALU.mult, ALU.add))
                        V.scalar_tensor_tensor(tile(x3, t), yg[:, s, 1, :], col(gate[:, 1, :], t), tile(x3, t), ALU.mult, ALU.add).then_inc(comb_used[m], 1)
                loop(NI, 2, turn)
                dve.wait_ge(comb_used[m], NT)

            def plain(s, q, done):
                normalise(q, xn[:, s, :], rstd).then_inc(done, 1)

            def affine(s, q, done):
                ch(normalise(q, xn[:, s, :], rstd))
                ch(V.tensor_tensor(xn[:, s, :], xn[:, s, :], gam, ALU.mult))
                V.tensor_tensor(xn[:, s, :], xn[:, s, :], bet, ALU.add).then_inc(done, 1)

            layernorm_stats(2)
            route_project(1, plain)
            ch(V.tensor_reduce(v1, lg, AX.X, ALU.max))
            V.tensor_tensor(tb, lg, bc(v1), ALU.subtract).then_inc(dve_to_act, 1)
            dve.wait_ge(act_to_dve, 3)
            ch(V.tensor_reduce(v1, ta, AX.X, ALU.add))
            ch(V.reciprocal(v1, v1))
            ch(V.tensor_tensor(pr, ta, bc(v1), ALU.mult))
            masks(pr, 2.0)
            ch(V.tensor_tensor(v3, v1, v2, ALU.add))
            ch(V.tensor_scalar(v3, v3, 1e-9, None, ALU.add))
            ch(V.reciprocal(v3, v3))
            ch(V.tensor_tensor(gate[:, 0, :], v1, v3, ALU.mult))
            ch(V.tensor_tensor(gate[:, 1, :], v2, v3, ALU.mult))
            places(0)
            dispatch(0, plain)

            def mixture(m):
                sm = ffn[m]

                def hidden(q):
                    if m == 0:
                        for part in range(2):
                            dve.wait_ge(sm["act"], q * 2 + (part + 1))
                            ins = V.tensor_tensor(hh[:, part * HALF:(part + 1) * HALF], sil[:, part * HALF:(part + 1) * HALF],
                                                  ps[:, 2 + part, 0:HALF], ALU.mult)
                        ins.then_inc(sm["hh"], 1)
                    else:
                        e = dve.value_load(eoff[0:1, bass.ds(q, 1)] if not isinstance(q, int) else eoff[0:1, q:q + 1], min_val=0, max_val=E8 - 1)
                        dve.wait_ge(sm["h"], q + 1)
                        V.tensor_tensor(sil[:, 0:H1], ps[:, 0, :], b1b[:, bass.ds(e * H1, H1)], ALU.add).then_inc(sm["bias"], 1)

                def result(q, s, i):
                    if m == 1:
                        e = dve.value_load(eoff[0:1, bass.ds(q, 1)] if not isinstance(q, int) else eoff[0:1, q:q + 1], min_val=0, max_val=E8 - 1)
                    dve.wait_ge(sm["y"], q + 1)
                    after(dve, ys_stored[m][s], i * 16)
                    if m == 0:
                        V.tensor_copy(ys[:, s, :], ps[:, 7, 0:C]).then_inc(sm["ys"], 1)
                    else:
                        V.tensor_tensor(ys[:, s, :], ps[:, 7, 0:C], b2b[:, bass.ds(e * C, C)], ALU.add).then_inc(sm["ys"], 1)

                def turn(i):
                    for s in range(2):
                        q = 2 * i + s
                        hidden(q)
                        if s == 1:
                            result(q - 1, 0, i)
                        elif not (isinstance(i, int) and i == 0):
                            result(q - 1, 1, i - 1)
                turns(dve, TT // 2, turn, peel=2)
                result(TT - 1, 1, TT // 2 - 1)

            mixture(0)
            combine(0)

            layernorm_stats(4)
            ch(V.tensor_tensor(cnt, rstd[:, :], dinv[:, :], ALU.mult))

            def scaled(i):
                for s in range(2):
                    t = 2 * i + s
                    ch(normalise(t, tile(a3, t), cnt), wait=False)
            loop(NI, 2, scaled)
            V.memset(v_signal, 0.0).then_inc(hop_start[1], 1)
            hop(1)

            def rescale(i):
                for s in range(2):
                    t = 2 * i + s
                    ch(V.tensor_scalar(tile(a3, t), tile(a3, t), col(dinv2, t), None, ALU.mult), wait=False)
            loop(NI, 2, rescale)
            V.memset(v_signal, 0.0).then_inc(hop_start[2], 1)
            hop(2)

            def logits(i):
                for s in range(2):
                    t = 2 * i + s
                    after(dve, proj[2]["tr"], t - 1)
                    V.tensor_scalar(xn[:, s, :], tile(a3, t), col(dinv, t), None, ALU.mult).then_inc(proj[2]["xn"], 1)
                for s in range(2):
                    t = 2 * i + s
                    dve.wait_ge(proj[2]["mm"], t + 1)
                    ch(V.tensor_tensor(tile(a3, t), ps[:, 2 + s, 0:C], bg, ALU.add))
                    V.tensor_reduce(col(rstd, t), tile(a3, t), AX.X, ALU.max, negate=True).then_inc(proj[2]["ev"], 1)
            loop(NI, 2, logits)
            V.memset(v_signal, 0.0).then_inc(dve_to_act, 1)
            dve.wait_ge(proj[2]["ev"], NT)
            dve.wait_ge(act_to_dve, 5)
            ch(V.tensor_tensor(rstd[:, :], rstd[:, :], dinv2[:, :], ALU.subtract))

            def add_logits(i):
                for s in range(2):
                    t = 2 * i + s
                    ch(V.scalar_tensor_tensor(tile(x3, t), tile(a3, t), col(rstd, t), tile(x3, t), ALU.add, ALU.add), wait=False)
            loop(NI, 2, add_logits)
            ch.sync()

            layernorm_stats(6)
            route_project(3, affine)
            masks(lg, BIG)
            V.tensor_tensor(v3, v2, v1, ALU.subtract).then_inc(dve_to_act, 1)
            dve.wait_ge(act_to_dve, 7)
            ch(V.tensor_scalar(v1, v3, 1.0, None, ALU.add))
            ch(V.reciprocal(gate[:, 0, :], v1))
            ch(V.tensor_tensor(gate[:, 1, :], v3, gate[:, 0, :], ALU.mult))
            places(1)
            dispatch(1, affine)
            mixture(1)
            combine(1)


_INS = ['x', 'src', 'dst', 'edge_weight', 'L0_gnn_weight', 'L0_ffn_router_w', 'L0_ffn_w1', 'L0_ffn_w2', 'L0_ffn_w3',
        'L1_gnn_W', 'L1_gnn_b', 'L1_ffn_gamma', 'L1_ffn_beta', 'L1_ffn_Wr', 'L1_ffn_br',
        'L1_ffn_W1', 'L1_ffn_b1', 'L1_ffn_W2', 'L1_ffn_b2']
_OUT = ((3125, 256), 'float32')


def kernel(**inputs):
    import numpy as _np
    import concourse.bacc as _bacc
    from concourse import mybir as _mybir
    from concourse.bass_utils import run_bass_kernel_spmd as _run

    nc = _bacc.Bacc("TRN2", target_bir_lowering=False, num_devices=1)
    arrays, args = {}, {}
    for name in _INS:
        a = _np.ascontiguousarray(inputs[name])
        arrays[f"in_{name}_dram"] = a
        args[name] = nc.dram_tensor(f"in_{name}_dram", a.shape, _mybir.dt.from_np(a.dtype), kind="ExternalInput").ap()
    out = nc.dram_tensor("out_dram", _OUT[0], _mybir.dt.from_np(_np.dtype(_OUT[1])), kind="ExternalOutput").ap()
    gnn_moe_program(nc, args['x'], args['src'], args['dst'], args['edge_weight'], args['L0_gnn_weight'],
                    args['L0_ffn_router_w'], args['L0_ffn_w1'], args['L0_ffn_w2'], args['L0_ffn_w3'],
                    args['L1_gnn_W'], args['L1_gnn_b'], args['L1_ffn_gamma'], args['L1_ffn_beta'],
                    args['L1_ffn_Wr'], args['L1_ffn_br'], args['L1_ffn_W1'], args['L1_ffn_b1'],
                    args['L1_ffn_W2'], args['L1_ffn_b2'], out)
    r = _run(nc, [arrays], core_ids=[0])
    return r.results[0]["out_dram"]
```

```python
import concourse.bass as bass
from concourse import mybir
from contextlib import ExitStack

FP32 = mybir.dt.float32
FP16 = mybir.dt.float16
BF16 = mybir.dt.bfloat16
I32 = mybir.dt.int32
ALU = mybir.AluOpType
ACT = mybir.ActivationFunctionType
AX = mybir.AxisListType

P = 128
NODES, C = 3125, 256
EDGES = 50000
NT = 26
FULL = NODES // P
REST = NODES - FULL * P
ROWS = NT * P
NB = FULL + 1
EC = 392
ELAST = EDGES - (P - 1) * EC
PADKEY = NT * P
NCH = 416
RANK_AT = 6
GU = 16
HT = NCH // GU
CP = 184
SLOTS = P * NCH
MID = 1600
SU = 4
DU = 14
E8 = 8
H0 = 682
H0C = 6
H0R = H0 - 5 * P
H1 = 512
TT = 56
TRASH = TT * P
XROWS = TRASH + 4 * P
EPS = 1e-5
BIG = 3.0e38
HALF = H0 // 2


class Chain:

    def __init__(self, eng, sem):
        self.eng, self.sem, self.n, self.i, self.per, self.start = eng, sem, 0, None, 0, 0

    def __call__(self, ins, wait=True):
        ins.then_inc(self.sem, 1)
        self.n += 1
        if wait:
            self.sync()

    def at(self):
        if self.i is None:
            return self.n
        return self.i * self.per + (self.start + self.n)

    def sync(self):
        self.eng.wait_ge(self.sem, self.at())

    def loop(self, count, per, body, lo=0):
        if lo == 0:
            body(0)
            lo = 1
        entry = self.n
        with self.eng.Fori(lo, count) as i:
            self.n, self.i, self.per, self.start = 0, i, per, entry - lo * per
            body(i)
            assert self.n == per, (self.n, per)
            self.i, self.n = None, entry + (count - lo) * per


def after(eng, sem, value):
    if isinstance(value, int) and value <= 0:
        return
    eng.wait_ge(sem, value)


def turns(eng, count, body, peel=1):
    for i in range(peel):
        body(i)
    with eng.Fori(peel, count) as i:
        body(i)


def gnn_moe_program(nc, x_in, src, dst, edge_weight, w_gnn0, router0, w1_0, w2_0, w3_0,
                    w_gnn1, b_gnn1, gamma, beta, wr1, br1, w1_1, b1_1, w2_1, b2_1, out):
    ctx = ExitStack()
    with ctx:
        def sb(name, shape, dt=FP32):
            return ctx.enter_context(nc.sbuf_tensor(name, shape, dt))

        def sem(name):
            return ctx.enter_context(nc.semaphore(name))

        def dram(name, shape):
            return nc.dram_tensor(name, shape, FP32, kind="Internal").ap()

        support_t = dram("support_t", (ROWS, C))
        u1_t = dram("u1_t", (ROWS, C))
        u2_t = dram("u2_t", (ROWS, C))
        xs_t = dram("xs_t", (XROWS, C))
        sorted_t = [dram("sorted0_t", (SLOTS, 3)), dram("sorted1_t", (SLOTS + NCH, 2))]
        kept_t = dram("kept_t", (P, 4 * EC))
        y_t = [dram("y0_t", (TRASH, C)), dram("y1_t", (TRASH, C))]
        tables = [support_t, u1_t, u2_t]

        X = sb("X", [P, NT * C])
        A = sb("A", [P, NT * C])
        W = sb("W", [P, 34112])
        S = sb("S", [P, 6 * C])
        iota_f = sb("iota_f", [P, P])
        ident = sb("ident", [P, P])
        below = sb("below", [P, P])
        ones = sb("ones", [P, P])
        iota_h = sb("iota_h", [P, NCH], FP16)
        pcol = sb("pcol", [P, 1])
        low_s = [sb("low0", [P, NCH]), sb("low1", [P, NCH])]
        idx_s = [sb("idx0", [P, NCH], I32), sb("idx1", [P, NCH], I32)]
        wgt_s = sb("wgt_s", [P, NCH])
        goff_sb = sb("goff_sb", [33, NCH + 2], I32)
        goff = [goff_sb[0:1, :], goff_sb[32:33, :]]
        dinv = sb("dinv", [P, NT])
        dinv2 = sb("dinv2", [P, NT])
        mv = sb("mv", [P, NT, 2])
        rstd = sb("rstd", [P, NT])
        stats = sb("stats", [P, 2, 6])
        pair = sb("pair", [P, 2, 2])
        small = sb("small", [P, 192])
        istage = sb("istage", [P, 32], I32)
        pstage = sb("pstage", [P, 2, 12])

        x3 = X[:, :].rearrange("p (t c) -> p t c", c=C)
        a3 = A[:, :].rearrange("p (t c) -> p t c", c=C)

        ps = ctx.enter_context(nc.psum_tensor("ps", [P, 8, 512], FP32))

        xn = S[:, 0:2 * C].rearrange("p (s c) -> p s c", s=2)
        xT = S[:, 2 * C:4 * C].rearrange("p (s c) -> p s c", s=2)
        ot = S[:, 4 * C:6 * C].rearrange("p (s c) -> p s c", s=2)

        def earr(k):
            return X[:, k * EC:(k + 1) * EC]

        key_f, low_f, oth_f, wh_f, wm_f, wl_f, lane_f, chunk_f, pos_f, t1_f, t2_f = [earr(k) for k in range(11)]
        key_i, oth_i, t1_i, t2_i = [earr(k).bitcast(I32) for k in range(11, 15)]
        w_f = earr(15)
        assert 16 * EC <= NT * C
        words0 = X[:, 11 * EC:11 * EC + 3 * CP].rearrange("p (t w) -> p t w", w=3)
        back0 = X[:, 0:3 * NCH].rearrange("p (t w) -> p t w", w=3)
        gs0, gc0 = X[0:1, 8 * EC:8 * EC + NCH], X[0:1, 8 * EC + NCH:8 * EC + 2 * NCH]
        K0 = GU * C + 4 * P
        kept = X[:, K0:K0 + 4 * EC]
        words1 = kept[:, 0:2 * EC].rearrange("p (t w) -> p t w", w=2)
        place1 = kept[:, 2 * EC:3 * EC].bitcast(I32)
        key1 = kept[:, 3 * EC:4 * EC]
        ta1, tb1, pos1 = [S[:, k * EC:(k + 1) * EC] for k in range(3)]
        gs1, gc1 = S[32:33, 0:NCH], S[32:33, NCH:2 * NCH]
        oc = A[:, 0:SU * NCH // 2].bitcast(BF16).rearrange("p (s n) -> p s n", s=SU)
        LO = SU * NCH // 2
        Lh = A[:, LO:LO + SU * 2 * 64].bitcast(FP16).rearrange("p (s k n) -> p s k n", s=SU, k=2)
        LB = LO + SU * 2 * 64
        Lb = A[:, LB:LB + SU * 4 * 64].bitcast(BF16).rearrange("p (s k n) -> p s k n", s=SU, k=4)
        low_oh = S[:, 0:DU * 64].bitcast(BF16).rearrange("p (s n) -> p s n", s=DU)
        tile_oh = S[:, DU * 64:DU * 64 + DU * NT // 2].bitcast(BF16).rearrange("p (s n) -> p s n", s=DU)
        zero = A[:, (NT - 1) * C:NT * C]
        raw13 = A[:, 0:2 * 1536].rearrange("p (w j c) -> p w j c", w=2, j=H0C)
        raw2 = A[:, 3072:3072 + 2 * H0].rearrange("p (m h) -> p m h", m=2)

        W13N = 2 * 2 * H0
        W2N = H0C * C
        W13 = W[:, 0:E8 * W13N]
        W2 = W[:, E8 * W13N:E8 * (W13N + W2N)]
        wg0 = W[:, 0:2 * C].rearrange("p (k n) -> p k n", k=2)
        rwn = W[0:E8, 2 * C:3 * C]
        rwT = sb("rwT", [P, 2, E8])
        o = 0

        def wslice(n):
            nonlocal o
            o += n
            return W[:, o - n:o]

        W1b = wslice(E8 * 2 * H1)
        W2b = wslice(E8 * 4 * C)
        b1b = wslice(E8 * H1)
        b2b = wslice(E8 * C)
        wgT = wslice(2 * C).rearrange("p (k n) -> p k n", k=2)
        wgn = wslice(2 * C).rearrange("p (k n) -> p k n", k=2)
        bg = wslice(C)
        gam = wslice(C)
        bet = wslice(C)
        wr_s = wslice(2 * E8).rearrange("p (k n) -> p k n", k=2)
        br_s = wslice(E8)
        rows1 = wslice(GU * C)
        oh1 = wslice(4 * P)
        rows0 = X[:, 0:GU * C]
        oh0 = X[:, GU * C:GU * C + 4 * P]
        hop_rows = [r.rearrange("p (g c) -> p g c", g=GU) for r in (rows0, rows1, rows1)]
        hop_oh = [r.rearrange("p (g c) -> p g c", g=4) for r in (oh0, oh1, oh1)]

        xs = A[:, 0:2 * C].rearrange("p (s c) -> p s c", s=2)
        fT = A[:, 512:512 + C]
        sil = A[:, 768:768 + H0]
        hh = A[:, 1450:1450 + H0]
        hT = A[:, 2132:2132 + H0C * P]
        ys = A[:, 2900:2900 + 2 * C].rearrange("p (s c) -> p s c", s=2)
        yg = A[:, 3412:3412 + 4 * C].rearrange("p (s k c) -> p s k c", s=2, k=2)
        keptA = A[:, 3412:3412 + 4 * EC]
        words1A = keptA[:, 0:2 * EC].rearrange("p (t w) -> p t w", w=2)
        place1A = keptA[:, 2 * EC:3 * EC].bitcast(I32)
        key1A = keptA[:, 3 * EC:4 * EC]
        back1 = A[:, 5000:5000 + 2 * NCH].rearrange("p (t w) -> p t w", w=2)
        R = 4436
        lg = A[:, R:R + NT * E8].rearrange("p (t e) -> p t e", e=E8)
        pr = A[:, R + 208:R + 416].rearrange("p (t e) -> p t e", e=E8)
        ta = A[:, R + 416:R + 624].rearrange("p (t e) -> p t e", e=E8)
        tb = A[:, R + 624:R + 832].rearrange("p (t e) -> p t e", e=E8)
        MS = A[:, R + 832:R + 832 + 2 * NT * E8].rearrange("p (e c) -> p e c", e=E8)
        v1 = A[:, R + 1248:R + 1248 + NT]
        v2 = A[:, R + 1274:R + 1274 + NT]
        v3 = A[:, R + 1300:R + 1300 + NT]
        fpos = A[:, R + 1326:R + 1326 + 2 * NT]
        ft1 = A[:, R + 1378:R + 1378 + 2 * NT]
        ft2 = A[:, R + 1430:R + 1430 + 2 * NT]
        wrev = A[:, R + 1482:R + 1490]
        gate = sb("gate", [P, 2, NT])
        scat_i = sb("scat_i", [P, 2, NT], I32)
        gath_i = sb("gath_i", [P, 2, NT], I32)
        eoff = sb("eoff", [1, TT], I32)
        v_signal = small[0:1, 190:191]
        cnt = small[:, 0:26]
        incl = small[:, 32:58]
        padn = small[:, 64:90]
        init = small[:, 96:122]
        i1 = small[:, 128:154].bitcast(I32)
        i2 = small[:, 160:186].bitcast(I32)
        est = S[0:1, 0:TT]
        ecount = S[0:1, TT:2 * TT]

        const_ready = sem("const_ready")
        dve_step = sem("dve_step")
        act_step = sem("act_step")
        pool_step = sem("pool_step")
        x_loaded = sem("x_loaded")
        wg0_loaded = sem("wg0_loaded")
        xs_zeroed = sem("xs_zeroed")
        edges_loaded = [sem("edges0_loaded"), sem("edges1_loaded")]
        sorted_zeroed = sem("sorted_zeroed")
        ranked = [sem("ranked0"), sem("ranked1")]
        placed = [[sem(f"placed{k}_{h}") for h in range(2)] for k in range(2)]
        placed_back = [sem("placed0_back"), sem("placed1_back")]
        kept_stored = sem("kept_stored")
        kept_loaded = sem("kept_loaded")
        counted_onehot = sem("counted_onehot")
        edges_cleared = sem("edges_cleared")
        x_free = sem("x_free")
        raw_loaded = sem("raw_loaded")
        raw_transposed = sem("raw_transposed")
        raw_copied = sem("raw_copied")
        gnn1_loaded = sem("gnn1_loaded")
        ffn1_loaded = sem("ffn1_loaded")
        small_mm_in = sem("small_mm_in")
        small_mm_out = sem("small_mm_out")
        x_reloaded = sem("x_reloaded")
        hops_added = [sem(f"hop{h}_added") for h in range(3)]
        hops_mm = [sem(f"hop{h}_mm") for h in range(3)]
        hops_oh = [sem(f"hop{h}_onehot") for h in range(3)]
        row_gathered = [sem(f"row_gathered{g}") for g in range(GU)]
        hop_table = [sem(f"hop{h}_table") for h in range(3)]
        hop_start = [sem(f"hop{h}_start") for h in range(3)]
        sort_onehot = sem("sort_onehot")
        sort_onehot_plain = sem("sort_onehot_plain")
        sort_weighted = sem("sort_weighted")
        sort_mm = sem("sort_mm")
        sort_ready = [sem(f"sort{k}_ready") for k in range(2)]
        proj = [{n: sem(f"proj{k}_{n}") for n in ("xn", "tr", "xt", "mm", "ev")} for k in range(4)]
        support_out = [sem(f"support_out{s}") for s in range(2)]
        routed = sem("routed")
        wgT_ready = sem("wgT_ready")
        dve_to_act = sem("dve_to_act")
        act_to_dve = sem("act_to_dve")
        disp_ready = [sem(f"disp{m}_ready") for m in range(2)]
        disp_done = [[sem(f"disp{m}_done{s}") for s in range(2)] for m in range(2)]
        ffn = [{n: sem(f"ffn{m}_{n}") for n in ("tx", "fT", "h", "act", "hh", "th", "hT", "y", "ys", "bias")} for m in range(2)]
        xs_loaded = [[sem(f"xs{m}_loaded{s}") for s in range(2)] for m in range(2)]
        ys_stored = [[sem(f"ys{m}_stored{s}") for s in range(2)] for m in range(2)]
        y_gathered = [[sem(f"y{m}_gathered{s}") for s in range(2)] for m in range(2)]
        comb_used = [sem(f"comb{m}_used") for m in range(2)]
        out_done = sem("out_done")

        block = ctx.enter_context(nc.Block())
        NI = NT // 2

        def tile(ap3, t):
            if isinstance(t, int):
                return ap3[:, t, :]
            return ap3[:, bass.ds(t, 1), :].rearrange("p a c -> p (a c)")

        def col(ap2, t):
            return ap2[:, bass.ds(t, 1)] if not isinstance(t, int) else ap2[:, t:t + 1]

        def load_edges(eng, arr, vec, done):
            eng.dma_start(arr[0:P - 1, :], vec[0:(P - 1) * EC].rearrange("(p t) -> p t", t=EC)).then_inc(done, 16)
            eng.dma_start(arr[P - 1:P, 0:ELAST], vec[(P - 1) * EC:EDGES].rearrange("(p t) -> p t", p=1)).then_inc(done, 16)

        @block.sync
        def _(sp):
            sp.wait_ge(const_ready, 1)
            sp.dma_start(x3[:, 0:FULL, :], x_in[0:FULL * P, :].rearrange("(t p) c -> p t c", p=P)).then_inc(x_loaded, 16)
            sp.dma_start(x3[0:REST, FULL, :], x_in[FULL * P:NODES, :]).then_inc(x_loaded, 16)
            sp.dma_start(wg0, w_gnn0.rearrange("(k p) n -> p k n", p=P)).then_inc(wg0_loaded, 16)
            sp.dma_start(rwn, router0).then_inc(wg0_loaded, 16)
            sp.wait_ge(const_ready, 2)
            sp.dma_start(xs_t.rearrange("(n p) c -> p n c", p=P),
                         zero.rearrange("p (a c) -> p a c", a=1).to_broadcast([P, XROWS // P, C])).then_inc(xs_zeroed, 16)
            for k in range(2):
                w = 3 - k
                sp.dma_start(sorted_t[k][0:SLOTS, :].rearrange("(p n) w -> p (n w)", p=P).rearrange("p (n m) -> p n m", m=NCH // 2),
                             zero[:, 0:NCH // 2].rearrange("p (a m) -> p a m", a=1).to_broadcast([P, 2 * w, NCH // 2])
                             ).then_inc(sorted_zeroed, 16)
            sp_rows = support_t.rearrange("(t p) c -> t p c", p=P)

            def store_support(i):
                for s in range(2):
                    q = 2 * i + s
                    sp.wait_ge(proj[0]["ev"], q + 1)
                    sp.nop(nofuse=True)
                    dstrow = sp_rows[q, :, :] if isinstance(q, int) else sp_rows[bass.ds(q, 1), :, :].rearrange("t p c -> (t p) c")
                    sp.dma_start(dstrow, ot[:, s, :]).then_inc(support_out[s], 16)
            turns(sp, NI, store_support)

            for h in range(2):
                sp.wait_ge(placed[0][h], 64 * (CP // 8))
            sp.wait_ge(sort_mm, EC - CP)
            sp.dma_start(back0, sorted_t[0].rearrange("(p n) w -> p n w", p=P)).then_inc(placed_back[0], 16)
            sp.wait_ge(edges_cleared, 2)
            load_edges(sp, place1, dst, edges_loaded[1])
            load_edges(sp, ta1.bitcast(I32), src, edges_loaded[1])
            sp.wait_ge(ranked[1], 1)
            sp.dma_start(kept_t, kept).then_inc(kept_stored, 16)
            sp.wait_ge(kept_stored, 16)

            sp.wait_ge(hops_added[0], NCH)
            sp.wait_ge(x_reloaded, 1)
            sp.dma_start(x3[:, 0:FULL, :], x_in[0:FULL * P, :].rearrange("(t p) c -> p t c", p=P)).then_inc(x_loaded, 16)
            sp.dma_start(x3[0:REST, FULL, :], x_in[FULL * P:NODES, :]).then_inc(x_loaded, 16)

            sp.wait_ge(routed, 1)
            sp.dma_start(keptA, kept_t).then_inc(kept_loaded, 16)

            def mixture(m):
                for s in range(2):
                    sp.wait_ge(disp_done[m][s], 32 * NI)
                xr = xs_t.rearrange("(t p) c -> t p c", p=P)
                yr = y_t[m].rearrange("(t p) c -> t p c", p=P)

                def load(q, s, n):
                    if not (isinstance(n, int) and n < 2):
                        sp.wait_ge(ffn[m]["tx"], n - 1)
                        sp.nop(nofuse=True)
                    row = xr[q, :, :] if isinstance(q, int) else xr[bass.ds(q, 1), :, :].rearrange("t p c -> (t p) c")
                    sp.dma_start(xs[:, s, :], row).then_inc(xs_loaded[m][s], 16)

                def store(q, s):
                    sp.wait_ge(ffn[m]["ys"], q + 1)
                    sp.nop(nofuse=True)
                    row = yr[q, :, :] if isinstance(q, int) else yr[bass.ds(q, 1), :, :].rearrange("t p c -> (t p) c")
                    sp.dma_start(row, ys[:, s, :]).then_inc(ys_stored[m][s], 16)

                load(0, 0, 0)
                load(1, 1, 1)

                with sp.Fori(1, TT // 2) as i:
                    for s in range(2):
                        load(2 * i + s, s, 2 * i + s)
                        store(2 * i + s - 2, s)
                store(TT - 2, 0)
                store(TT - 1, 1)

            mixture(0)
            for h in range(2):
                sp.wait_ge(placed[1][h], 64 * (EC // 8))
            sp.dma_start(back1, sorted_t[1][0:SLOTS, :].rearrange("(p n) w -> p n w", p=P)).then_inc(placed_back[1], 16)
            sp.wait_ge(ffn[0]["y"], TT)
            sp.dma_start(wgn, w_gnn1.rearrange("(m p) c -> p m c", p=P)).then_inc(gnn1_loaded, 16)
            sp.dma_start(bg, b_gnn1.rearrange("(a n) -> a n", a=1).to_broadcast([P, C])).then_inc(gnn1_loaded, 16)
            sp.dma_start(gam, gamma.rearrange("(a n) -> a n", a=1).to_broadcast([P, C])).then_inc(gnn1_loaded, 16)
            sp.dma_start(bet, beta.rearrange("(a n) -> a n", a=1).to_broadcast([P, C])).then_inc(gnn1_loaded, 16)
            sp.dma_start(wr_s, wr1.rearrange("(k p) e -> p k e", p=P)).then_inc(gnn1_loaded, 16)
            sp.dma_start(br_s, br1.rearrange("(a n) -> a n", a=1).to_broadcast([P, E8])).then_inc(gnn1_loaded, 16)
            for h in (1, 2):
                sp.wait_ge(hop_start[h], 1)
                sp.dma_start(tables[h].rearrange("(t p) c -> p t c", p=P), a3).then_inc(hop_table[h], 16)
                if h == 1:
                    sp.dma_start(W1b.rearrange("p (e k n) -> p e k n", e=E8, k=2),
                                 w1_1.rearrange("e (k p) n -> p e k n", p=P)).then_inc(ffn1_loaded, 16)
                    sp.dma_start(W2b.rearrange("p (e k n) -> p e k n", e=E8, k=4),
                                 w2_1.rearrange("e (k p) n -> p e k n", p=P)).then_inc(ffn1_loaded, 16)
                    sp.dma_start(b1b, b1_1.rearrange("(a e) n -> a (e n)", a=1).to_broadcast([P, E8 * H1])).then_inc(ffn1_loaded, 16)
                    sp.dma_start(b2b, b2_1.rearrange("(a e) n -> a (e n)", a=1).to_broadcast([P, E8 * C])).then_inc(ffn1_loaded, 16)
            mixture(1)
            sp.wait_ge(comb_used[1], NT)
            sp.dma_start(out[0:FULL * P, :].rearrange("(t p) c -> p t c", p=P), x3[:, 0:FULL, :]).then_inc(out_done, 16)
            sp.dma_start(out[FULL * P:NODES, :], x3[0:REST, FULL, :]).then_inc(out_done, 16)
            sp.wait_ge(out_done, 32)
            sp.wait_ge(xs_zeroed, 16)
            sp.wait_ge(sorted_zeroed, 32)
            for s in range(2):
                sp.wait_ge(support_out[s], 16 * NI)
                for m in range(2):
                    sp.wait_ge(ys_stored[m][s], 16 * TT // 2)
                    sp.wait_ge(disp_done[m][s], 32 * NI)
            for h in (1, 2):
                sp.wait_ge(hop_table[h], 16)

        @block.gpsimd
        def _(pool):
            pool.iota(iota_f[:, :], [[1, P]], base=0, channel_multiplier=0, allow_small_or_imprecise_dtypes=True).then_inc(pool_step, 1)
            pool.iota(iota_h[:, :], [[1, NCH]], base=0, channel_multiplier=0, allow_small_or_imprecise_dtypes=True).then_inc(pool_step, 1)
            pool.iota(pcol[:, :], [[0, 1]], base=0, channel_multiplier=1, allow_small_or_imprecise_dtypes=True).then_inc(pool_step, 1)
            pch = Chain(pool, pool_step)
            pch.n = 3

            def stage(*pairs):
                for dst_ap, src_ap in pairs:
                    pch(pool.tensor_copy(dst_ap, src_ap), wait=False)
                pch.sync()
                pool.nop(nofuse=True)

            def at(ap, lo, n):
                return ap[:, lo:lo + n] if isinstance(lo, int) else ap[:, bass.ds(lo, n)]

            def hop(h):
                edges = idx_s[0 if h == 0 else 1]
                rows = hop_rows[h]

                def turn(i):
                    for half in range(2):
                        g0 = i * GU + 8 * half
                        after(pool, hops_mm[h], g0 - 8)
                        st = istage[:, 8 * half:8 * half + 8]
                        stage((st, at(edges, g0, 8)))
                        for g in range(8):
                            pool.indirect_dma_start(rows[:, 8 * half + g, :], None, tables[h],
                                                    bass.IndirectOffsetOnAxis(ap=st[:, g:g + 1], axis=0)
                                                    ).then_inc(row_gathered[8 * half + g], 16)
                pch.loop(HT, 2, turn)

            def place(k, places, words, cols):
                w = 3 - k

                def turn(i):
                    for half in range(2):
                        c0 = i * 8 + 4 * half
                        after(pool, placed[k][half], i * 64)
                        st = istage[:, 24 + 4 * half:28 + 4 * half]
                        pst = pstage[:, half, 0:4 * w].rearrange("p (t w) -> p t w", w=w)
                        stage((st, at(places, c0, 4)), (pst, words[:, c0:c0 + 4, :] if isinstance(c0, int) else words[:, bass.ds(c0, 4), :]))
                        for g in range(4):
                            pool.indirect_dma_start(sorted_t[k], bass.IndirectOffsetOnAxis(ap=st[:, g:g + 1], axis=0),
                                                    pst[:, g, :], None).then_inc(placed[k][half], 16)
                pch.loop(cols // 8, 4, turn)

            def pair_of(ap, t):
                return ap[:, :, t] if isinstance(t, int) else ap[:, :, bass.ds(t, 1)].rearrange("p k a -> p (k a)")

            def mixture_dispatch(m):
                def turn(i):
                    for s in range(2):
                        t = 2 * i + s
                        pool.wait_ge(disp_ready[m], t + 1)
                        st = istage[:, 16 + 2 * s:18 + 2 * s]
                        after(pool, disp_done[m][s], i * 32)
                        stage((st, pair_of(scat_i, t)))
                        for k in range(2):
                            pool.indirect_dma_start(xs_t, bass.IndirectOffsetOnAxis(ap=st[:, k:k + 1], axis=0),
                                                    xn[:, s, :], None).then_inc(disp_done[m][s], 16)
                pch.loop(NI, 2, turn)

            def mixture_gather(m):
                for s in range(2):
                    pool.wait_ge(ys_stored[m][s], 16 * TT // 2)

                def turn(i):
                    for s in range(2):
                        t = 2 * i + s
                        after(pool, comb_used[m], t - 1)
                        st = istage[:, 20 + 2 * s:22 + 2 * s]
                        stage((st, pair_of(gath_i, t)))
                        for k in range(2):
                            pool.indirect_dma_start(yg[:, s, k, :], None, y_t[m],
                                                    bass.IndirectOffsetOnAxis(ap=st[:, k:k + 1], axis=0)
                                                    ).then_inc(y_gathered[m][s], 16)
                pch.loop(NI, 2, turn)

            pool.wait_ge(edges_cleared, 1)
            load_edges(pool, key_i, src, edges_loaded[0])
            load_edges(pool, oth_i, dst, edges_loaded[0])
            load_edges(pool, w_f, edge_weight, edges_loaded[0])
            pool.wait_ge(sorted_zeroed, 32)
            pool.wait_ge(ranked[0], 1)
            place(0, t2_i, words0, CP)
            for s in range(2):
                pool.wait_ge(support_out[s], 16 * NI)
            pool.wait_ge(sort_ready[0], 1)
            pool.wait_ge(hop_start[0], 1)
            hop(0)
            pool.wait_ge(xs_zeroed, 16)
            mixture_dispatch(0)
            pool.wait_ge(kept_loaded, 16)
            place(1, place1A, words1A, EC)
            mixture_gather(0)
            pool.wait_ge(sort_ready[1], 1)
            pool.wait_ge(hop_table[1], 16)
            hop(1)
            pool.wait_ge(hop_table[2], 16)
            hop(2)
            mixture_dispatch(1)
            mixture_gather(1)

        @block.tensor
        def _(pe):
            def project(k, rhs, n):
                sm = proj[k]

                def product(q, s):
                    pe.wait_ge(sm["xt"], q + 1)
                    after(pe, sm["ev"], q - 1)
                    for b in range(2):
                        last = nc.tensor.matmul(ps[:, 2 + s, 0:n], xT[:, s, b * P:(b + 1) * P], rhs[:, b, :],
                                                start=(b == 0), stop=(b == 1))
                    last.then_inc(sm["mm"], 1)

                def turn(i):
                    for s in range(2):
                        q = 2 * i + s
                        pe.wait_ge(sm["xn"], q + 1)
                        after(pe, sm["xt"], q - 1)
                        for b in range(2):
                            last = nc.tensor.transpose(ps[:, s, b * P:(b + 1) * P], xn[:, s, b * P:(b + 1) * P], ident[:, :])
                        last.then_inc(sm["tr"], 1)
                    if not (isinstance(i, int) and i == 0):
                        for s in range(2):
                            product(2 * i - 2 + s, s)
                turns(pe, NI, turn, peel=2)
                for s in range(2):
                    product(NT - 2 + s, s)

            pe.wait_ge(const_ready, 4)
            pe.wait_ge(wg0_loaded, 32)
            project(0, wg0, C)
            for b in range(2):
                last = nc.tensor.transpose(ps[:, 4, b * E8:(b + 1) * E8], rwn[:, b * P:(b + 1) * P], ident[0:E8, 0:E8])
            last.then_inc(small_mm_out, 1)

            def prefix(k, n):
                pe.wait_ge(small_mm_in, k)
                nc.tensor.matmul(ps[:, 7, 0:n], below[:, :], cnt[:, 0:n], start=True, stop=True)
                nc.tensor.matmul(ps[:, 7, 32:32 + n], ones[:, :], cnt[:, 0:n], start=True, stop=True).then_inc(small_mm_out, 1)

            def prep(e):
                pe.wait_ge(raw_loaded, e * 96 + 96)
                for w in range(2):
                    for b in range(2):
                        after(pe, raw_copied, e * 12 + 2 * b + (2 if w else -6))
                        for j in range(H0C):
                            n = P if j < 5 else H0R
                            last = nc.tensor.transpose(ps[:, 2 * b + j // 4, (j % 4) * P:(j % 4) * P + n],
                                                       raw13[0:n, w, j, b * P:(b + 1) * P], ident[0:n, 0:n])
                            if j == 3 or j == 5:
                                last.then_inc(raw_transposed, 1)
                after(pe, raw_copied, e * 12)
                for j in range(H0C):
                    n = P if j < 5 else H0R
                    for mb in range(2):
                        last = nc.tensor.transpose(ps[0:n, 4 + j // 2, j % 2 * C + mb * P:j % 2 * C + (mb + 1) * P],
                                                   raw2[:, mb, j * P:j * P + n], ident[:, :])
                    if j % 2:
                        last.then_inc(raw_transposed, 1)
            pe.wait_ge(proj[0]["ev"], NT)
            pe.wait_ge(act_step, 1)
            prep(0)
            prefix(1, NB)
            with pe.Fori(1, E8) as e:
                prep(e)

            def sort_columns(i):
                for s in range(SU):
                    q = SU * i + s
                    pe.wait_ge(sort_onehot, q + 1)
                    pe.wait_ge(sort_weighted, q + 1)
                    start = isinstance(i, int) and s == 0
                    for j in range(5):
                        piece = Lh[:, s, j, :] if j < 2 else Lb[:, s, j - 1, :]
                        last = nc.tensor.matmul(ps[:, j, 0:NCH], piece, oc[:, s, :],
                                                start=start, stop=not start, skip_group_check=True)
                    last.then_inc(sort_mm, 1)

            def hop(h):
                rows, oh = hop_rows[h], hop_oh[h]

                def turn(i):
                    for g in range(GU):
                        q = GU * i + g
                        pe.wait_ge(row_gathered[g], i * 16 + (16 * HT * h + 16))
                        pe.wait_ge(hops_oh[h], q + 1)
                        after(pe, hops_added[h], q - 3)
                        nc.tensor.matmul(ps[:, g % 4, 0:C], oh[:, g % 4, :], rows[:, g, :],
                                         start=True, stop=True).then_inc(hops_mm[h], 1)
                if h == 0:
                    turns(pe, RANK_AT, turn)
                    prefix(2, NB)
                    with pe.Fori(RANK_AT, HT) as i:
                        turn(i)
                else:
                    turns(pe, HT, turn)

            def mixture(m):
                sm = ffn[m]
                nj = H0C if m == 0 else 4

                def rows_of(j):
                    return H0R if (m == 0 and j == 5) else P

                def turn_x(q, s, i):
                    pe.wait_ge(xs_loaded[m][s], i * 16 + 16)
                    for b in range(2):
                        last = nc.tensor.transpose(ps[:, 6, b * P:(b + 1) * P], xs[:, s, b * P:(b + 1) * P], ident[:, :])
                    last.then_inc(sm["tx"], 1)

                def turn_h(q):
                    pe.wait_ge(sm["hh"], q + 1)
                    for j in range(nj):
                        n = rows_of(j)
                        last = nc.tensor.transpose(ps[0:n, 4 + j // 4, (j % 4) * P:(j % 4 + 1) * P], hh[:, j * P:j * P + n], ident[:, :])
                    last.then_inc(sm["th"], 1)

                def up(q, e):
                    pe.wait_ge(sm["fT"], q + 1)
                    if m == 0:
                        for part in range(4):
                            for b in range(2):
                                at = b * 2 * H0 + part * HALF
                                last = nc.tensor.matmul(ps[:, part, 0:HALF], fT[:, b * P:(b + 1) * P],
                                                        W13[:, bass.ds(e * W13N + at, HALF)], start=(b == 0), stop=(b == 1))
                        last.then_inc(sm["h"], 1)
                    else:
                        for b in range(2):
                            last = nc.tensor.matmul(ps[:, 0, :], fT[:, b * P:(b + 1) * P],
                                                    W1b[:, bass.ds(e * (2 * H1) + b * H1, H1)], start=(b == 0), stop=(b == 1))
                        last.then_inc(sm["h"], 1)

                def down(q, e, count=None):
                    pe.wait_ge(sm["hT"], q + 1)
                    after(pe, sm["ys"], q)
                    w, n_w = (W2, W2N) if m == 0 else (W2b, 4 * C)
                    if count is not None:
                        pe.wait_ge(counted_onehot, count + 1)
                        for j in range(DU):
                            nc.tensor.matmul(ps[:, 7, C:C + NT], low_oh[:, j, :], tile_oh[:, j, :],
                                             start=(j == 0), stop=(j == DU - 1))
                    for j in range(nj):
                        n = rows_of(j)
                        last = nc.tensor.matmul(ps[:, 7, 0:C], hT[0:n, j * P:(j + 1) * P],
                                                w[0:n, bass.ds(e * n_w + j * C, C)], start=(j == 0), stop=(j == nj - 1))
                    last.then_inc(sm["y"], 1)

                def expert(q):
                    return pe.value_load(eoff[0:1, bass.ds(q, 1)] if not isinstance(q, int) else eoff[0:1, q:q + 1], min_val=0, max_val=E8 - 1)

                def turn(i):
                    for s in range(2):
                        q = 2 * i + s
                        turn_x(q, s, i)
                        if not (isinstance(i, int) and s == 0):
                            turn_h(q - 1)
                        up(q, expert(q))
                        if not (isinstance(i, int) and s == 0):
                            down(q - 1, expert(q - 1), i if m == 0 and s == 1 else None)
                turns(pe, TT // 2, turn)
                turn_h(TT - 1)
                down(TT - 1, expert(TT - 1))

            pe.wait_ge(raw_copied, 12 * E8)
            pe.wait_ge(raw_copied, 12 * E8)
            turns(pe, (EC - CP) // SU, sort_columns)
            hop(0)
            pe.wait_ge(act_step, 1)
            project(1, rwT, E8)
            prefix(3, E8)
            pe.wait_ge(routed, 1)
            mixture(0)
            pe.wait_ge(gnn1_loaded, 16 * 6)
            for b in range(2):
                for mb in range(2):
                    last = nc.tensor.transpose(ps[:, b, mb * P:(mb + 1) * P], wgn[:, mb, b * P:(b + 1) * P], ident[:, :])
            last.then_inc(small_mm_out, 1)
            hop(1)
            hop(2)
            pe.wait_ge(wgT_ready, 1)
            project(2, wgT, C)
            project(3, wr_s, E8)
            prefix(4, E8)
            pe.wait_ge(routed, 2)
            pe.wait_ge(ffn1_loaded, 16 * 4)
            mixture(1)

        @block.scalar
        def _(act):
            AF = nc.scalar.activation

            def project(k, evacuate):
                sm = proj[k]

                def evacuation(q, s, n):
                    act.wait_ge(sm["mm"], q + 1)
                    after(act, support_out[s], n * 16)
                    AF(ot[:, s, :], ps[:, 2 + s, 0:C], ACT.Copy).then_inc(sm["ev"], 1)

                def turn(i):
                    for s in range(2):
                        q = 2 * i + s
                        act.wait_ge(sm["tr"], q + 1)
                        after(act, sm["mm"], q - 1)
                        AF(xT[:, s, :], ps[:, s, 0:C], ACT.Copy).then_inc(sm["xt"], 1)
                    if evacuate and not (isinstance(i, int) and i == 0):
                        for s in range(2):
                            evacuation(2 * i - 2 + s, s, i - 1)
                turns(act, NI, turn, peel=2)
                if evacuate:
                    for s in range(2):
                        evacuation(NT - 2 + s, s, NI - 1)

            def root(k):
                act.wait_ge(dve_to_act, k)
                AF(rstd[:, :], rstd[:, :], ACT.Sqrt).then_inc(act_to_dve, 1)

            root(1)
            project(0, True)
            act.wait_ge(small_mm_out, 1)
            AF(rwT[:, :, :].rearrange("p k e -> p (k e)"), ps[:, 4, 0:2 * E8], ACT.Copy).then_inc(act_step, 1)

            def prep(e):
                if isinstance(e, int):
                    act.wait_ge(const_ready, 3)
                    act.wait_ge(proj[0]["mm"], NT)
                else:
                    act.wait_ge(raw_transposed, e * 11)
                act.nop(nofuse=True)
                for w, t in ((0, w1_0), (1, w3_0)):
                    tv = t[e, :, :] if isinstance(e, int) else t[bass.ds(e, 1), :, :].rearrange("a h c -> (a h) c")
                    act.dma_start(raw13[:, w, 0:5, :], tv[0:5 * P, :].rearrange("(j p) c -> p j c", p=P)).then_inc(raw_loaded, 16)
                    act.dma_start(raw13[0:H0R, w, 5, :], tv[5 * P:H0, :]).then_inc(raw_loaded, 16)
                tv = w2_0[e, :, :] if isinstance(e, int) else w2_0[bass.ds(e, 1), :, :].rearrange("a c h -> (a c) h")
                act.dma_start(raw2, tv.rearrange("(m p) h -> p m h", p=P)).then_inc(raw_loaded, 32)
                n = 0
                for w in range(2):
                    for b in range(2):
                        for half in range(2):
                            n += 1
                            width = 512 if half == 0 else H0 - 512
                            at = b * 2 * H0 + w * H0 + half * 512
                            act.wait_ge(raw_transposed, e * 11 + n)
                            AF(W13[:, bass.ds(e * W13N + at, width)] if not isinstance(e, int) else W13[:, at:at + width],
                               ps[:, 2 * b + half, 0:width], ACT.Copy).then_inc(raw_copied, 1)
                for j0, j1, r, bank, at in ((0, 2, P, 4, 0), (2, 4, P, 5, 0), (4, 5, P, 6, 0), (5, 6, H0R, 6, C)):
                    n += at == 0
                    width = (j1 - j0) * C
                    act.wait_ge(raw_transposed, e * 11 + n)
                    AF(W2[0:r, bass.ds(e * W2N + j0 * C, width)] if not isinstance(e, int) else W2[0:r, j0 * C:j0 * C + width],
                       ps[0:r, bank, at:at + width], ACT.Copy).then_inc(raw_copied, 1)
            turns(act, E8, prep)

            def weigh(i):
                for s in range(SU):
                    q = SU * i + s
                    act.wait_ge(sort_onehot_plain, q + 1)
                    after(act, sort_mm, q - SU + 1)
                    for j, part in enumerate((wh_f, wm_f, wl_f)):
                        last = AF(Lb[:, s, 1 + j, :], Lb[:, s, 0, :], ACT.Copy, scale=col(part, q + CP))
                    last.then_inc(sort_weighted, 1)
            turns(act, (EC - CP) // SU, weigh)

            def mixture(m):
                sm = ffn[m]

                def transposed_x(q):
                    act.wait_ge(sm["tx"], q + 1)
                    AF(fT, ps[:, 6, 0:C], ACT.Copy).then_inc(sm["fT"], 1)

                def transposed_h(q):
                    act.wait_ge(sm["th"], q + 1)
                    if m == 0:
                        AF(hT[:, 0:512], ps[:, 4, :], ACT.Copy)
                        AF(hT[:, 512:640], ps[:, 5, 0:P], ACT.Copy)
                        AF(hT[0:H0R, 640:768], ps[0:H0R, 5, P:2 * P], ACT.Copy).then_inc(sm["hT"], 1)
                    else:
                        AF(hT[:, 0:512], ps[:, 4, :], ACT.Copy).then_inc(sm["hT"], 1)

                def nonlinear(q):
                    if m == 0:
                        act.wait_ge(sm["h"], q + 1)
                        for part in range(2):
                            AF(sil[:, part * HALF:(part + 1) * HALF], ps[:, part, 0:HALF], ACT.Silu).then_inc(sm["act"], 1)
                    else:
                        act.wait_ge(sm["bias"], q + 1)
                        AF(hh[:, 0:H1], sil[:, 0:H1], ACT.Gelu).then_inc(sm["hh"], 1)

                def turn(i):
                    for s in range(2):
                        q = 2 * i + s
                        transposed_x(q)
                        if not (isinstance(i, int) and s == 0):
                            transposed_h(q - 1)
                        nonlinear(q)
                turns(act, TT // 2, turn)
                transposed_h(TT - 1)

            root(2)
            project(1, False)
            act.wait_ge(dve_to_act, 3)
            AF(ta, tb, ACT.Exp).then_inc(act_to_dve, 1)
            mixture(0)
            act.wait_ge(small_mm_out, 5)
            AF(wgT[:, 0, :], ps[:, 0, 0:C], ACT.Copy)
            AF(wgT[:, 1, :], ps[:, 1, 0:C], ACT.Copy).then_inc(wgT_ready, 1)
            act.wait_ge(dve_to_act, 4)
            AF(dinv[:, :], dinv2[:, :], ACT.Sqrt)
            root(4)
            project(2, False)
            act.wait_ge(dve_to_act, 5)

            def exps(i):
                for s in range(2):
                    t = 2 * i + s
                    after(act, act_step, t)
                    AF(xn[:, s, :], tile(a3, t), ACT.Exp, bias=col(rstd, t), accum_out=col(dinv2, t)).then_inc(act_step, 1)
            turns(act, NI, exps)
            act.wait_ge(act_step, 1 + NT)
            AF(dinv2[:, :], dinv2[:, :], ACT.Ln).then_inc(act_to_dve, 1)
            root(6)
            project(3, False)
            act.wait_ge(dve_to_act, 7)
            AF(v3, v3, ACT.Exp).then_inc(act_to_dve, 1)
            mixture(1)

        @block.vector
        def _(dve):
            V = nc.vector
            ch = Chain(dve, dve_step)

            loop = ch.loop

            def tile_stats(i):
                for s in range(2):
                    ch(V.bn_stats(stats[:, s, :], tile(x3, 2 * i + s)), wait=(s == 1))
                dve.nop(nofuse=True)
                for s in range(2):
                    ch(V.bn_aggr(pair[:, s, :], stats[:, s, :]), wait=(s == 1))
                ch(V.tensor_copy(mv[:, bass.ds(2 * i, 2), :] if not isinstance(i, int) else mv[:, 0:2, :], pair[:, :, :]))

            def inverse_root(k):
                V.tensor_scalar(rstd[:, :], mv[:, :, 1], EPS, None, ALU.add).then_inc(dve_to_act, 1)
                dve.wait_ge(act_to_dve, k)
                ch(V.reciprocal(rstd[:, :], rstd[:, :]))

            def layernorm_stats(k):
                loop(NI, 5, tile_stats)
                inverse_root(k)

            def normalise(t, out_ap, scale):
                return V.tensor_scalar(out_ap, tile(x3, t), mv_mean(t), col(scale, t), ALU.subtract, ALU.mult)

            def mv_mean(t):
                return mv[:, bass.ds(t, 1), 0:1].rearrange("p a b -> p (a b)") if not isinstance(t, int) else mv[:, t, 0:1]

            ch(V.memset(small[:, :], 0.0), wait=False)
            ch(V.memset(x3[:, FULL:NT, :], 0.0))
            V.memset(zero, 0.0).then_inc(const_ready, 1)
            V.memset(ones[:, :], 1.0).then_inc(const_ready, 1)
            dve.wait_ge(pool_step, 3)
            V.tensor_scalar(ident[:, :], iota_f[:, :], pcol[:, :], None, ALU.is_equal).then_inc(const_ready, 1)
            V.tensor_scalar(below[:, :], iota_f[:, :], pcol[:, :], None, ALU.is_gt).then_inc(const_ready, 1)

            dve.wait_ge(x_loaded, 32)
            layernorm_stats(1)

            def give(i):
                for s in range(2):
                    q = 2 * i + s
                    after(dve, proj[0]["tr"], q - 1)
                    normalise(q, xn[:, s, :], rstd).then_inc(proj[0]["xn"], 1)
            turns(dve, NI, give)

            def padded_ends(n, bits):
                ch(V.tensor_scalar(i1[:, 0:n], ps[:, 7, 32:32 + n], float((1 << bits) - 1), None, ALU.add))
                ch(V.tensor_scalar(i2[:, 0:n], i1[:, 0:n], bits, bits, ALU.arith_shift_right, ALU.logical_shift_left))
                ch(V.tensor_copy(padn[:, 0:n], i2[:, 0:n]))
                ch(V.tensor_tensor_scan(incl[:, 0:n], padn[:, 0:n], padn[:, 0:n], 0.0, ALU.add, ALU.max))
                ch(V.tensor_tensor(init[:, 0:n], incl[:, 0:n], padn[:, 0:n], ALU.subtract))
                ch(V.tensor_tensor(init[:, 0:n], init[:, 0:n], ps[:, 7, 0:n], ALU.add))

            def table(starts, count, n, width, ends, row=0):
                ch(V.memset(count, 0.0))
                for b in range(n):
                    ch(V.scalar_tensor_tensor(count, starts, incl[row:row + 1, b:b + 1], count, ALU.is_ge, ALU.add))
                ch(V.tensor_scalar(count, count, float(ends), float(width), ALU.min, ALU.mult))

            def split_key(key, low_out, tile_out, low_i, tile_i):
                ch(V.tensor_scalar(tile_i, key, 7, None, ALU.arith_shift_right), wait=False)
                ch(V.tensor_scalar(low_i, key, P - 1, None, ALU.bitwise_and))
                ch(V.tensor_copy(tile_out, tile_i), wait=False)
                ch(V.tensor_scalar(low_out, low_i, 1.0, None, ALU.add))

            def running(b, key, bucket, first, oh_t, scan_t, pos):
                ch(V.tensor_scalar(oh_t, key, bucket, None, ALU.is_equal))
                ch(V.tensor_tensor_scan(scan_t, oh_t, oh_t, first, ALU.add, ALU.max))
                ch(V.tensor_tensor(scan_t, oh_t, scan_t, ALU.mult))
                ch(V.tensor_tensor(pos, pos, scan_t, ALU.add))

            def offsets(k, gs, gc, row):
                ch(V.tensor_scalar(gs, iota_h[row:row + 1, 0:NCH], float(P), None, ALU.mult))
                table(gs, gc, NB, C, NB - 1, row)
                ch(V.memset(goff[k][:, 0:2], 0), wait=False)
                ch(V.tensor_copy(goff[k][:, 2:NCH + 2], gc))

            dve.wait_ge(proj[0]["xn"], NT)
            V.memset(key_i, PADKEY)
            V.memset(w_f, 0.0)
            V.memset(oth_i, 0).then_inc(edges_cleared, 1)
            dve.wait_ge(edges_loaded[0], 96)
            split_key(key_i, low_f, key_f, t2_i, t1_i)
            ch(V.tensor_scalar(oth_f, oth_i, -float(MID), None, ALU.add), wait=False)
            for b in range(NB):
                ch(V.tensor_scalar((t1_f, t2_f, pos_f, lane_f)[b % 4], key_f, float(b), None, ALU.is_equal, ALU.add,
                                   accum_out=cnt[:, b:b + 1]), wait=(b % 4 == 3))
            ch.sync()
            V.memset(pos_f, 0.0).then_inc(small_mm_in, 1)
            bf = t1_i.bitcast(BF16)[:, 0:EC]
            for n, part in enumerate((wh_f, wm_f, wl_f)):
                ch(V.tensor_copy(bf, w_f if n == 0 else t1_f))
                ch(V.tensor_copy(part, bf))
                if n < 2:
                    ch(V.tensor_tensor(t1_f, w_f if n == 0 else t1_f, part, ALU.subtract))
            for n, part in enumerate((low_f, oth_f, w_f)):
                ch(V.tensor_copy(words0[:, :, n], part[:, 0:CP]), wait=False)
            dve.wait_ge(small_mm_out, 2)
            padded_ends(NB, 7)
            for b in range(NB):
                running(b, key_f, float(b), init[:, b:b + 1], t1_f, t2_f, pos_f)
            ch(V.tensor_scalar(t1_i, pos_f, -1.0, None, ALU.add))
            ch(V.tensor_scalar(t2_i, t1_i, P - 1, None, ALU.bitwise_and), wait=False)
            ch(V.tensor_scalar(t1_i, t1_i, 7, None, ALU.arith_shift_right))
            ch(V.tensor_copy(lane_f, t2_i), wait=False)
            ch(V.tensor_copy(chunk_f, t1_i))
            V.scalar_tensor_tensor(t2_i, lane_f, float(NCH), chunk_f, ALU.mult, ALU.add).then_inc(ranked[0], 1)
            dve.wait_ge(raw_transposed, 11 * E8)

            def sort_columns(i):
                for s in range(SU):
                    q = SU * i + s
                    c = q + CP
                    after(dve, sort_mm, q - SU + 1)
                    V.tensor_scalar(Lb[:, s, 0, :], iota_h[:, 0:P], col(lane_f, c), None, ALU.is_equal).then_inc(sort_onehot_plain, 1)
                    V.tensor_scalar(oc[:, s, :], iota_h[:, :], col(chunk_f, c), None, ALU.is_equal)
                    V.tensor_scalar(Lh[:, s, 0, :], iota_h[:, 0:P], col(lane_f, c), col(low_f, c), ALU.is_equal, ALU.mult)
                    V.tensor_scalar(Lh[:, s, 1, :], iota_h[:, 0:P], col(lane_f, c), col(oth_f, c), ALU.is_equal, ALU.mult).then_inc(sort_onehot, 1)
            turns(dve, (EC - CP) // SU, sort_columns)
            offsets(0, gs0, gc0, 0)
            dve.wait_ge(sort_mm, EC - CP)
            dve.wait_ge(placed_back[0], 16)
            ch(V.scalar_tensor_tensor(low_s[0][:, :], back0[:, :, 0], -1.0, ps[:, 0, 0:NCH], ALU.add, ALU.add), wait=False)
            ch(V.scalar_tensor_tensor(idx_s[0][:, :], back0[:, :, 1], float(MID), ps[:, 1, 0:NCH], ALU.add, ALU.add), wait=False)
            ch(V.tensor_tensor(wgt_s[:, :], back0[:, :, 2], ps[:, 4, 0:NCH], ALU.add))
            ch(V.tensor_tensor(wgt_s[:, :], wgt_s[:, :], ps[:, 3, 0:NCH], ALU.add))
            V.tensor_tensor(wgt_s[:, :], wgt_s[:, :], ps[:, 2, 0:NCH], ALU.add).then_inc(sort_ready[0], 1)
            dve.wait_ge(sort_ready[0], 1)
            dve.wait_ge(xs_zeroed, 16)
            dve.wait_ge(sorted_zeroed, 32)
            V.memset(A[:, :], 0.0).then_inc(hop_start[0], 1)
            dve.wait_ge(hop_start[0], 1)

            def hop(h):
                e = 0 if h == 0 else 1
                oh = hop_oh[h]

                def onehot(q, g):
                    after(dve, hops_mm[h], q - 3)
                    if h == 0:
                        ins = V.tensor_scalar(oh[:, g % 4, :], iota_f[:, :], col(low_s[e], q), col(wgt_s, q), ALU.is_equal, ALU.mult)
                    else:
                        ins = V.tensor_scalar(oh[:, g % 4, :], iota_f[:, :], col(low_s[e], q), None, ALU.is_equal)
                    ins.then_inc(hops_oh[h], 1)

                def add(q, g, at):
                    dve.wait_ge(hops_mm[h], q + 1)
                    after(dve, hops_added[h], q)
                    a = A[:, bass.ds(at, C)]
                    V.tensor_tensor(a, a, ps[:, g % 4, 0:C], ALU.add).then_inc(hops_added[h], 1)

                def at_of(n):
                    return dve.value_load(goff[e][0:1, bass.ds(n, 1)] if not isinstance(n, int) else goff[e][0:1, n:n + 1],
                                          min_val=0, max_val=(NB - 1) * C)

                def turn(i, beside=()):
                    for g in range(GU):
                        q = GU * i + g
                        onehot(q, g)
                        if not (isinstance(i, int) and i == 0 and g < 2):
                            add(q - 2, (g - 2) % GU, at_of(q))
                        if g in beside:
                            beside[g](i)

                if h == 0:
                    turn(0, {1: second_clear, 9: second_words})
                    loop(RANK_AT, 5, lambda i: turn(i, {3 * n: second_count(n) for n in range(5)}), lo=1)
                    turn(RANK_AT, {0: second_counted, 8: second_ends})
                    loop(RANK_AT + 14, 8, lambda i: turn(i, {2: second_rank(0), 10: second_rank(1)}), lo=RANK_AT + 1)
                    turn(RANK_AT + 14, {2: second_places, 6: second_offsets})
                    with dve.Fori(RANK_AT + 15, HT) as i:
                        turn(i)
                else:
                    turns(dve, HT, turn)
                for q in (NCH - 2, NCH - 1):
                    add(q, q % GU, at_of(q + 2))
                dve.wait_ge(hops_added[h], NCH)

            def second_clear(i):
                V.memset(ta1.bitcast(I32), 0)
                V.memset(place1, PADKEY).then_inc(edges_cleared, 1)

            def second_words(i):
                dve.wait_ge(edges_loaded[1], 64)
                ch(V.tensor_copy(words1[:, :, 1], ta1.bitcast(I32)), wait=False)
                split_key(place1, words1[:, :, 0], key1, tb1.bitcast(I32), pos1.bitcast(I32))

            def second_count(n):
                def count(i):
                    b = 5 * i - 5 + n
                    ch(V.tensor_scalar(tb1, key1, iota_f[:, bass.ds(b, 1)], None, ALU.is_equal, ALU.add,
                                       accum_out=cnt[:, bass.ds(b, 1)]))
                return count

            def second_counted(i):
                V.memset(pos1, 0.0).then_inc(small_mm_in, 1)

            def second_ends(i):
                dve.wait_ge(small_mm_out, 3)
                padded_ends(NB, 7)

            def second_rank(n):
                def rank(i):
                    b = 2 * i - 2 * (RANK_AT + 1) + n
                    running(b, key1, iota_f[:, bass.ds(b, 1)], init[:, bass.ds(b, 1)], ta1, tb1, pos1)
                return rank

            def second_places(i):
                a_i, b_i = ta1.bitcast(I32), tb1.bitcast(I32)
                ch(V.tensor_scalar(a_i, pos1, -1.0, None, ALU.add))
                ch(V.tensor_scalar(b_i, a_i, P - 1, None, ALU.bitwise_and))
                ch(V.tensor_scalar(a_i, a_i, 7, None, ALU.arith_shift_right))
                ch(V.scalar_tensor_tensor(pos1, b_i, float(NCH), a_i, ALU.mult, ALU.add))
                ch(V.tensor_scalar(ta1, iota_h[:, 0:EC], float(SLOTS - (P - 1) * NCH + 1), None, ALU.add))
                ch(V.scalar_tensor_tensor(tb1, key1, float(NT), ta1, ALU.is_equal, ALU.mult))
                V.tensor_tensor(place1, pos1, tb1, ALU.add).then_inc(ranked[1], 1)

            def second_offsets(i):
                offsets(1, gs1, gc1, 32)

            hop(0)

            dve.wait_ge(kept_stored, 16)
            V.memset(x3[:, FULL:NT, :], 0.0).then_inc(x_reloaded, 1)
            dve.wait_ge(x_loaded, 64)
            ch(V.scalar_tensor_tensor(X[:, :], A[:, :], 0.0, X[:, :], ALU.max, ALU.add))

            def route_project(k, full):
                def turn(i):
                    for s in range(2):
                        q = 2 * i + s
                        after(dve, proj[k]["tr"], q - 1)
                        full(s, q, proj[k]["xn"])
                    if not (isinstance(i, int) and i == 0):
                        for s in range(2):
                            take(2 * i - 2 + s, s)

                def take(q, s):
                    if True:
                        dve.wait_ge(proj[k]["mm"], q + 1)
                        dstt = lg[:, bass.ds(q, 1), :].rearrange("p a e -> p (a e)") if not isinstance(q, int) else lg[:, q, :]
                        if k == 1:
                            V.tensor_copy(dstt, ps[:, 2 + s, 0:E8]).then_inc(proj[k]["ev"], 1)
                        else:
                            V.tensor_tensor(dstt, ps[:, 2 + s, 0:E8], br_s, ALU.add).then_inc(proj[k]["ev"], 1)
                if k == 1:
                    turns(dve, NI, turn)
                else:
                    loop(NI, 4, turn)
                for s in range(2):
                    take(NT - 2 + s, s)
                dve.wait_ge(proj[k]["ev"], NT)

            def bc(v):
                return v.rearrange("p (t a) -> p t a", a=1).to_broadcast([P, NT, E8])

            def masks(val, drop):
                ch(V.tensor_copy(wrev, iota_f[:, 0:E8]))
                ch(V.tensor_scalar(wrev, wrev, -1.0, float(E8), ALU.mult, ALU.add))
                wb = wrev.rearrange("p (a e) -> p a e", a=1).to_broadcast([P, NT, E8])
                for k in range(2):
                    ch(V.tensor_reduce(v1 if k == 0 else v2, val, AX.X, ALU.max))
                    ch(V.tensor_tensor(ta, val, bc(v1 if k == 0 else v2), ALU.is_equal))
                    ch(V.tensor_tensor(ta, ta, wb, ALU.mult))
                    ch(V.tensor_reduce(v3, ta, AX.X, ALU.max))
                    Mk = MS[:, :, k * NT:(k + 1) * NT].rearrange("p e t -> p t e")
                    ch(V.tensor_tensor(Mk, ta, bc(v3), ALU.is_equal))
                    if k == 0:
                        ch(V.tensor_scalar(ta, Mk, -drop, None, ALU.mult))
                        ch(V.tensor_tensor(val, val, ta, ALU.add))
                for k in range(2):
                    mk = MS[:, :, k * NT + FULL]
                    ch(V.tensor_scalar(v3[:, 0:1], pcol[:, :], float(REST), None, ALU.is_lt))
                    ch(V.tensor_scalar(mk, mk, v3[:, 0:1], None, ALU.mult))
                    ch(V.memset(MS[:, :, k * NT + NT - 1], 0.0))

            def places(m):
                V.tensor_reduce(cnt[:, 0:E8], MS, AX.X, ALU.add).then_inc(small_mm_in, 1)
                dve.wait_ge(small_mm_out, 4 + 2 * m)
                padded_ends(E8, 7)
                ch(V.memset(fpos, 0.0))
                for e in range(E8):
                    ch(V.tensor_tensor_scan(ft1, MS[:, e, :], MS[:, e, :], init[:, e:e + 1], ALU.add, ALU.max))
                    ch(V.tensor_tensor(ft1, ft1, MS[:, e, :], ALU.mult))
                    ch(V.tensor_tensor(fpos, fpos, ft1, ALU.add))
                ch(V.tensor_scalar(v3[:, 0:1], pcol[:, :], float(REST), None, ALU.is_ge))
                for k in range(2):
                    ch(V.tensor_scalar(v2[:, 0:1], pcol[:, :], float(TRASH + 1 + P * k), None, ALU.add))
                    ch(V.tensor_tensor(v2[:, 1:2], v2[:, 0:1], v3[:, 0:1], ALU.mult))
                    f = fpos[:, k * NT + FULL:k * NT + FULL + 1]
                    ch(V.tensor_tensor(f, f, v2[:, 1:2], ALU.add))
                    ch(V.tensor_scalar(fpos[:, k * NT + NT - 1:k * NT + NT], v2[:, 0:1], float(2 * P), None, ALU.add))
                ch(V.tensor_scalar(scat_i[:, :, :].rearrange("p k t -> p (k t)"), fpos, -1.0, None, ALU.add))
                ch(V.tensor_scalar(gath_i[:, :, :].rearrange("p k t -> p (k t)"), fpos, -1.0, float(TRASH - 1), ALU.add, ALU.min))
                ch(V.tensor_scalar(est, iota_f[0:1, 0:TT], float(P), None, ALU.mult))
                table(est, ecount, E8, 1, E8 - 1)
                V.tensor_copy(eoff[:, :], ecount).then_inc(routed, 1)
                dve.wait_ge(routed, m + 1)

            def dispatch(m, full):
                def turn(i):
                    for s in range(2):
                        q = 2 * i + s
                        after(dve, disp_done[m][s], i * 32)
                        full(s, q, disp_ready[m])
                if m == 0:
                    turns(dve, NI, turn)
                else:
                    loop(NI, 4, turn)

            def combine(m):
                def turn(i):
                    for s in range(2):
                        t = 2 * i + s
                        dve.wait_ge(y_gathered[m][s], i * 32 + 32)
                        ch(V.scalar_tensor_tensor(tile(x3, t), yg[:, s, 0, :], col(gate[:, 0, :], t), tile(x3, t), ALU.mult, ALU.add))
                        V.scalar_tensor_tensor(tile(x3, t), yg[:, s, 1, :], col(gate[:, 1, :], t), tile(x3, t), ALU.mult, ALU.add).then_inc(comb_used[m], 1)
                    if m == 0:
                        dve.wait_ge(comb_used[m], 2 * i + 2)
                        dve.nop(nofuse=True)
                        tile_stats(i)
                loop(NI, 7 if m == 0 else 2, turn)
                dve.wait_ge(comb_used[m], NT)

            def plain(s, q, done):
                normalise(q, xn[:, s, :], rstd).then_inc(done, 1)

            def affine(s, q, done):
                ch(normalise(q, xn[:, s, :], rstd))
                ch(V.tensor_tensor(xn[:, s, :], xn[:, s, :], gam, ALU.mult))
                V.tensor_tensor(xn[:, s, :], xn[:, s, :], bet, ALU.add).then_inc(done, 1)

            layernorm_stats(2)
            route_project(1, plain)
            ch(V.tensor_reduce(v1, lg, AX.X, ALU.max))
            V.tensor_tensor(tb, lg, bc(v1), ALU.subtract).then_inc(dve_to_act, 1)
            dve.wait_ge(act_to_dve, 3)
            ch(V.tensor_reduce(v1, ta, AX.X, ALU.add))
            ch(V.reciprocal(v1, v1))
            ch(V.tensor_tensor(pr, ta, bc(v1), ALU.mult))
            masks(pr, 2.0)
            ch(V.tensor_tensor(v3, v1, v2, ALU.add))
            ch(V.tensor_scalar(v3, v3, 1e-9, None, ALU.add))
            ch(V.reciprocal(v3, v3))
            ch(V.tensor_tensor(gate[:, 0, :], v1, v3, ALU.mult))
            ch(V.tensor_tensor(gate[:, 1, :], v2, v3, ALU.mult))
            places(0)
            dispatch(0, plain)

            def mixture(m):
                sm = ffn[m]

                def some(arr, lo, n):
                    part = arr[:, lo:lo + DU] if isinstance(lo, int) else arr[:, bass.ds(lo, DU)]
                    return part.rearrange("p (t a) -> p t a", a=1).to_broadcast([P, DU, n])

                def hidden(q):
                    if m == 0:
                        for part in range(2):
                            dve.wait_ge(sm["act"], q * 2 + (part + 1))
                            ins = V.tensor_tensor(hh[:, part * HALF:(part + 1) * HALF], sil[:, part * HALF:(part + 1) * HALF],
                                                  ps[:, 2 + part, 0:HALF], ALU.mult)
                        ins.then_inc(sm["hh"], 1)
                    else:
                        e = dve.value_load(eoff[0:1, bass.ds(q, 1)] if not isinstance(q, int) else eoff[0:1, q:q + 1], min_val=0, max_val=E8 - 1)
                        dve.wait_ge(sm["h"], q + 1)
                        V.tensor_tensor(sil[:, 0:H1], ps[:, 0, :], b1b[:, bass.ds(e * H1, H1)], ALU.add).then_inc(sm["bias"], 1)

                def result(q, s, i):
                    if m == 1:
                        e = dve.value_load(eoff[0:1, bass.ds(q, 1)] if not isinstance(q, int) else eoff[0:1, q:q + 1], min_val=0, max_val=E8 - 1)
                    dve.wait_ge(sm["y"], q + 1)
                    after(dve, ys_stored[m][s], i * 16)
                    if m == 0 and s == 0:
                        V.tensor_tensor(dinv2[:, :], dinv2[:, :], ps[:, 7, C:C + NT], ALU.add)
                    if m == 0:
                        V.tensor_copy(ys[:, s, :], ps[:, 7, 0:C]).then_inc(sm["ys"], 1)
                    else:
                        V.tensor_tensor(ys[:, s, :], ps[:, 7, 0:C], b2b[:, bass.ds(e * C, C)], ALU.add).then_inc(sm["ys"], 1)

                def turn(i):
                    if m == 0:
                        after(dve, sm["y"], 2 * i - 1)
                        V.tensor_tensor(low_oh, iota_h[:, 1:P + 1].rearrange("p (a n) -> p a n", a=1).to_broadcast([P, DU, P]),
                                        some(words1A[:, :, 0], i * DU, P), ALU.is_equal)
                        V.tensor_tensor(tile_oh, iota_h[:, 0:NT].rearrange("p (a n) -> p a n", a=1).to_broadcast([P, DU, NT]),
                                        some(key1A, i * DU, NT), ALU.is_equal).then_inc(counted_onehot, 1)
                    for s in range(2):
                        q = 2 * i + s
                        hidden(q)
                        if s == 1:
                            result(q - 1, 0, i)
                        elif not (isinstance(i, int) and i == 0):
                            result(q - 1, 1, i - 1)
                turns(dve, TT // 2, turn, peel=2)
                result(TT - 1, 1, TT // 2 - 1)

            ch(V.memset(dinv2[:, :], 1.0))
            dve.wait_ge(kept_loaded, 16)
            for s in range(2):
                dve.wait_ge(disp_done[0][s], 32 * NI)
            mixture(0)
            dve.wait_ge(placed_back[1], 16)
            ch(V.tensor_scalar(low_s[1][:, :], back1[:, :, 0], -1.0, None, ALU.add), wait=False)
            V.tensor_copy(idx_s[1][:, :], back1[:, :, 1]).then_inc(sort_ready[1], 1)
            ch(V.reciprocal(dinv2[:, :], dinv2[:, :]))
            combine(0)

            inverse_root(4)
            ch(V.tensor_tensor(cnt, rstd[:, :], dinv[:, :], ALU.mult))

            def scaled(i):
                for s in range(2):
                    t = 2 * i + s
                    ch(normalise(t, tile(a3, t), cnt), wait=False)
            loop(NI, 2, scaled)
            V.memset(v_signal, 0.0).then_inc(hop_start[1], 1)
            hop(1)

            def rescale(i):
                for s in range(2):
                    t = 2 * i + s
                    ch(V.tensor_scalar(tile(a3, t), tile(a3, t), col(dinv2, t), None, ALU.mult), wait=False)
            loop(NI, 2, rescale)
            V.memset(v_signal, 0.0).then_inc(hop_start[2], 1)
            hop(2)

            def logits(i):
                for s in range(2):
                    t = 2 * i + s
                    after(dve, proj[2]["tr"], t - 1)
                    V.tensor_scalar(xn[:, s, :], tile(a3, t), col(dinv, t), None, ALU.mult).then_inc(proj[2]["xn"], 1)
                if not (isinstance(i, int) and i == 0):
                    for s in range(2):
                        take_logits(2 * i - 2 + s, s)

            def take_logits(t, s):
                dve.wait_ge(proj[2]["mm"], t + 1)
                ch(V.tensor_tensor(tile(a3, t), ps[:, 2 + s, 0:C], bg, ALU.add))
                V.tensor_reduce(col(rstd, t), tile(a3, t), AX.X, ALU.max, negate=True).then_inc(proj[2]["ev"], 1)
            loop(NI, 2, logits)
            for s in range(2):
                take_logits(NT - 2 + s, s)
            V.memset(v_signal, 0.0).then_inc(dve_to_act, 1)
            dve.wait_ge(proj[2]["ev"], NT)
            dve.wait_ge(act_to_dve, 5)
            ch(V.tensor_tensor(rstd[:, :], rstd[:, :], dinv2[:, :], ALU.subtract))

            def add_logits(i):
                for s in range(2):
                    t = 2 * i + s
                    ch(V.scalar_tensor_tensor(tile(x3, t), tile(a3, t), col(rstd, t), tile(x3, t), ALU.add, ALU.add), wait=False)
            loop(NI, 2, add_logits)
            ch.sync()

            layernorm_stats(6)
            route_project(3, affine)
            masks(lg, BIG)
            V.tensor_tensor(v3, v2, v1, ALU.subtract).then_inc(dve_to_act, 1)
            dve.wait_ge(act_to_dve, 7)
            ch(V.tensor_scalar(v1, v3, 1.0, None, ALU.add))
            ch(V.reciprocal(gate[:, 0, :], v1))
            ch(V.tensor_tensor(gate[:, 1, :], v3, gate[:, 0, :], ALU.mult))
            places(1)
            dispatch(1, affine)
            mixture(1)
            combine(1)


_INS = ['x', 'src', 'dst', 'edge_weight', 'L0_gnn_weight', 'L0_ffn_router_w', 'L0_ffn_w1', 'L0_ffn_w2', 'L0_ffn_w3',
        'L1_gnn_W', 'L1_gnn_b', 'L1_ffn_gamma', 'L1_ffn_beta', 'L1_ffn_Wr', 'L1_ffn_br',
        'L1_ffn_W1', 'L1_ffn_b1', 'L1_ffn_W2', 'L1_ffn_b2']
_OUT = ((3125, 256), 'float32')


def kernel(**inputs):
    import numpy as _np
    import concourse.bacc as _bacc
    from concourse import mybir as _mybir
    from concourse.bass_utils import run_bass_kernel_spmd as _run

    nc = _bacc.Bacc("TRN2", target_bir_lowering=False, num_devices=1)
    arrays, args = {}, {}
    for name in _INS:
        a = _np.ascontiguousarray(inputs[name])
        arrays[f"in_{name}_dram"] = a
        args[name] = nc.dram_tensor(f"in_{name}_dram", a.shape, _mybir.dt.from_np(a.dtype), kind="ExternalInput").ap()
    out = nc.dram_tensor("out_dram", _OUT[0], _mybir.dt.from_np(_np.dtype(_OUT[1])), kind="ExternalOutput").ap()
    gnn_moe_program(nc, args['x'], args['src'], args['dst'], args['edge_weight'], args['L0_gnn_weight'],
                    args['L0_ffn_router_w'], args['L0_ffn_w1'], args['L0_ffn_w2'], args['L0_ffn_w3'],
                    args['L1_gnn_W'], args['L1_gnn_b'], args['L1_ffn_gamma'], args['L1_ffn_beta'],
                    args['L1_ffn_Wr'], args['L1_ffn_br'], args['L1_ffn_W1'], args['L1_ffn_b1'],
                    args['L1_ffn_W2'], args['L1_ffn_b2'], out)
    r = _run(nc, [arrays], core_ids=[0])
    return r.results[0]["out_dram"]
```

```python
import concourse.bass as bass
from concourse import mybir
from contextlib import ExitStack

FP32 = mybir.dt.float32
FP16 = mybir.dt.float16
BF16 = mybir.dt.bfloat16
I32 = mybir.dt.int32
ALU = mybir.AluOpType
ACT = mybir.ActivationFunctionType
AX = mybir.AxisListType

P = 128
NODES, C = 3125, 256
EDGES = 50000
NT = 26
FULL = NODES // P
REST = NODES - FULL * P
ROWS = NT * P
NB = FULL + 1
EC = 392
ELAST = EDGES - (P - 1) * EC
PADKEY = NT * P
NCH = 416
RANK_AT = 6
GU = 16
HT = NCH // GU
CP = 176
SLOTS = P * NCH
MID = 1600
SU = 4
DU = 14
E8 = 8
H0 = 682
H0C = 6
H0R = H0 - 5 * P
H1 = 512
TT = 56
TP = 4
FT = NT // TP
TR = NT - FT * TP
FIRST = 3
PRE = 4
GP = (EC // (TT // 2) - 2) // 2
EPS = 1e-5
BIG = 3.0e38
HALF = H0 // 2
CLAMPED = "table() limits the offsets to those of the last tile or expert before they are stored"


class Chain:

    def __init__(self, eng, sem):
        self.eng, self.sem, self.n, self.i, self.per, self.start = eng, sem, 0, None, 0, 0

    def __call__(self, ins, wait=True):
        ins.then_inc(self.sem, 1)
        self.n += 1
        if wait:
            self.sync()

    def at(self):
        if self.i is None:
            return self.n
        return self.i * self.per + (self.start + self.n)

    def sync(self, lag=0):
        self.eng.wait_ge(self.sem, self.at() - lag)

    def loop(self, count, per, body, lo=0):
        if lo == 0:
            body(0)
            lo = 1
        entry = self.n
        with self.eng.Fori(lo, count) as i:
            self.n, self.i, self.per, self.start = 0, i, per, entry - lo * per
            body(i)
            assert self.n == per, (self.n, per)
            self.i, self.n = None, entry + (count - lo) * per


def after(eng, sem, value):
    if isinstance(value, int) and value <= 0:
        return
    eng.wait_ge(sem, value)


def turns(eng, count, body, peel=1):
    for i in range(peel):
        body(i)
    with eng.Fori(peel, count) as i:
        body(i)


def gnn_moe_program(nc, x_in, src, dst, edge_weight, w_gnn0, router0, w1_0, w2_0, w3_0,
                    w_gnn1, b_gnn1, gamma, beta, wr1, br1, w1_1, b1_1, w2_1, b2_1, out):
    ctx = ExitStack()
    with ctx:
        def sb(name, shape, dt=FP32):
            return ctx.enter_context(nc.sbuf_tensor(name, shape, dt))

        def sem(name):
            return ctx.enter_context(nc.semaphore(name))

        def dram(name, shape):
            return nc.dram_tensor(name, shape, FP32, kind="Internal").ap()

        support_t = dram("support_t", (ROWS, C))
        u1_t = dram("u1_t", (ROWS, C))
        u2_t = dram("u2_t", (ROWS, C))
        xn_t = dram("xn_t", (ROWS, C))
        sorted_t = [dram("sorted0_t", (SLOTS, 3)), dram("sorted1_t", (SLOTS + NCH, 2))]
        kept_t = dram("kept_t", (P, 4 * EC))
        y_t = [dram("y0_t", (TT * P, C)), dram("y1_t", (TT * P, C))]
        tables = [support_t, u1_t, u2_t]

        X = sb("X", [P, NT * C])
        A = sb("A", [P, NT * C])
        W = sb("W", [P, 34112])
        S = sb("S", [P, 6 * C])
        iota_f = sb("iota_f", [P, P])
        ident = sb("ident", [P, P])
        below = sb("below", [P, P])
        ones = sb("ones", [P, P])
        iota_h = sb("iota_h", [P, NCH], FP16)
        pcol = sb("pcol", [P, 1])
        low_s = [sb("low0", [P, NCH]), sb("low1", [P, NCH])]
        idx_s = [sb("idx0", [P, NCH], I32), sb("idx1", [P, NCH], I32)]
        wgt_s = sb("wgt_s", [P, NCH])
        goff_sb = sb("goff_sb", [33, NCH + 2], I32)
        goff = [goff_sb[0:1, :], goff_sb[32:33, :]]
        dinv = sb("dinv", [P, NT])
        dinv2 = sb("dinv2", [P, NT])
        mv = sb("mv", [P, NT, 2])
        rstd = sb("rstd", [P, NT])
        stats = S[:, 0:NT // 2 * 6].rearrange("p (t n) -> p t n", n=6)
        small = sb("small", [P, 192])
        istage = sb("istage", [P, 32], I32)
        pstage = sb("pstage", [P, 2, 14])

        x3 = X[:, :].rearrange("p (t c) -> p t c", c=C)
        a3 = A[:, :].rearrange("p (t c) -> p t c", c=C)

        ps = ctx.enter_context(nc.psum_tensor("ps", [P, 8, 512], FP32))

        def slots(area, at):
            return area[:, at:at + TP * C].rearrange("p (s c) -> p s c", s=TP)
        ot = slots(S, 0)
        exp_out = slots(S, 0)

        def earr(k):
            return X[:, k * EC:(k + 1) * EC]

        key_f, low_f, oth_f, wh_f, wm_f, wl_f, lane_f, chunk_f, pos_f, t1_f, t2_f = [earr(k) for k in range(11)]
        key_i, oth_i, t1_i, t2_i = [earr(k).bitcast(I32) for k in range(11, 15)]
        w_f = earr(15)
        assert 16 * EC <= NT * C
        words0 = X[:, 11 * EC:11 * EC + 3 * CP].rearrange("p (t w) -> p t w", w=3)
        back0 = X[:, 0:3 * NCH].rearrange("p (t w) -> p t w", w=3)
        behind0 = X[0:NB, 6 * EC:6 * EC + NCH]
        K0 = GU * C + 4 * P
        kept = X[:, K0:K0 + 4 * EC]
        words1 = kept[:, 0:2 * EC].rearrange("p (t w) -> p t w", w=2)
        place1 = kept[:, 2 * EC:3 * EC].bitcast(I32)
        key1 = kept[:, 3 * EC:4 * EC]
        ta1, tb1, pos1 = [S[:, k * EC:(k + 1) * EC] for k in range(3)]
        behind1 = S[0:NB, 0:NCH]
        oc = A[:, 0:SU * NCH // 2].bitcast(BF16).rearrange("p (s n) -> p s n", s=SU)
        LO = SU * NCH // 2
        Lh = A[:, LO:LO + SU * 2 * 64].bitcast(FP16).rearrange("p (s k n) -> p s k n", s=SU, k=2)
        LB = LO + SU * 2 * 64
        Lb = A[:, LB:LB + SU * 4 * 64].bitcast(BF16).rearrange("p (s k n) -> p s k n", s=SU, k=4)
        low_oh = S[:, 0:DU * 64].bitcast(BF16).rearrange("p (s n) -> p s n", s=DU)
        tile_oh = S[:, DU * 64:DU * 64 + DU * NT // 2].bitcast(BF16).rearrange("p (s n) -> p s n", s=DU)
        ZW = NCH // 4
        zero = A[:, NT * C - ZW:NT * C]
        raw13 = A[:, 0:2 * 1536].rearrange("p (w j c) -> p w j c", w=2, j=H0C)
        raw2 = A[:, 3072:3072 + 2 * H0].rearrange("p (m h) -> p m h", m=2)

        W13N = 2 * 2 * H0
        W2N = H0C * C
        W13 = W[:, 0:E8 * W13N]
        W2 = W[:, E8 * W13N:E8 * (W13N + W2N)]
        wg0 = S[:, TP * C:TP * C + 2 * C].rearrange("p (k n) -> p k n", k=2)
        rwn = W[0:E8, E8 * (W13N + W2N) - C:E8 * (W13N + W2N)]
        rwT = sb("rwT", [P, 2, E8])
        x0 = W[:, E8 * (W13N + W2N) - C - NT * C:E8 * (W13N + W2N) - C].rearrange("p (t c) -> p t c", c=C)
        assert NT * C + C <= (E8 - FIRST) * W2N
        o = 0

        def wslice(n):
            nonlocal o
            o += n
            return W[:, o - n:o]

        W1b = wslice(E8 * 2 * H1)
        W2b = wslice(E8 * 4 * C)
        b1b = wslice(E8 * H1)
        b2b = wslice(E8 * C)
        wgT = wslice(2 * C).rearrange("p (k n) -> p k n", k=2)
        wgn = wslice(2 * C).rearrange("p (k n) -> p k n", k=2)
        bg = wslice(C)
        gamT = wslice(2)
        betT = wslice(2)
        wr_s = wslice(2 * E8).rearrange("p (k n) -> p k n", k=2)
        br_s = wslice(E8)
        rows1 = wslice(GU * C)
        oh1 = wslice(4 * P)
        rows0 = X[:, 0:GU * C]
        oh0 = X[:, GU * C:GU * C + 4 * P]
        hop_rows = [r.rearrange("p (g c) -> p g c", g=GU) for r in (rows0, rows1, rows1)]
        hop_oh = [r.rearrange("p (g c) -> p g c", g=4) for r in (oh0, oh1, oh1)]

        PA = 3072 + 2 * H0
        xn = [slots(A, PA), slots(A, 0), slots(rows1, 0), slots(A, 0)]
        xT = [slots(A, PA + TP * C), slots(A, TP * C), slots(rows1, TP * C), slots(A, TP * C)]
        inv_lane = [A[:, k * NB * 64:(k + 1) * NB * 64].bitcast(FP16).rearrange("p (t n) -> p t n", t=NB) for k in range(2)]
        INV = P
        inv_tile = [S[:, INV + k * NB * TT // 2:INV + (k + 1) * NB * TT // 2].bitcast(FP16).rearrange("p (t n) -> p t n", t=NB)
                    for k in range(2)]

        xs = A[:, 0:2 * C].rearrange("p (s c) -> p s c", s=2)
        fT = A[:, 512:512 + C]
        sil = A[:, 768:768 + H0]
        hh = A[:, 1450:1450 + H0]
        hT = A[:, 2132:2132 + H0C * P]
        ys = A[:, 2900:2900 + 2 * C].rearrange("p (s c) -> p s c", s=2)
        yg = A[:, 0:2 * TP * C].rearrange("p (s k c) -> p s k c", s=TP, k=2)
        keptA = A[:, 3412:3412 + 4 * EC]
        words1A = keptA[:, 0:2 * EC].rearrange("p (t w) -> p t w", w=2)
        place1A = keptA[:, 2 * EC:3 * EC].bitcast(I32)
        key1A = keptA[:, 3 * EC:4 * EC]
        back1 = A[:, 5000:5000 + 2 * NCH].rearrange("p (t w) -> p t w", w=2)
        R = 5100
        lg = A[:, R:R + NT * E8].rearrange("p (t e) -> p t e", e=E8)
        pr = A[:, R + 208:R + 416].rearrange("p (t e) -> p t e", e=E8)
        ta = A[:, R + 416:R + 624].rearrange("p (t e) -> p t e", e=E8)
        tb = A[:, R + 624:R + 832].rearrange("p (t e) -> p t e", e=E8)
        MS = A[:, R + 832:R + 832 + 2 * NT * E8].rearrange("p (e c) -> p e c", e=E8)
        v1 = A[:, R + 1248:R + 1248 + NT]
        v2 = A[:, R + 1274:R + 1274 + NT]
        v3 = A[:, R + 1300:R + 1300 + NT]
        fpos = A[:, R + 1326:R + 1326 + 2 * NT]
        ft1 = A[:, R + 1378:R + 1378 + 2 * NT]
        ft2 = A[:, R + 1430:R + 1430 + 2 * NT]
        run = A[:, TP * C:TP * C + 2 * NT * E8]
        wrev = A[:, R + 1482:R + 1490]
        token = A[:, R + 1490:R + 1490 + NT]
        gate = sb("gate", [P, 2, NT])
        gath_i = sb("gath_i", [P, 2, NT], I32)
        token_of = sb("token_of", [P, TT], I32)
        eoff = sb("eoff", [1, TT], I32)
        cnt = small[:, 0:26]
        incl = small[:, 32:58]
        padn = small[:, 64:90]
        init = small[:, 96:122]
        i1 = small[:, 128:154].bitcast(I32)
        i2 = small[:, 160:186].bitcast(I32)
        est = S[0:1, 0:TT]
        ecount = S[0:1, TT:2 * TT]

        const_ready = sem("const_ready")
        dve_step = sem("dve_step")
        act_step = sem("act_step")
        pool_step = sem("pool_step")
        x_half_loaded = [sem(f"x_half{h}_loaded") for h in range(2)]
        wg0_loaded = sem("wg0_loaded")
        edges_loaded = [sem("edges0_loaded"), sem("edges1_loaded")]
        sorted_zeroed = sem("sorted_zeroed")
        ranked = [sem("ranked0"), sem("ranked1")]
        placed = [[sem(f"placed{k}_{h}") for h in range(2)] for k in range(2)]
        placed_back = [sem("placed0_back"), sem("placed1_back")]
        kept_stored = sem("kept_stored")
        relu_added = sem("relu_added")
        xn_stored = [[sem(f"xn{m}_stored{h}") for h in range(2)] for m in range(2)]
        token_onehots = sem("token_onehots")
        token_mm = sem("token_mm")
        token_ready = sem("token_ready")
        kept_loaded = sem("kept_loaded")
        counted_onehot = sem("counted_onehot")
        edges_cleared = sem("edges_cleared")
        raw_loaded = [sem(f"raw_w{k}_loaded") for k in (1, 3, 2)]
        raw_transposed = sem("raw_transposed")
        raw_copied = sem("raw_copied")
        gnn1_loaded = sem("gnn1_loaded")
        ffn1_loaded = sem("ffn1_loaded")
        small_mm_in = sem("small_mm_in")
        small_mm_out = sem("small_mm_out")
        x_reloaded = sem("x_reloaded")
        hops_added = [sem(f"hop{h}_added") for h in range(3)]
        hops_mm = [sem(f"hop{h}_mm") for h in range(3)]
        hops_oh = [sem(f"hop{h}_onehot") for h in range(3)]
        row_gathered = [sem(f"row_gathered{g}") for g in range(GU)]
        hop_table = [sem(f"hop{h}_table") for h in range(3)]
        hop_staged = [sem(f"hop{h}_staged") for h in range(3)]
        hop_start = [sem(f"hop{h}_start") for h in range(3)]
        sort_onehot = sem("sort_onehot")
        sort_onehot_plain = sem("sort_onehot_plain")
        sort_weighted = sem("sort_weighted")
        sort_mm = sem("sort_mm")
        sort_ready = [sem(f"sort{k}_ready") for k in range(2)]
        proj = [{n: sem(f"proj{k}_{n}") for n in ("xn", "tr", "xt", "mm", "ev")} for k in range(4)]
        support_out = [sem(f"support_out{s}") for s in range(2)]
        routed = sem("routed")
        wgT_ready = sem("wgT_ready")
        dve_to_act = sem("dve_to_act")
        act_to_dve = sem("act_to_dve")
        log_sum_ready = sem("log_sum_ready")
        ffn = [{n: sem(f"ffn{m}_{n}") for n in ("tx", "fT", "h", "act", "hh", "th", "hT", "y", "ys", "bias")} for m in range(2)]
        xs_loaded = [[sem(f"xs{m}_loaded{s}") for s in range(2)] for m in range(2)]
        ys_stored = [[sem(f"ys{m}_stored{s}") for s in range(2)] for m in range(2)]
        y_gathered = [[sem(f"y{m}_gathered{s}") for s in range(TP)] for m in range(2)]
        comb_used = [sem(f"comb{m}_used") for m in range(2)]
        out_done = sem("out_done")

        block = ctx.enter_context(nc.Block())
        NI = NT // 2

        def tile(ap3, t):
            if isinstance(t, int):
                return ap3[:, t, :]
            return ap3[:, bass.ds(t, 1), :].rearrange("p a c -> p (a c)")

        def col(ap2, t):
            return ap2[:, bass.ds(t, 1)] if not isinstance(t, int) else ap2[:, t:t + 1]

        def stores_of(h):
            return 16 * (FT + (1 if h < TR // 2 else 0))

        ON_DVE, ON_PE = (mybir.EngineType.DVE,), (mybir.EngineType.PE,)

        def in_registers(engine, row, lo, n, most):
            part = row[0:1, lo:lo + n] if isinstance(lo, int) else row[0:1, bass.ds(lo, n)]
            _, regs = nc.values_load_multi_w_load_instructions(part, engines=engine, min_val=0, max_val=most,
                                                              skip_runtime_bounds_check_because=CLAMPED)
            return regs

        def load_edges(eng, arr, vec, done):
            eng.dma_start(arr[0:P - 1, :], vec[0:(P - 1) * EC].rearrange("(p t) -> p t", t=EC)).then_inc(done, 16)
            eng.dma_start(arr[P - 1:P, 0:ELAST], vec[(P - 1) * EC:EDGES].rearrange("(p t) -> p t", p=1)).then_inc(done, 16)

        @block.sync
        def _(sp):
            def load_x(to):
                sp.dma_start(to[:, 0:NI, :], x_in[0:NI * P, :].rearrange("(t p) c -> p t c", p=P)).then_inc(x_half_loaded[0], 16)
                sp.dma_start(to[:, NI:FULL, :], x_in[NI * P:FULL * P, :].rearrange("(t p) c -> p t c", p=P)).then_inc(x_half_loaded[1], 16)
                sp.dma_start(to[0:REST, FULL, :], x_in[FULL * P:NODES, :]).then_inc(x_half_loaded[1], 16)

            sp.wait_ge(const_ready, 1)
            sp.wait_ge(edges_loaded[0], 96)
            load_x(x0)
            sp.dma_start(wg0, w_gnn0.rearrange("(k p) n -> p k n", p=P)).then_inc(wg0_loaded, 16)
            sp.dma_start(rwn, router0).then_inc(wg0_loaded, 16)
            sp.wait_ge(const_ready, 2)
            for k in range(2):
                w = 3 - k
                sp.dma_start(sorted_t[k][0:SLOTS, :].rearrange("(p n) w -> p (n w)", p=P).rearrange("p (n m) -> p n m", m=ZW),
                             zero.rearrange("p (a m) -> p a m", a=1).to_broadcast([P, 4 * w, ZW])
                             ).then_inc(sorted_zeroed, 16)
            def store_tiles(table, from_slots, ready, done):
                rows = table.rearrange("(t p) c -> p t c", p=P)

                def turn(i, halves=2):
                    for h in range(halves):
                        q = TP * i + 2 * h
                        sp.wait_ge(ready, q + 2)
                        sp.nop(nofuse=True)
                        sp.dma_start(rows[:, q:q + 2, :] if isinstance(q, int) else rows[:, bass.ds(q, 2), :],
                                     from_slots[:, 2 * h:2 * h + 2, :]).then_inc(done[h], 16)
                turns(sp, FT, turn)
                turn(FT, TR // 2)
            store_tiles(support_t, ot, proj[0]["ev"], support_out)

            for h in range(2):
                sp.wait_ge(placed[0][h], 64 * (CP // 8))
            sp.wait_ge(sort_mm, EC - CP)
            sp.dma_start(back0, sorted_t[0].rearrange("(p n) w -> p n w", p=P)).then_inc(placed_back[0], 16)
            sp.wait_ge(edges_cleared, 2)
            load_edges(sp, place1, dst, edges_loaded[1])
            load_edges(sp, ta1.bitcast(I32), src, edges_loaded[1])
            sp.wait_ge(ranked[1], 1)
            sp.dma_start(kept_t, kept).then_inc(kept_stored, 16)
            sp.wait_ge(kept_stored, 16)

            sp.wait_ge(hops_added[0], NCH)
            sp.wait_ge(x_reloaded, 1)
            load_x(x3)

            sp.wait_ge(relu_added, 2)
            sp.dma_start(keptA, kept_t).then_inc(kept_loaded, 16)

            def mixture(m):
                yr = y_t[m].rearrange("(t p) c -> t p c", p=P)

                def store(q, s):
                    sp.wait_ge(ffn[m]["ys"], q + 1)
                    sp.nop(nofuse=True)
                    row = yr[q, :, :] if isinstance(q, int) else yr[bass.ds(q, 1), :, :].rearrange("t p c -> (t p) c")
                    sp.dma_start(row, ys[:, s, :]).then_inc(ys_stored[m][s], 16)

                with sp.Fori(0, TT // 2) as i:
                    for s in range(2):
                        store(2 * i + s, s)

            store_tiles(xn_t, xn[1], proj[1]["xn"], xn_stored[0])
            mixture(0)
            for h in range(2):
                sp.wait_ge(placed[1][h], 64 * (EC // 8))
            sp.dma_start(back1, sorted_t[1][0:SLOTS, :].rearrange("(p n) w -> p n w", p=P)).then_inc(placed_back[1], 16)
            sp.wait_ge(ffn[0]["y"], TT)
            sp.dma_start(wgn, w_gnn1.rearrange("(m p) c -> p m c", p=P)).then_inc(gnn1_loaded, 16)
            sp.dma_start(bg, b_gnn1.rearrange("(a n) -> a n", a=1).to_broadcast([P, C])).then_inc(gnn1_loaded, 16)
            for k in range(2):
                sp.dma_start(gamT[:, k:k + 1], gamma[k * P:(k + 1) * P].rearrange("(p a) -> p a", a=1)).then_inc(gnn1_loaded, 16)
                sp.dma_start(betT[:, k:k + 1], beta[k * P:(k + 1) * P].rearrange("(p a) -> p a", a=1)).then_inc(gnn1_loaded, 16)
            sp.dma_start(wr_s, wr1.rearrange("(k p) e -> p k e", p=P)).then_inc(gnn1_loaded, 16)
            sp.dma_start(br_s, br1.rearrange("(a n) -> a n", a=1).to_broadcast([P, E8])).then_inc(gnn1_loaded, 16)
            for h in (1, 2):
                for half in range(2):
                    sp.wait_ge(hop_start[h], half + 1)
                    sp.dma_start(tables[h].rearrange("(t p) c -> p t c", p=P)[:, half * NI:(half + 1) * NI, :],
                                 a3[:, half * NI:(half + 1) * NI, :]).then_inc(hop_table[h], 16)
                if h == 1:
                    W1v = W1b.rearrange("p (e k n) -> p e k n", e=E8, k=2)
                    W2v = W2b.rearrange("p (e k n) -> p e k n", e=E8, k=4)
                    for e in range(E8):
                        sp.wait_ge(hops_mm[1], (e + 1) * (NCH // (E8 + 2)))
                        sp.dma_start(W1v[:, e], w1_1[e].rearrange("(k p) n -> p k n", p=P)).then_inc(ffn1_loaded, 16)
                        sp.dma_start(W2v[:, e], w2_1[e].rearrange("(k p) n -> p k n", p=P)).then_inc(ffn1_loaded, 16)
                    sp.dma_start(b1b, b1_1.rearrange("(a e) n -> a (e n)", a=1).to_broadcast([P, E8 * H1])).then_inc(ffn1_loaded, 16)
                    sp.dma_start(b2b, b2_1.rearrange("(a e) n -> a (e n)", a=1).to_broadcast([P, E8 * C])).then_inc(ffn1_loaded, 16)
            store_tiles(xn_t, xn[3], proj[3]["xn"], xn_stored[1])
            mixture(1)
            assert FT * TP == FULL
            for i in range(FT):
                sp.wait_ge(comb_used[1], TP * (i + 1))
                sp.dma_start(out[TP * i * P:TP * (i + 1) * P, :].rearrange("(t p) c -> p t c", p=P),
                             x3[:, TP * i:TP * (i + 1), :]).then_inc(out_done, 16)
            sp.wait_ge(comb_used[1], NT)
            sp.dma_start(out[FULL * P:NODES, :], x3[0:REST, FULL, :]).then_inc(out_done, 16)
            sp.wait_ge(out_done, 16 * (FT + 1))
            sp.wait_ge(sorted_zeroed, 32)
            for s in range(2):
                sp.wait_ge(support_out[s], stores_of(s))
                for m in range(2):
                    sp.wait_ge(ys_stored[m][s], 16 * TT // 2)
                    sp.wait_ge(xn_stored[m][s], stores_of(s))
            for h in (1, 2):
                sp.wait_ge(hop_table[h], 32)

        @block.gpsimd
        def _(pool):
            pool.iota(iota_f[:, :], [[1, P]], base=0, channel_multiplier=0, allow_small_or_imprecise_dtypes=True).then_inc(pool_step, 1)
            pool.iota(iota_h[:, :], [[1, NCH]], base=0, channel_multiplier=0, allow_small_or_imprecise_dtypes=True).then_inc(pool_step, 1)
            pool.iota(pcol[:, :], [[0, 1]], base=0, channel_multiplier=1, allow_small_or_imprecise_dtypes=True).then_inc(pool_step, 1)
            pch = Chain(pool, pool_step)
            pch.n = 3

            def stage(*pairs):
                for dst_ap, src_ap in pairs:
                    pch(pool.tensor_copy(dst_ap, src_ap), wait=False)
                pch.sync()
                pool.nop(nofuse=True)

            def at(ap, lo, n):
                return ap[:, lo:lo + n] if isinstance(lo, int) else ap[:, bass.ds(lo, n)]

            def hop(h):
                rows = hop_rows[h]

                def turn(i):
                    for half in range(2):
                        pool.wait_ge(hop_staged[h], 2 * i + (half + 1))
                        pool.nop(nofuse=True)
                        st = istage[:, 8 * half:8 * half + 8]
                        for g in range(8):
                            pool.indirect_dma_start(rows[:, 8 * half + g, :], None, tables[h],
                                                    bass.IndirectOffsetOnAxis(ap=st[:, g:g + 1], axis=0)
                                                    ).then_inc(row_gathered[8 * half + g], 16)
                turns(pool, HT, turn)

            def place(k, places, words, count, n):
                def turn(i):
                    for half in range(2):
                        place_group(k, places, words, i * 2 * n + n * half, half, n, i * (16 * n))
                pch.loop(count, 4, turn)

            def place_group(k, places, words, c0, half, n, done_before):
                w = 3 - k
                after(pool, placed[k][half], done_before)
                st = istage[:, 8 * half:8 * half + n]
                pst = pstage[:, half, 0:n * w].rearrange("p (t w) -> p t w", w=w)
                stage((st, at(places, c0, n)), (pst, words[:, c0:c0 + n, :] if isinstance(c0, int) else words[:, bass.ds(c0, n), :]))
                for g in range(n):
                    pool.indirect_dma_start(sorted_t[k], bass.IndirectOffsetOnAxis(ap=st[:, g:g + 1], axis=0),
                                            pst[:, g, :], None).then_inc(placed[k][half], 16)

            def mixture_rows(m):
                pool.wait_ge(token_ready, m + 1)
                for h in range(2):
                    pool.wait_ge(xn_stored[m][h], stores_of(h))

                def turn(i):
                    st = istage[:, 16:18]
                    for s in range(2):
                        after(pool, xs_loaded[m][s], i * 16)
                    stage((st, at(token_of, 2 * i, 2)))
                    for s in range(2):
                        if not (isinstance(i, int) and i == 0):
                            pool.wait_ge(ffn[m]["tx"], 2 * i + (s - 1))
                            pool.nop(nofuse=True)
                        pool.indirect_dma_start(xs[:, s, :], None, xn_t,
                                                bass.IndirectOffsetOnAxis(ap=st[:, s:s + 1], axis=0)
                                                ).then_inc(xs_loaded[m][s], 16)
                        if m == 0:
                            place_group(1, place1A, words1A, i * 2 * GP + (PRE * 2 * (GP + 1) + GP * s), s, GP,
                                        i * (16 * GP) + 16 * PRE * (GP + 1))
                pch.loop(TT // 2, 5 if m == 0 else 1, turn)

            def mixture_gather(m):
                for s in range(2):
                    pool.wait_ge(ys_stored[m][s], 16 * TT // 2)

                def turn(i, halves=2):
                    for h in range(halves):
                        t = TP * i + 2 * h
                        after(pool, comb_used[m], t - 2)
                        st = istage[:, 20 + 4 * h:24 + 4 * h].rearrange("p (k s) -> p k s", k=2)
                        stage((st, gath_i[:, :, t:t + 2] if isinstance(t, int) else gath_i[:, :, bass.ds(t, 2)]))
                        for s in range(2):
                            for k in range(2):
                                pool.indirect_dma_start(yg[:, 2 * h + s, k, :], None, y_t[m],
                                                        bass.IndirectOffsetOnAxis(ap=st[:, k, s:s + 1], axis=0)
                                                        ).then_inc(y_gathered[m][2 * h + s], 16)
                pch.loop(FT, 2, turn)
                turn(FT, TR // 2)

            pool.wait_ge(edges_cleared, 1)
            load_edges(pool, key_i, src, edges_loaded[0])
            load_edges(pool, oth_i, dst, edges_loaded[0])
            load_edges(pool, w_f, edge_weight, edges_loaded[0])
            pool.wait_ge(sorted_zeroed, 32)
            pool.wait_ge(ranked[0], 1)
            place(0, t2_i, words0, CP // 8, 4)
            for s in range(2):
                pool.wait_ge(support_out[s], stores_of(s))
            pool.wait_ge(sort_ready[0], 1)
            hop(0)
            pool.wait_ge(kept_loaded, 16)
            place(1, place1A, words1A, PRE, GP + 1)
            mixture_rows(0)
            mixture_gather(0)
            pool.wait_ge(sort_ready[1], 1)
            pool.wait_ge(hop_table[1], 32)
            hop(1)
            pool.wait_ge(hop_table[2], 32)
            hop(2)
            mixture_rows(1)
            mixture_gather(1)

        @block.tensor
        def _(pe):
            def project(k, rhs, n):
                sm = proj[k]

                def product(q, s):
                    pe.wait_ge(sm["xt"], q + 1)
                    after(pe, sm["ev"], q - (TP - 1))
                    for b in range(2):
                        last = nc.tensor.matmul(ps[:, TP + s, 0:n], xT[k][:, s, b * P:(b + 1) * P], rhs[:, b, :],
                                                start=(b == 0), stop=(b == 1))
                    last.then_inc(sm["mm"], 1)

                def turn(i, tiles=TP):
                    for s in range(tiles):
                        q = TP * i + s
                        pe.wait_ge(sm["xn"], q + 1)
                        after(pe, sm["xt"], q - (TP - 1))
                        for b in range(2):
                            last = nc.tensor.transpose(ps[:, s, b * P:(b + 1) * P], xn[k][:, s, b * P:(b + 1) * P], ident[:, :])
                        last.then_inc(sm["tr"], 1)
                    if not (isinstance(i, int) and i == 0):
                        for s in range(TP):
                            product(TP * (i - 1) + s, s)
                turns(pe, FT, turn, peel=2)
                turn(FT, TR)
                for s in range(TR):
                    product(TP * FT + s, s)

            def prefix(k, n):
                pe.wait_ge(small_mm_in, k)
                nc.tensor.matmul(ps[:, 7, 0:n], below[:, :], cnt[:, 0:n], start=True, stop=True)
                nc.tensor.matmul(ps[:, 7, 32:32 + n], ones[:, :], cnt[:, 0:n], start=True, stop=True).then_inc(small_mm_out, 1)

            def buckets_behind(k, below_t):
                pe.wait_ge(small_mm_in, k)
                nc.tensor.matmul(ps[0:33, 7, 64:64 + NCH], ones[0:NB, 0:33], below_t, start=True, stop=True).then_inc(small_mm_out, 1)

            def invert(m):
                for k in range(2):
                    pe.wait_ge(token_onehots, 2 * m + k + 1)
                    for t in range(NB):
                        last = nc.tensor.matmul(ps[:, 6, 0:TT], inv_lane[k][:, t, :], inv_tile[k][:, t, :],
                                                start=(k == 0 and t == 0), stop=(k == 1 and t == NB - 1), skip_group_check=True)
                    last.then_inc(token_mm, 1)

            def prep(e):
                for w in range(2):
                    pe.wait_ge(raw_loaded[w], e * 32 + 32)
                    for b in range(2):
                        after(pe, raw_copied, e * 12 + 2 * b + (2 if w else -6))
                        for j in range(H0C):
                            n = P if j < 5 else H0R
                            last = nc.tensor.transpose(ps[:, 2 * b + j // 4, (j % 4) * P:(j % 4) * P + n],
                                                       raw13[0:n, w, j, b * P:(b + 1) * P], ident[0:n, 0:n])
                            if j == 3 or j == 5:
                                last.then_inc(raw_transposed, 1)
                pe.wait_ge(raw_loaded[2], e * 16 + 16)
                after(pe, raw_copied, e * 12)
                for j in range(H0C):
                    n = P if j < 5 else H0R
                    for mb in range(2):
                        last = nc.tensor.transpose(ps[0:n, 4 + j // 2, j % 2 * C + mb * P:j % 2 * C + (mb + 1) * P],
                                                   raw2[:, mb, j * P:j * P + n], ident[:, :])
                    if j % 2:
                        last.then_inc(raw_transposed, 1)
            pe.wait_ge(const_ready, 4)
            for e in range(FIRST):
                prep(e)
                if e == 0:
                    prefix(1, NB)
                    buckets_behind(2, behind0)
            pe.wait_ge(wg0_loaded, 32)
            pe.wait_ge(raw_copied, 12 * FIRST)
            project(0, wg0, C)
            pe.wait_ge(proj[0]["ev"], NT)
            for b in range(2):
                last = nc.tensor.transpose(ps[:, 4, b * E8:(b + 1) * E8], rwn[:, b * P:(b + 1) * P], ident[0:E8, 0:E8])
            last.then_inc(small_mm_out, 1)
            pe.wait_ge(act_step, 1)
            with pe.Fori(FIRST, E8) as e:
                prep(e)

            def sort_columns(i):
                for s in range(SU):
                    q = SU * i + s
                    pe.wait_ge(sort_onehot, q + 1)
                    pe.wait_ge(sort_weighted, q + 1)
                    start = isinstance(i, int) and s == 0
                    for j in range(5):
                        piece = Lh[:, s, j, :] if j < 2 else Lb[:, s, j - 1, :]
                        last = nc.tensor.matmul(ps[:, j, 0:NCH], piece, oc[:, s, :],
                                                start=start, stop=not start, skip_group_check=True)
                    last.then_inc(sort_mm, 1)

            def hop(h):
                rows, oh = hop_rows[h], hop_oh[h]

                def turn(i):
                    for g in range(GU):
                        q = GU * i + g
                        pe.wait_ge(row_gathered[g], i * 16 + (16 * HT * h + 16))
                        pe.wait_ge(hops_oh[h], q + 1)
                        after(pe, hops_added[h], q - 3)
                        nc.tensor.matmul(ps[:, g % 4, 0:C], oh[:, g % 4, :], rows[:, g, :],
                                         start=True, stop=True).then_inc(hops_mm[h], 1)
                if h == 0:
                    turns(pe, RANK_AT, turn)
                    prefix(3, NB)
                    turn(RANK_AT)
                    buckets_behind(4, behind1)
                    with pe.Fori(RANK_AT + 1, HT) as i:
                        turn(i)
                else:
                    turns(pe, HT, turn)

            def mixture(m):
                sm = ffn[m]
                nj = H0C if m == 0 else 4

                def rows_of(j):
                    return H0R if (m == 0 and j == 5) else P

                def turn_x(q, s, i):
                    pe.wait_ge(xs_loaded[m][s], i * 16 + 16)
                    for b in range(2):
                        last = nc.tensor.transpose(ps[:, 6, b * P:(b + 1) * P], xs[:, s, b * P:(b + 1) * P], ident[:, :])
                    last.then_inc(sm["tx"], 1)

                def turn_h(q):
                    pe.wait_ge(sm["hh"], q + 1)
                    for j in range(nj):
                        n = rows_of(j)
                        last = nc.tensor.transpose(ps[0:n, 4 + j // 4, (j % 4) * P:(j % 4 + 1) * P], hh[:, j * P:j * P + n], ident[:, :])
                    last.then_inc(sm["th"], 1)

                def up(q, e):
                    pe.wait_ge(sm["fT"], q + 1)
                    if m == 0:
                        for part in range(4):
                            for b in range(2):
                                at = b * 2 * H0 + part * HALF
                                last = nc.tensor.matmul(ps[:, part, 0:HALF], fT[:, b * P:(b + 1) * P],
                                                        W13[:, bass.ds(e * W13N + at, HALF)], start=(b == 0), stop=(b == 1))
                        last.then_inc(sm["h"], 1)
                    else:
                        for b in range(2):
                            last = nc.tensor.matmul(ps[:, 0, :], fT[:, b * P:(b + 1) * P],
                                                    W1b[:, bass.ds(e * (2 * H1) + b * H1, H1)], start=(b == 0), stop=(b == 1))
                        last.then_inc(sm["h"], 1)

                def down(q, e, count=None):
                    pe.wait_ge(sm["hT"], q + 1)
                    after(pe, sm["ys"], q)
                    w, n_w = (W2, W2N) if m == 0 else (W2b, 4 * C)
                    if count is not None:
                        pe.wait_ge(counted_onehot, count + 1)
                        for j in range(DU):
                            nc.tensor.matmul(ps[:, 7, C:C + NT], low_oh[:, j, :], tile_oh[:, j, :],
                                             start=(j == 0), stop=(j == DU - 1))
                    for j in range(nj):
                        n = rows_of(j)
                        last = nc.tensor.matmul(ps[:, 7, 0:C], hT[0:n, j * P:(j + 1) * P],
                                                w[0:n, bass.ds(e * n_w + j * C, C)], start=(j == 0), stop=(j == nj - 1))
                    last.then_inc(sm["y"], 1)

                def expert(q):
                    return in_registers(ON_PE, eoff, q, 1, E8 - 1)[0]

                def turn(i, last=False):
                    for s in range(2):
                        q = 2 * i + s
                        first = isinstance(i, int) and i == 0 and s == 0
                        if not first:
                            turn_h(q - 1)
                        up(q, expert(q))
                        if not (last and s == 1):
                            turn_x(q + 1, 1 - s, i + s)
                        if not first:
                            down(q - 1, expert(q - 1), i if m == 0 and s == 1 else None)
                turn_x(0, 0, 0)
                turns(pe, TT // 2 - 1, turn)
                turn(TT // 2 - 1, last=True)
                turn_h(TT - 1)
                down(TT - 1, expert(TT - 1))

            pe.wait_ge(raw_copied, 12 * E8)
            turns(pe, (EC - CP) // SU, sort_columns)
            hop(0)
            pe.wait_ge(act_step, 1)
            project(1, rwT, E8)
            prefix(5, E8)
            invert(0)
            pe.wait_ge(routed, 1)
            mixture(0)
            pe.wait_ge(gnn1_loaded, 16 * 8)
            for b in range(2):
                for mb in range(2):
                    last = nc.tensor.transpose(ps[:, b, mb * P:(mb + 1) * P], wgn[:, mb, b * P:(b + 1) * P], ident[:, :])
            last.then_inc(small_mm_out, 1)
            hop(1)
            hop(2)
            pe.wait_ge(wgT_ready, 1)
            project(2, wgT, C)
            project(3, wr_s, E8)
            prefix(6, E8)
            invert(1)
            pe.wait_ge(routed, 2)
            pe.wait_ge(ffn1_loaded, 16 * (2 * E8 + 2))
            mixture(1)

        @block.scalar
        def _(act):
            AF = nc.scalar.activation

            def evacuation(q, s, n):
                act.wait_ge(proj[0]["mm"], q + 1)
                after(act, support_out[s // 2], n * 16)
                AF(ot[:, s, :], ps[:, TP + s, 0:C], ACT.Copy).then_inc(proj[0]["ev"], 1)

            def exps(q, s, n):
                act.wait_ge(proj[2]["ev"], q + 1)
                after(act, act_step, q - (TP - 2))
                AF(exp_out[:, s, :], tile(a3, q), ACT.Exp, bias=col(rstd, q), accum_out=col(dinv2, q)).then_inc(act_step, 1)

            def project(k, evacuate=None):
                late = 2 if k == 2 else 1
                sm = proj[k]

                def turn(i, tiles=TP):
                    for s in range(tiles):
                        q = TP * i + s
                        act.wait_ge(sm["tr"], q + 1)
                        after(act, sm["mm"], q - (TP - 1))
                        if k == 3:
                            scale_shift(xT[k][:, s, :], ps[:, s, 0:C]).then_inc(sm["xt"], 1)
                        else:
                            AF(xT[k][:, s, :], ps[:, s, 0:C], ACT.Copy).then_inc(sm["xt"], 1)
                    if evacuate and not (isinstance(i, int) and i < late):
                        for s in range(TP):
                            evacuate(TP * (i - late) + s, s, i - late)
                turns(act, FT, turn, peel=3)
                turn(FT, TR)
                if evacuate:
                    for i in range(FT + 1 - late, FT + 1):
                        for s in range(TP if i < FT else TR):
                            evacuate(TP * i + s, s, i)

            def scale_shift(out_ap, in_ap):
                for b in range(2):
                    last = AF(out_ap[:, b * P:(b + 1) * P], in_ap[:, b * P:(b + 1) * P], ACT.Identity,
                              scale=gamT[:, b:b + 1], bias=betT[:, b:b + 1])
                return last

            def root(k):
                act.wait_ge(dve_to_act, k)
                AF(rstd[:, :], rstd[:, :], ACT.Sqrt).then_inc(act_to_dve, 1)

            def load_raw(part, e):
                if part < 2:
                    t = (w1_0, w3_0)[part]
                    tv = t[e, :, :] if isinstance(e, int) else t[bass.ds(e, 1), :, :].rearrange("a h c -> (a h) c")
                    act.dma_start(raw13[:, part, 0:5, :], tv[0:5 * P, :].rearrange("(j p) c -> p j c", p=P)).then_inc(raw_loaded[part], 16)
                    act.dma_start(raw13[0:H0R, part, 5, :], tv[5 * P:H0, :]).then_inc(raw_loaded[part], 16)
                else:
                    tv = w2_0[e, :, :] if isinstance(e, int) else w2_0[bass.ds(e, 1), :, :].rearrange("a c h -> (a c) h")
                    act.dma_start(raw2, tv.rearrange("(m p) h -> p m h", p=P)).then_inc(raw_loaded[2], 16)

            def prep(e, last=False):
                def next_raw(part):
                    if not last:
                        act.nop(nofuse=True)
                        load_raw(part, e + 1)
                n = 0
                for w in range(2):
                    for b in range(2):
                        for half in range(2):
                            n += 1
                            width = 512 if half == 0 else H0 - 512
                            at = b * 2 * H0 + w * H0 + half * 512
                            act.wait_ge(raw_transposed, e * 11 + n)
                            if n % 4 == 0:
                                next_raw(w)
                            AF(W13[:, bass.ds(e * W13N + at, width)] if not isinstance(e, int) else W13[:, e * W13N + at:e * W13N + at + width],
                               ps[:, 2 * b + half, 0:width], ACT.Copy).then_inc(raw_copied, 1)
                for j0, j1, r, bank, at in ((0, 2, P, 4, 0), (2, 4, P, 5, 0), (4, 5, P, 6, 0), (5, 6, H0R, 6, C)):
                    n += at == 0
                    width = (j1 - j0) * C
                    act.wait_ge(raw_transposed, e * 11 + n)
                    if j0 == 4:
                        next_raw(2)
                    AF(W2[0:r, bass.ds(e * W2N + j0 * C, width)] if not isinstance(e, int) else W2[0:r, e * W2N + j0 * C:e * W2N + j0 * C + width],
                       ps[0:r, bank, at:at + width], ACT.Copy).then_inc(raw_copied, 1)

            act.wait_ge(edges_loaded[0], 96)
            for part in range(3):
                load_raw(part, 0)
            for e in range(FIRST):
                if e == FIRST - 1:
                    root(1)
                prep(e)
            project(0, evacuation)
            act.wait_ge(small_mm_out, 3)
            AF(rwT[:, :, :].rearrange("p k e -> p (k e)"), ps[:, 4, 0:2 * E8], ACT.Copy).then_inc(act_step, 1)
            with act.Fori(FIRST, E8 - 1) as e:
                prep(e)
            prep(E8 - 1, last=True)

            def weigh(i):
                for s in range(SU):
                    q = SU * i + s
                    act.wait_ge(sort_onehot_plain, q + 1)
                    after(act, sort_mm, q - SU + 1)
                    for j, part in enumerate((wh_f, wm_f, wl_f)):
                        last = AF(Lb[:, s, 1 + j, :], Lb[:, s, 0, :], ACT.Copy, scale=col(part, q + CP))
                    last.then_inc(sort_weighted, 1)
            turns(act, (EC - CP) // SU, weigh)

            def stage_indices(h):
                edges = idx_s[0 if h == 0 else 1]
                act.wait_ge(sort_ready[0 if h == 0 else 1], 1)

                def turn(i):
                    for half in range(2):
                        g0 = i * GU + 8 * half
                        after(act, hops_mm[h], g0 - 8)
                        AF(istage[:, 8 * half:8 * half + 8], edges[:, g0:g0 + 8] if isinstance(g0, int) else edges[:, bass.ds(g0, 8)],
                           ACT.Copy).then_inc(hop_staged[h], 1)
                turns(act, HT, turn)

            def mixture(m):
                sm = ffn[m]

                def transposed_x(q):
                    act.wait_ge(sm["tx"], q + 1)
                    if m == 1:
                        scale_shift(fT, ps[:, 6, 0:C]).then_inc(sm["fT"], 1)
                    else:
                        AF(fT, ps[:, 6, 0:C], ACT.Copy).then_inc(sm["fT"], 1)

                def transposed_h(q):
                    act.wait_ge(sm["th"], q + 1)
                    if m == 0:
                        AF(hT[:, 0:512], ps[:, 4, :], ACT.Copy)
                        AF(hT[:, 512:640], ps[:, 5, 0:P], ACT.Copy)
                        AF(hT[0:H0R, 640:768], ps[0:H0R, 5, P:2 * P], ACT.Copy).then_inc(sm["hT"], 1)
                    else:
                        AF(hT[:, 0:512], ps[:, 4, :], ACT.Copy).then_inc(sm["hT"], 1)

                def nonlinear(q):
                    if m == 0:
                        act.wait_ge(sm["h"], q + 1)
                        for part in range(2):
                            AF(sil[:, part * HALF:(part + 1) * HALF], ps[:, part, 0:HALF], ACT.Silu).then_inc(sm["act"], 1)
                    else:
                        act.wait_ge(sm["bias"], q + 1)
                        AF(hh[:, 0:H1], sil[:, 0:H1], ACT.Gelu).then_inc(sm["hh"], 1)

                def turn(i, last=False):
                    for s in range(2):
                        q = 2 * i + s
                        if not (isinstance(i, int) and i == 0 and s == 0):
                            transposed_h(q - 1)
                        if m == 0:
                            nonlinear(q)
                        if not (last and s == 1):
                            transposed_x(q + 1)
                        if m == 1:
                            nonlinear(q)
                transposed_x(0)
                turns(act, TT // 2 - 1, turn)
                turn(TT // 2 - 1, last=True)
                transposed_h(TT - 1)

            stage_indices(0)
            root(2)
            project(1)
            act.wait_ge(dve_to_act, 3)
            AF(ta, tb, ACT.Exp).then_inc(act_to_dve, 1)
            mixture(0)
            act.wait_ge(small_mm_out, 7)
            AF(wgT[:, 0, :], ps[:, 0, 0:C], ACT.Copy)
            AF(wgT[:, 1, :], ps[:, 1, 0:C], ACT.Copy).then_inc(wgT_ready, 1)
            act.wait_ge(dve_to_act, 4)
            AF(dinv[:, :], dinv2[:, :], ACT.Sqrt)
            root(4)
            for h in (1, 2):
                if h == 2:
                    act.wait_ge(hops_mm[1], NCH)
                stage_indices(h)
            project(2, exps)
            act.wait_ge(act_step, 1 + NT)
            AF(dinv2[:, :], dinv2[:, :], ACT.Ln).then_inc(log_sum_ready, 1)
            root(5)
            project(3)
            act.wait_ge(dve_to_act, 6)
            AF(v3, v3, ACT.Exp).then_inc(act_to_dve, 1)
            mixture(1)

        @block.vector
        def _(dve):
            V = nc.vector
            ch = Chain(dve, dve_step)

            loop = ch.loop

            MID_TURN = -(-NI // TP)

            def tile_stats(lo, hi, xv=x3):
                for t in range(lo, hi):
                    ch(V.bn_stats(stats[:, t - lo, :], xv[:, t, :]), wait=False)
                ch.sync()
                for t in range(lo, hi):
                    ch(V.bn_aggr(mv[:, t, :], stats[:, t - lo, :]), wait=False)
                ch.sync()

            def half_stats(half, xv=x3):
                tile_stats(NI * half, NI * (half + 1), xv)

            def inverse_root(k):
                V.tensor_scalar(rstd[:, :], mv[:, :, 1], EPS, None, ALU.add).then_inc(dve_to_act, 1)
                dve.wait_ge(act_to_dve, k)
                ch(V.reciprocal(rstd[:, :], rstd[:, :]))

            def normalise(t, out_ap, scale, xv=x3):
                return V.tensor_scalar(out_ap, tile(xv, t), mv_mean(t), col(scale, t), ALU.subtract, ALU.mult)

            def mv_mean(t):
                return mv[:, bass.ds(t, 1), 0:1].rearrange("p a b -> p (a b)") if not isinstance(t, int) else mv[:, t, 0:1]

            V.memset(key_i, PADKEY)
            V.memset(w_f, 0.0)
            V.memset(oth_i, 0).then_inc(edges_cleared, 1)
            ch(V.memset(small[:, :], 0.0), wait=False)
            V.memset(x0[:, FULL:NT, :], 0.0).then_inc(const_ready, 1)
            ch(V.memset(zero, 0.0))
            V.memset(ones[:, :], 1.0).then_inc(const_ready, 1)
            dve.wait_ge(pool_step, 3)
            V.tensor_scalar(ident[:, :], iota_f[:, :], pcol[:, :], None, ALU.is_equal).then_inc(const_ready, 1)
            V.tensor_scalar(below[:, :], iota_f[:, :], pcol[:, :], None, ALU.is_gt).then_inc(const_ready, 1)

            def padded_ends(n, bits):
                ch(V.tensor_scalar(i1[:, 0:n], ps[:, 7, 32:32 + n], float((1 << bits) - 1), None, ALU.add))
                ch(V.tensor_scalar(i2[:, 0:n], i1[:, 0:n], bits, bits, ALU.arith_shift_right, ALU.logical_shift_left))
                ch(V.tensor_copy(padn[:, 0:n], i2[:, 0:n]))
                ch(V.tensor_tensor_scan(incl[:, 0:n], padn[:, 0:n], padn[:, 0:n], 0.0, ALU.add, ALU.max))
                ch(V.tensor_tensor(init[:, 0:n], incl[:, 0:n], padn[:, 0:n], ALU.subtract))
                ch(V.tensor_tensor(init[:, 0:n], init[:, 0:n], ps[:, 7, 0:n], ALU.add))

            def running_pair(b):
                pair = [(n, t) for n, t in ((b, (t1_f, t2_f)), (b + 1, (earr(13), earr(14)))) if n < NB]
                lag = len(pair) - 1
                for n, (t, _) in pair:
                    ch(V.tensor_scalar(t, key_f, float(n), None, ALU.is_equal), wait=False)
                for n, (t, u) in pair:
                    ch.sync(lag)
                    ch(V.tensor_tensor_scan(u, t, t, init[:, n:n + 1], ALU.add, ALU.max), wait=False)
                for n, (t, u) in pair:
                    ch.sync(lag)
                    ch(V.tensor_tensor(u, t, u, ALU.mult), wait=False)
                for n, (t, u) in pair:
                    ch.sync(lag if n == b else 0)
                    ch(V.tensor_tensor(pos_f, pos_f, u, ALU.add), wait=False)
                ch.sync()

            def offsets_begin(below_t):
                ch(V.tensor_tensor(padn[0:NB, 0:NB], incl[0:NB, 0:NB], ident[0:NB, 0:NB], ALU.mult))
                ch(V.tensor_reduce(small[0:NB, 188:189], padn[0:NB, 0:NB], AX.X, ALU.add))
                V.tensor_scalar(below_t, iota_h[0:NB, 0:NCH], float(P), small[0:NB, 188:189], ALU.mult, ALU.is_ge).then_inc(small_mm_in, 1)

            def table(starts, count, n, width, ends):
                ch(V.memset(count, 0.0))
                for b in range(n):
                    ch(V.scalar_tensor_tensor(count, starts, incl[0:1, b:b + 1], count, ALU.is_ge, ALU.add))
                ch(V.tensor_scalar(count, count, float(ends), float(width), ALU.min, ALU.mult))

            def split_key(key, low_out, tile_out, low_i, tile_i):
                ch(V.tensor_scalar(tile_i, key, 7, None, ALU.arith_shift_right), wait=False)
                ch(V.tensor_scalar(low_i, key, P - 1, None, ALU.bitwise_and))
                ch(V.tensor_copy(tile_out, tile_i), wait=False)
                ch(V.tensor_scalar(low_out, low_i, 1.0, None, ALU.add))

            def running(b, key, bucket, first, oh_t, scan_t, pos):
                ch(V.tensor_scalar(oh_t, key, bucket, None, ALU.is_equal))
                ch(V.tensor_tensor_scan(scan_t, oh_t, oh_t, first, ALU.add, ALU.max))
                ch(V.tensor_tensor(scan_t, oh_t, scan_t, ALU.mult))
                ch(V.tensor_tensor(pos, pos, scan_t, ALU.add))

            def offsets(k, row):
                ch(V.memset(goff[k][:, 0:2], 0), wait=False)
                ch(V.tensor_scalar(goff[k][:, 2:NCH + 2], ps[row:row + 1, 7, 64:64 + NCH], float(NB - 1), float(C), ALU.min, ALU.mult))

            dve.wait_ge(edges_loaded[0], 96)
            split_key(key_i, low_f, key_f, t2_i, t1_i)
            ch(V.tensor_scalar(oth_f, oth_i, -float(MID), None, ALU.add), wait=False)
            for b in range(NB):
                ch(V.tensor_scalar((t1_f, t2_f, pos_f, lane_f)[b % 4], key_f, float(b), None, ALU.is_equal, ALU.add,
                                   accum_out=cnt[:, b:b + 1]), wait=(b % 4 == 3))
            ch.sync()
            V.memset(pos_f, 0.0).then_inc(small_mm_in, 1)
            bf = t1_i.bitcast(BF16)[:, 0:EC]
            for n, part in enumerate((wh_f, wm_f, wl_f)):
                ch(V.tensor_copy(bf, w_f if n == 0 else t1_f))
                ch(V.tensor_copy(part, bf))
                if n < 2:
                    ch(V.tensor_tensor(t1_f, w_f if n == 0 else t1_f, part, ALU.subtract))
            for n, part in enumerate((low_f, oth_f, w_f)):
                ch(V.tensor_copy(words0[:, :, n], part[:, 0:CP]), wait=False)
            dve.wait_ge(small_mm_out, 1)
            padded_ends(NB, 7)
            offsets_begin(behind0)
            dve.wait_ge(small_mm_out, 2)
            offsets(0, 0)

            for half in range(2):
                dve.wait_ge(x_half_loaded[half], 16 + 16 * half)
                half_stats(half, x0)
            inverse_root(1)

            def give(i, tiles=TP):
                for s in range(tiles):
                    q = TP * i + s
                    after(dve, proj[0]["tr"], q - (TP - 1))
                    normalise(q, xn[0][:, s, :], rstd, x0).then_inc(proj[0]["xn"], 1)
            for n in range(NB // 2 + 1):
                if n <= FT:
                    give(n, TP if n < FT else TR)
                running_pair(2 * n)
            ch(V.tensor_scalar(t1_i, pos_f, -1.0, None, ALU.add))
            ch(V.tensor_scalar(t2_i, t1_i, P - 1, None, ALU.bitwise_and), wait=False)
            ch(V.tensor_scalar(t1_i, t1_i, 7, None, ALU.arith_shift_right))
            ch(V.tensor_copy(lane_f, t2_i), wait=False)
            ch(V.tensor_copy(chunk_f, t1_i))
            V.scalar_tensor_tensor(t2_i, lane_f, float(NCH), chunk_f, ALU.mult, ALU.add).then_inc(ranked[0], 1)
            dve.wait_ge(raw_transposed, 11 * E8)

            def sort_columns(i):
                for s in range(SU):
                    q = SU * i + s
                    c = q + CP
                    after(dve, sort_mm, q - SU + 1)
                    V.tensor_scalar(Lb[:, s, 0, :], iota_h[:, 0:P], col(lane_f, c), None, ALU.is_equal).then_inc(sort_onehot_plain, 1)
                    V.tensor_scalar(oc[:, s, :], iota_h[:, :], col(chunk_f, c), None, ALU.is_equal)
                    V.tensor_scalar(Lh[:, s, 0, :], iota_h[:, 0:P], col(lane_f, c), col(low_f, c), ALU.is_equal, ALU.mult)
                    V.tensor_scalar(Lh[:, s, 1, :], iota_h[:, 0:P], col(lane_f, c), col(oth_f, c), ALU.is_equal, ALU.mult).then_inc(sort_onehot, 1)
            turns(dve, (EC - CP) // SU, sort_columns)
            dve.wait_ge(sort_mm, EC - CP)
            dve.wait_ge(placed_back[0], 16)
            ch(V.scalar_tensor_tensor(low_s[0][:, :], back0[:, :, 0], -1.0, ps[:, 0, 0:NCH], ALU.add, ALU.add), wait=False)
            ch(V.scalar_tensor_tensor(idx_s[0][:, :], back0[:, :, 1], float(MID), ps[:, 1, 0:NCH], ALU.add, ALU.add), wait=False)
            ch(V.tensor_tensor(wgt_s[:, :], back0[:, :, 2], ps[:, 4, 0:NCH], ALU.add))
            ch(V.tensor_tensor(wgt_s[:, :], wgt_s[:, :], ps[:, 3, 0:NCH], ALU.add))
            V.tensor_tensor(wgt_s[:, :], wgt_s[:, :], ps[:, 2, 0:NCH], ALU.add).then_inc(sort_ready[0], 1)
            dve.wait_ge(sort_ready[0], 1)
            dve.wait_ge(sorted_zeroed, 32)
            V.memset(A[:, :], 0.0).then_inc(hop_start[0], 1)
            dve.wait_ge(hop_start[0], 1)

            def hop(h):
                e = 0 if h == 0 else 1
                oh = hop_oh[h]

                def onehot(q, g):
                    after(dve, hops_mm[h], q - 3)
                    if h == 0:
                        ins = V.tensor_scalar(oh[:, g % 4, :], iota_f[:, :], col(low_s[e], q), col(wgt_s, q), ALU.is_equal, ALU.mult)
                    else:
                        ins = V.tensor_scalar(oh[:, g % 4, :], iota_f[:, :], col(low_s[e], q), None, ALU.is_equal)
                    ins.then_inc(hops_oh[h], 1)

                def add(q, g, at):
                    dve.wait_ge(hops_mm[h], q + 1)
                    after(dve, hops_added[h], q)
                    a = A[:, bass.ds(at, C)]
                    V.tensor_tensor(a, a, ps[:, g % 4, 0:C], ALU.add).then_inc(hops_added[h], 1)

                def offsets_of(n):
                    return in_registers(ON_DVE, goff[e], n, 8, (NB - 1) * C)

                def turn(i, beside=()):
                    for g in range(GU):
                        q = GU * i + g
                        if g % 8 == 0:
                            offs = offsets_of(q)
                        onehot(q, g)
                        if not (isinstance(i, int) and i == 0 and g < 2):
                            add(q - 2, (g - 2) % GU, offs[g % 8])
                        if g in beside:
                            beside[g](i)

                if h == 0:
                    turn(0, {1: second_clear, 9: second_words})
                    loop(RANK_AT, 5, lambda i: turn(i, {3 * n: second_count(n) for n in range(5)}), lo=1)
                    turn(RANK_AT, {0: second_counted, 8: second_ends})
                    loop(RANK_AT + 14, 8, lambda i: turn(i, {2: second_rank(0), 10: second_rank(1)}), lo=RANK_AT + 1)
                    turn(RANK_AT + 14, {2: second_places, 6: second_offsets})
                    with dve.Fori(RANK_AT + 15, HT) as i:
                        turn(i)
                else:
                    turns(dve, HT, turn)
                offs = in_registers(ON_DVE, goff[e], NCH, 2, (NB - 1) * C)
                for q in (NCH - 2, NCH - 1):
                    add(q, q % GU, offs[q % 2])
                dve.wait_ge(hops_added[h], NCH)

            def second_clear(i):
                V.memset(ta1.bitcast(I32), 0)
                V.memset(place1, PADKEY).then_inc(edges_cleared, 1)

            def second_words(i):
                dve.wait_ge(edges_loaded[1], 64)
                ch(V.tensor_copy(words1[:, :, 1], ta1.bitcast(I32)), wait=False)
                split_key(place1, words1[:, :, 0], key1, tb1.bitcast(I32), pos1.bitcast(I32))

            def second_count(n):
                def count(i):
                    b = 5 * i - 5 + n
                    ch(V.tensor_scalar(tb1, key1, iota_f[:, bass.ds(b, 1)], None, ALU.is_equal, ALU.add,
                                       accum_out=cnt[:, bass.ds(b, 1)]))
                return count

            def second_counted(i):
                V.memset(pos1, 0.0).then_inc(small_mm_in, 1)

            def second_ends(i):
                dve.wait_ge(small_mm_out, 4)
                padded_ends(NB, 7)
                offsets_begin(behind1)

            def second_rank(n):
                def rank(i):
                    dve.wait_ge(small_mm_out, 5)
                    b = 2 * i - 2 * (RANK_AT + 1) + n
                    running(b, key1, iota_f[:, bass.ds(b, 1)], init[:, bass.ds(b, 1)], ta1, tb1, pos1)
                return rank

            def second_places(i):
                a_i, b_i = ta1.bitcast(I32), tb1.bitcast(I32)
                ch(V.tensor_scalar(a_i, pos1, -1.0, None, ALU.add))
                ch(V.tensor_scalar(b_i, a_i, P - 1, None, ALU.bitwise_and))
                ch(V.tensor_scalar(a_i, a_i, 7, None, ALU.arith_shift_right))
                ch(V.scalar_tensor_tensor(pos1, b_i, float(NCH), a_i, ALU.mult, ALU.add))
                ch(V.tensor_scalar(ta1, iota_h[:, 0:EC], float(SLOTS - (P - 1) * NCH + 1), None, ALU.add))
                ch(V.scalar_tensor_tensor(tb1, key1, float(NT), ta1, ALU.is_equal, ALU.mult))
                V.tensor_tensor(place1, pos1, tb1, ALU.add).then_inc(ranked[1], 1)

            def second_offsets(i):
                offsets(1, 32)

            hop(0)

            dve.wait_ge(kept_stored, 16)
            V.memset(x3[:, FULL:NT, :], 0.0).then_inc(x_reloaded, 1)
            for half in range(2):
                dve.wait_ge(x_half_loaded[half], 2 * (16 + 16 * half))
                part = slice(half * NI * C, (half + 1) * NI * C)
                V.scalar_tensor_tensor(X[:, part], A[:, part], 0.0, X[:, part], ALU.max, ALU.add).then_inc(relu_added, 1)
                dve.wait_ge(relu_added, half + 1)
                half_stats(half)

            def route_project(k):
                m = 0 if k == 1 else 1

                def turn(i, tiles=TP):
                    for s in range(tiles):
                        q = TP * i + s
                        after(dve, proj[k]["tr"], q - (TP - 1))
                        if s % 2 == 0:
                            after(dve, xn_stored[m][s // 2], i * 16)
                        normalise(q, xn[k][:, s, :], rstd).then_inc(proj[k]["xn"], 1)
                    if not (isinstance(i, int) and i < 2):
                        take(TP * (i - 2), TP)

                def take(q, n):
                    dve.wait_ge(proj[k]["mm"], q + n)
                    dstt = lg[:, bass.ds(q, n), :] if not isinstance(q, int) else lg[:, q:q + n, :]
                    got = ps[:, TP:TP + n, 0:E8]
                    if k == 1:
                        V.tensor_copy(dstt, got).then_inc(proj[k]["ev"], n)
                    else:
                        V.tensor_tensor(dstt, got, br_s.rearrange("p (a e) -> p a e", a=1).to_broadcast([P, n, E8]),
                                        ALU.add).then_inc(proj[k]["ev"], n)
                turns(dve, FT, turn, peel=2)
                turn(FT, TR)
                take(TP * (FT - 1), TP)
                take(TP * FT, TR)
                dve.wait_ge(proj[k]["ev"], NT)

            def bc(v):
                return v.rearrange("p (t a) -> p t a", a=1).to_broadcast([P, NT, E8])

            def masks(val, drop):
                ch(V.tensor_copy(wrev, iota_f[:, 0:E8]))
                ch(V.tensor_scalar(wrev, wrev, -1.0, float(E8), ALU.mult, ALU.add))
                wb = wrev.rearrange("p (a e) -> p a e", a=1).to_broadcast([P, NT, E8])
                for k in range(2):
                    ch(V.tensor_reduce(v1 if k == 0 else v2, val, AX.X, ALU.max))
                    ch(V.tensor_tensor(ta, val, bc(v1 if k == 0 else v2), ALU.is_equal))
                    ch(V.tensor_tensor(ta, ta, wb, ALU.mult))
                    ch(V.tensor_reduce(v3, ta, AX.X, ALU.max))
                    Mk = MS[:, :, k * NT:(k + 1) * NT].rearrange("p e t -> p t e")
                    ch(V.tensor_tensor(Mk, ta, bc(v3), ALU.is_equal))
                    if k == 0:
                        ch(V.tensor_scalar(ta, Mk, -drop, None, ALU.mult))
                        ch(V.tensor_tensor(val, val, ta, ALU.add))
                for k in range(2):
                    mk = MS[:, :, k * NT + FULL]
                    ch(V.tensor_scalar(v3[:, 0:1], pcol[:, :], float(REST), None, ALU.is_lt))
                    ch(V.tensor_scalar(mk, mk, v3[:, 0:1], None, ALU.mult))
                    ch(V.memset(MS[:, :, k * NT + NT - 1], 0.0))

            def places(m):
                V.tensor_reduce(cnt[:, 0:E8], MS, AX.X, ALU.add).then_inc(small_mm_in, 1)
                dve.wait_ge(small_mm_out, 6 + 2 * m)
                padded_ends(E8, 7)
                ms = MS.rearrange("p e c -> p (e c)")
                ch(V.tensor_tensor_scan(run, ms, ms, 0.0, ALU.add, ALU.max))
                run3 = run.rearrange("p (e c) -> p e c", e=E8)
                ch(V.tensor_tensor(init[:, 1:E8], init[:, 1:E8], run3[:, 0:E8 - 1, 2 * NT - 1], ALU.subtract))
                ch(V.tensor_tensor(run3, run3, init[:, 0:E8].rearrange("p (e a) -> p e a", a=1).to_broadcast([P, E8, 2 * NT]), ALU.add))
                ch(V.tensor_tensor(run3, run3, MS, ALU.mult))
                ch(V.tensor_reduce(fpos, run3.rearrange("p e c -> p c e"), AX.X, ALU.add))
                ch(V.tensor_scalar(gath_i[:, :, :].rearrange("p k t -> p (k t)"), fpos, -1.0, 0.0, ALU.add, ALU.max), wait=False)
                ch(V.tensor_scalar(ft1.bitcast(I32), fpos, -1.0, None, ALU.add))
                ch(V.tensor_scalar(ft2.bitcast(I32), ft1.bitcast(I32), P - 1, None, ALU.bitwise_and))
                ch(V.tensor_copy(fpos, ft2.bitcast(I32)))
                ch(V.tensor_scalar(ft2.bitcast(I32), ft1.bitcast(I32), 7, None, ALU.arith_shift_right))
                ch(V.tensor_copy(ft1, ft2.bitcast(I32)))
                ch(V.tensor_scalar(token, iota_f[:, 0:NT], float(P), pcol[:, :], ALU.mult, ALU.add))
                ch(V.tensor_scalar(token, token, -float(MID), None, ALU.add))
                for h in range(2):
                    dve.wait_ge(xn_stored[m][h], stores_of(h))
                for k in range(2):
                    def spread(cols, n):
                        return cols.rearrange("p (t a) -> p t a", a=1).to_broadcast([P, NB, n])
                    lanes, tiles = fpos[:, k * NT:k * NT + NB], ft1[:, k * NT:k * NT + NB]
                    ch(V.tensor_tensor(inv_tile[k], iota_h[:, 0:TT].rearrange("p (a n) -> p a n", a=1).to_broadcast([P, NB, TT]),
                                       spread(tiles, TT), ALU.is_equal), wait=False)
                    ch(V.tensor_tensor(inv_lane[k], iota_h[:, 0:P].rearrange("p (a n) -> p a n", a=1).to_broadcast([P, NB, P]),
                                       spread(lanes, P), ALU.is_equal))
                    V.tensor_tensor(inv_tile[k], inv_tile[k], spread(token[:, 0:NB], TT), ALU.mult).then_inc(token_onehots, 1)
                ch(V.tensor_scalar(est, iota_f[0:1, 0:TT], float(P), None, ALU.mult))
                table(est, ecount, E8, 1, E8 - 1)
                V.tensor_copy(eoff[:, :], ecount).then_inc(routed, 1)
                dve.wait_ge(routed, m + 1)
                dve.wait_ge(token_mm, 2 * m + 2)
                V.tensor_scalar(token_of[:, :], ps[:, 6, 0:TT], float(MID), None, ALU.add).then_inc(token_ready, 1)

            def combine(m):
                def turn(i, tiles=TP):
                    for s in range(tiles):
                        t = TP * i + s
                        dve.wait_ge(y_gathered[m][s], i * 32 + 32)
                        ch(V.scalar_tensor_tensor(tile(x3, t), yg[:, s, 0, :], col(gate[:, 0, :], t), tile(x3, t), ALU.mult, ALU.add))
                        V.scalar_tensor_tensor(tile(x3, t), yg[:, s, 1, :], col(gate[:, 1, :], t), tile(x3, t), ALU.mult, ALU.add).then_inc(comb_used[m], 1)
                if m == 0:
                    loop(MID_TURN, TP, turn)
                    dve.wait_ge(comb_used[m], MID_TURN * TP)
                    half_stats(0)
                    loop(FT, TP, turn, lo=MID_TURN)
                    dve.wait_ge(comb_used[m], FT * TP)
                    tile_stats(NI, FT * TP)
                else:
                    loop(FT, TP, turn)
                turn(FT, TR)
                dve.wait_ge(comb_used[m], NT)

            inverse_root(2)
            route_project(1)
            ch(V.tensor_reduce(v1, lg, AX.X, ALU.max))
            V.tensor_tensor(tb, lg, bc(v1), ALU.subtract).then_inc(dve_to_act, 1)
            dve.wait_ge(act_to_dve, 3)
            ch(V.tensor_reduce(v1, ta, AX.X, ALU.add))
            ch(V.reciprocal(v1, v1))
            ch(V.tensor_tensor(pr, ta, bc(v1), ALU.mult))
            masks(pr, 2.0)
            ch(V.tensor_tensor(v3, v1, v2, ALU.add))
            ch(V.tensor_scalar(v3, v3, 1e-9, None, ALU.add))
            ch(V.reciprocal(v3, v3))
            ch(V.tensor_tensor(gate[:, 0, :], v1, v3, ALU.mult))
            ch(V.tensor_tensor(gate[:, 1, :], v2, v3, ALU.mult))
            places(0)

            def mixture(m):
                sm = ffn[m]

                def some(arr, lo, n):
                    part = arr[:, lo:lo + DU] if isinstance(lo, int) else arr[:, bass.ds(lo, DU)]
                    return part.rearrange("p (t a) -> p t a", a=1).to_broadcast([P, DU, n])

                def hidden(q):
                    if m == 0:
                        for part in range(2):
                            dve.wait_ge(sm["act"], q * 2 + (part + 1))
                            ins = V.tensor_tensor(hh[:, part * HALF:(part + 1) * HALF], sil[:, part * HALF:(part + 1) * HALF],
                                                  ps[:, 2 + part, 0:HALF], ALU.mult)
                        ins.then_inc(sm["hh"], 1)
                    else:
                        e = in_registers(ON_DVE, eoff, q, 1, E8 - 1)[0]
                        dve.wait_ge(sm["h"], q + 1)
                        V.tensor_tensor(sil[:, 0:H1], ps[:, 0, :], b1b[:, bass.ds(e * H1, H1)], ALU.add).then_inc(sm["bias"], 1)

                def result(q, s, i):
                    if m == 1:
                        e = in_registers(ON_DVE, eoff, q, 1, E8 - 1)[0]
                    dve.wait_ge(sm["y"], q + 1)
                    after(dve, ys_stored[m][s], i * 16)
                    if m == 0 and s == 0:
                        V.tensor_tensor(dinv2[:, :], dinv2[:, :], ps[:, 7, C:C + NT], ALU.add)
                    if m == 0:
                        V.tensor_copy(ys[:, s, :], ps[:, 7, 0:C]).then_inc(sm["ys"], 1)
                    else:
                        V.tensor_tensor(ys[:, s, :], ps[:, 7, 0:C], b2b[:, bass.ds(e * C, C)], ALU.add).then_inc(sm["ys"], 1)

                def turn(i):
                    if m == 0:
                        after(dve, sm["y"], 2 * i - 1)
                        V.tensor_tensor(low_oh, iota_h[:, 1:P + 1].rearrange("p (a n) -> p a n", a=1).to_broadcast([P, DU, P]),
                                        some(words1A[:, :, 0], i * DU, P), ALU.is_equal)
                        V.tensor_tensor(tile_oh, iota_h[:, 0:NT].rearrange("p (a n) -> p a n", a=1).to_broadcast([P, DU, NT]),
                                        some(key1A, i * DU, NT), ALU.is_equal).then_inc(counted_onehot, 1)
                    for s in range(2):
                        q = 2 * i + s
                        hidden(q)
                        if s == 1:
                            result(q - 1, 0, i)
                        elif not (isinstance(i, int) and i == 0):
                            result(q - 1, 1, i - 1)
                turns(dve, TT // 2, turn, peel=2)
                result(TT - 1, 1, TT // 2 - 1)

            ch(V.memset(dinv2[:, :], 1.0))
            dve.wait_ge(kept_loaded, 16)
            mixture(0)
            dve.wait_ge(placed_back[1], 16)
            ch(V.tensor_scalar(low_s[1][:, :], back1[:, :, 0], -1.0, None, ALU.add), wait=False)
            V.tensor_copy(idx_s[1][:, :], back1[:, :, 1]).then_inc(sort_ready[1], 1)
            ch(V.reciprocal(dinv2[:, :], dinv2[:, :]))
            combine(0)

            tile_stats(FT * TP, NT)
            inverse_root(4)
            ch(V.tensor_tensor(cnt, rstd[:, :], dinv[:, :], ALU.mult))

            for t in range(NT):
                ins = normalise(t, tile(a3, t), cnt)
                if t % NI == NI - 1:
                    ins.then_inc(hop_start[1], 1)
            dve.wait_ge(hop_start[1], 2)
            hop(1)

            for half in range(2):
                part = a3[:, half * NI:(half + 1) * NI, :]
                by = dinv2[:, half * NI:(half + 1) * NI].rearrange("p (t a) -> p t a", a=1).to_broadcast([P, NI, C])
                V.tensor_tensor(part, part, by, ALU.mult).then_inc(hop_start[2], 1)
            dve.wait_ge(hop_start[2], 2)
            hop(2)

            def logits(i, tiles=TP):
                for s in range(tiles):
                    t = TP * i + s
                    after(dve, proj[2]["tr"], t - (TP - 1))
                    V.tensor_scalar(xn[2][:, s, :], tile(a3, t), col(dinv, t), None, ALU.mult).then_inc(proj[2]["xn"], 1)
                if not (isinstance(i, int) and i < 2):
                    for s in range(TP):
                        take_logits(TP * (i - 2) + s, s)

            def take_logits(t, s):
                dve.wait_ge(proj[2]["mm"], t + 1)
                ch(V.tensor_tensor(tile(a3, t), ps[:, TP + s, 0:C], bg, ALU.add))
                V.tensor_reduce(col(rstd, t), tile(a3, t), AX.X, ALU.max, negate=True).then_inc(proj[2]["ev"], 1)
            logits(0)
            logits(1)
            loop(FT, TP, logits, lo=2)
            logits(FT, TR)
            for s in range(TP):
                take_logits(TP * (FT - 1) + s, s)
            for s in range(TR):
                take_logits(TP * FT + s, s)
            dve.wait_ge(proj[2]["ev"], NT)
            dve.wait_ge(log_sum_ready, 1)
            ch(V.tensor_tensor(rstd[:, :], rstd[:, :], dinv2[:, :], ALU.subtract))

            for half in range(2):
                for t in range(half * NI, (half + 1) * NI):
                    ch(V.scalar_tensor_tensor(tile(x3, t), tile(a3, t), col(rstd, t), tile(x3, t), ALU.add, ALU.add), wait=False)
                ch.sync()
                half_stats(half)

            inverse_root(5)
            route_project(3)
            masks(lg, BIG)
            V.tensor_tensor(v3, v2, v1, ALU.subtract).then_inc(dve_to_act, 1)
            dve.wait_ge(act_to_dve, 6)
            ch(V.tensor_scalar(v1, v3, 1.0, None, ALU.add))
            ch(V.reciprocal(gate[:, 0, :], v1))
            ch(V.tensor_tensor(gate[:, 1, :], v3, gate[:, 0, :], ALU.mult))
            places(1)
            mixture(1)
            combine(1)


_INS = ['x', 'src', 'dst', 'edge_weight', 'L0_gnn_weight', 'L0_ffn_router_w', 'L0_ffn_w1', 'L0_ffn_w2', 'L0_ffn_w3',
        'L1_gnn_W', 'L1_gnn_b', 'L1_ffn_gamma', 'L1_ffn_beta', 'L1_ffn_Wr', 'L1_ffn_br',
        'L1_ffn_W1', 'L1_ffn_b1', 'L1_ffn_W2', 'L1_ffn_b2']
_OUT = ((3125, 256), 'float32')


def kernel(**inputs):
    import numpy as _np
    import concourse.bacc as _bacc
    from concourse import mybir as _mybir
    from concourse.bass_utils import run_bass_kernel_spmd as _run

    nc = _bacc.Bacc("TRN2", target_bir_lowering=False, num_devices=1)
    arrays, args = {}, {}
    for name in _INS:
        a = _np.ascontiguousarray(inputs[name])
        arrays[f"in_{name}_dram"] = a
        args[name] = nc.dram_tensor(f"in_{name}_dram", a.shape, _mybir.dt.from_np(a.dtype), kind="ExternalInput").ap()
    out = nc.dram_tensor("out_dram", _OUT[0], _mybir.dt.from_np(_np.dtype(_OUT[1])), kind="ExternalOutput").ap()
    gnn_moe_program(nc, args['x'], args['src'], args['dst'], args['edge_weight'], args['L0_gnn_weight'],
                    args['L0_ffn_router_w'], args['L0_ffn_w1'], args['L0_ffn_w2'], args['L0_ffn_w3'],
                    args['L1_gnn_W'], args['L1_gnn_b'], args['L1_ffn_gamma'], args['L1_ffn_beta'],
                    args['L1_ffn_Wr'], args['L1_ffn_br'], args['L1_ffn_W1'], args['L1_ffn_b1'],
                    args['L1_ffn_W2'], args['L1_ffn_b2'], out)
    r = _run(nc, [arrays], core_ids=[0])
    return r.results[0]["out_dram"]
```
